# Optimizing a Trainium2 kernel written in Bass

```python
import numpy as np
import jax
import jax.numpy as jnp

def _softmax(x, axis=-1):
    return jax.nn.softmax(x, axis=axis)

def _gelu(x):
    return jax.nn.gelu(x, approximate=True)

def _silu(x):
    return jax.nn.silu(x)

def _sigmoid(x):
    return jax.nn.sigmoid(x)

def _layernorm(x, axis=-1, eps=1e-05):
    m = jnp.mean(x, axis=axis, keepdims=True)
    v = jnp.var(x, axis=axis, keepdims=True)
    return (x - m) / jnp.sqrt(v + eps)

def _scatter_add(tgt, idx, src, axis=0):
    return tgt.at[idx].add(src)

def _segment_sum(src, seg, n):
    return jax.ops.segment_sum(src, seg, n)
kernel_name = 'mk_gnn_resnorm_d4_gnn_r32_247f32'

def setup_inputs(seed: int=0):
    np.random.seed(seed)
    _w = jnp.asarray

    def _rec_inputs():
        import jax
        import jax.numpy as jnp
        _gk = jax.random.key(seed)
        x = -0.0003713 + 1 * jax.random.normal(jax.random.fold_in(_gk, 1), (3125, 256), jnp.float32)
        src = jax.random.randint(jax.random.fold_in(_gk, 2), (50000,), 0, 3125, jnp.int32)
        dst = jnp.minimum((3125 * jax.random.uniform(jax.random.fold_in(_gk, 3), (50000,)) ** 2.0).astype(jnp.int32), 99999)
        _o = jnp.argsort(dst, stable=True)
        src = src[_o]
        dst = dst[_o]
        edge_type_3 = jax.random.randint(jax.random.fold_in(_gk, 12), (50000,), 0, 3, jnp.int32)
        node_type_4 = jax.random.randint(jax.random.fold_in(_gk, 13), (3125,), 0, 4, jnp.int32)
        return (x, src, dst, edge_type_3, node_type_4)
    x, src, dst, edge_type_3, node_type_4 = _rec_inputs()

    def _L0_gnn_setup():
        import jax, jax.numpy as jnp
        import numpy as np
        N, E, C_IN = (50000, 25000, 256)
        H = 2
        C1 = 64
        C2 = 128
        NEG_SLOPE = 0.2

        def glorot(key, shape):
            fan_in, fan_out = (shape[0], shape[1])
            lim = jnp.sqrt(6.0 / (fan_in + fan_out))
            return jax.random.uniform(key, shape, jnp.float32, -lim, lim)

        def gatv2_conv(x, src, dst, Wl, Wr, att, b, heads, c_out):
            n = x.shape[0]
            xl = (x @ Wl).reshape(n, heads, c_out)
            xr = (x @ Wr).reshape(n, heads, c_out)
            e = jax.nn.leaky_relu(xl[src] + xr[dst], NEG_SLOPE)
            logit = jnp.einsum('ehc,hc->eh', e, att)
            m = jax.ops.segment_max(logit, dst, num_segments=n)
            a = jnp.exp(logit - m[dst])
            denom = jax.ops.segment_sum(a, dst, num_segments=n)
            alpha = a / denom[dst]
            out = jax.ops.segment_sum(alpha[:, :, None] * xl[src], dst, num_segments=n)
            return out.reshape(n, heads * c_out) + b
        key = jax.random.key(seed)
        ks = jax.random.split(key, 12)
        x = jax.random.normal(ks[0], (N, C_IN), jnp.float32)
        edge_index = jax.random.randint(ks[1], (2, E), 0, N, jnp.int64)
        Wl0 = glorot(ks[2], (C_IN, H * C1))
        Wr0 = glorot(ks[3], (C_IN, H * C1))
        att0 = glorot(ks[4], (H, C1))
        b0 = jnp.zeros((H * C1,), jnp.float32)
        Wl1 = glorot(ks[5], (H * C1, H * C2))
        Wr1 = glorot(ks[6], (H * C1, H * C2))
        att1 = glorot(ks[7], (H, C2))
        b1 = jnp.zeros((H * C2,), jnp.float32)
        return {'x': x, 'edge_index': edge_index, 'Wl0': Wl0, 'Wr0': Wr0, 'att0': att0, 'b0': b0, 'Wl1': Wl1, 'Wr1': Wr1, 'att1': att1, 'b1': b1}
    _L0_gnn_all = _L0_gnn_setup()
    _L0_gnn_in = {k: v for k, v in _L0_gnn_all.items() if k in ('Wl0', 'Wr0', 'att0', 'b0', 'Wl1', 'Wr1', 'att1', 'b1')}
    del _L0_gnn_all

    def _L1_gnn_setup():
        import jax, jax.numpy as jnp
        import numpy as np
        N = 50000
        IN_CH = 256
        HEADS = 8
        OUT_CH = 32
        E = 25000
        key = jax.random.key(seed)
        k1, k2, k3, k4, k5 = jax.random.split(key, 5)
        x = jax.random.normal(k1, (N, IN_CH), dtype=jnp.float32)
        edge_index = jax.random.randint(k2, (2, E), 0, N, dtype=jnp.int64)
        W = jax.random.normal(k3, (HEADS * OUT_CH, IN_CH), dtype=jnp.float32) / np.sqrt(IN_CH)
        bound = float(np.sqrt(6.0 / (HEADS + OUT_CH)))
        attn_l = jax.random.uniform(k4, (1, HEADS, OUT_CH), minval=-bound, maxval=bound, dtype=jnp.float32)
        attn_r = jax.random.uniform(k5, (1, HEADS, OUT_CH), minval=-bound, maxval=bound, dtype=jnp.float32)
        return {'x': x, 'edge_index': edge_index, 'W': W, 'attn_l': attn_l, 'attn_r': attn_r}
    _L1_gnn_all = _L1_gnn_setup()
    _L1_gnn_in = {k: v for k, v in _L1_gnn_all.items() if k in ('W', 'attn_l', 'attn_r')}
    del _L1_gnn_all

    def _L2_gnn_setup():
        import jax, jax.numpy as jnp
        import numpy as np
        import math
        L, H, HD, D = (3, 8, 32, 256)
        TN, TE = (4, 3)

        def _layer_norm(x, g, b, eps=1e-05):
            m = jnp.mean(x, axis=-1, keepdims=True)
            v = jnp.var(x, axis=-1, keepdims=True)
            return (x - m) / jnp.sqrt(v + eps) * g + b

        def _typed_transform(xh, W, types):
            out = jnp.zeros_like(xh)
            for t in range(W.shape[0]):
                y = jnp.einsum('mhd,hde->mhe', xh, W[t])
                out = jnp.where((types == t)[:, None, None], y, out)
            return out
        N, E = (625, 10000)
        key = jax.random.key(seed)
        ks = jax.random.split(key, 16)
        inp = {}
        inp['x'] = jax.random.normal(ks[0], (N, D), dtype=jnp.float32)
        inp['edge_index'] = jax.random.randint(ks[1], (2, E), 0, N)
        inp['edge_type'] = jax.random.randint(ks[2], (E,), 0, TE)
        inp['node_type'] = jax.random.randint(ks[3], (N,), 0, TN)
        inp['W_Q'] = jax.random.normal(ks[4], (L, TN, H, HD, HD), dtype=jnp.float32) * 0.02
        inp['W_K'] = jax.random.normal(ks[5], (L, TN, H, HD, HD), dtype=jnp.float32) * 0.02
        inp['W_V'] = jax.random.normal(ks[6], (L, TN, H, HD, HD), dtype=jnp.float32) * 0.02
        inp['W_E'] = jax.random.normal(ks[7], (L, TE, H, HD, HD), dtype=jnp.float32) * 0.02
        inp['mu'] = jnp.ones((L, H, TE), dtype=jnp.float32)
        inp['Wo'] = jax.random.normal(ks[8], (L, D, D), dtype=jnp.float32) * 0.02
        inp['bo'] = jnp.zeros((L, D), dtype=jnp.float32)
        inp['ln1_g'] = jnp.ones((L, D), dtype=jnp.float32)
        inp['ln1_b'] = jnp.zeros((L, D), dtype=jnp.float32)
        inp['ln2_g'] = jnp.ones((L, D), dtype=jnp.float32)
        inp['ln2_b'] = jnp.zeros((L, D), dtype=jnp.float32)
        inp['w1'] = jax.random.normal(ks[9], (L, D, 4 * D), dtype=jnp.float32) * 0.02
        inp['b1'] = jnp.zeros((L, 4 * D), dtype=jnp.float32)
        inp['w2'] = jax.random.normal(ks[10], (L, 4 * D, D), dtype=jnp.float32) * 0.02
        inp['b2'] = jnp.zeros((L, D), dtype=jnp.float32)
        inp['out_g'] = jnp.ones((D,), dtype=jnp.float32)
        inp['out_b'] = jnp.zeros((D,), dtype=jnp.float32)
        return inp
    _L2_gnn_all = _L2_gnn_setup()
    _L2_gnn_in = {k: v for k, v in _L2_gnn_all.items() if k in ('W_Q', 'W_K', 'W_V', 'W_E', 'mu', 'Wo', 'bo', 'ln1_g', 'ln1_b', 'ln2_g', 'ln2_b', 'w1', 'b1', 'w2', 'b2', 'out_g', 'out_b')}
    del _L2_gnn_all

    def _L3_gnn_setup():
        import jax, jax.numpy as jnp
        import numpy as np
        N_NODES = 3125
        N_EDGES = 10000
        D_IN, D_HID, D_OUT = (256, 1024, 256)
        BN_EPS = 1e-05
        key = jax.random.key(seed)
        ks = jax.random.split(key, 6)
        x = jax.random.normal(ks[0], (N_NODES, D_IN), dtype=jnp.float32)
        edge_index = jax.random.randint(ks[1], (2, N_EDGES), 0, N_NODES, dtype=jnp.int64)
        W1 = jax.random.normal(ks[2], (D_IN, D_HID), dtype=jnp.float32) * (1.0 / np.sqrt(D_IN))
        b1 = jnp.zeros((D_HID,), dtype=jnp.float32)
        gamma = jnp.ones((D_HID,), dtype=jnp.float32)
        beta = jnp.zeros((D_HID,), dtype=jnp.float32)
        W2 = jax.random.normal(ks[3], (D_HID, D_OUT), dtype=jnp.float32) * (1.0 / np.sqrt(D_HID))
        b2 = jnp.zeros((D_OUT,), dtype=jnp.float32)
        return {'x': x, 'edge_index': edge_index, 'W1': W1, 'b1': b1, 'gamma': gamma, 'beta': beta, 'W2': W2, 'b2': b2}
    _L3_gnn_all = _L3_gnn_setup()
    _L3_gnn_in = {k: v for k, v in _L3_gnn_all.items() if k in ('W1', 'b1', 'gamma', 'beta', 'W2', 'b2')}
    del _L3_gnn_all
    return {'x': x, 'src': src, 'dst': dst, 'edge_type_3': edge_type_3, 'node_type_4': node_type_4, 'L0_gnn_Wl0': _L0_gnn_in['Wl0'], 'L0_gnn_Wr0': _L0_gnn_in['Wr0'], 'L0_gnn_att0': _L0_gnn_in['att0'], 'L0_gnn_b0': _L0_gnn_in['b0'], 'L0_gnn_Wl1': _L0_gnn_in['Wl1'], 'L0_gnn_Wr1': _L0_gnn_in['Wr1'], 'L0_gnn_att1': _L0_gnn_in['att1'], 'L0_gnn_b1': _L0_gnn_in['b1'], 'L1_gnn_W': _L1_gnn_in['W'], 'L1_gnn_attn_l': _L1_gnn_in['attn_l'], 'L1_gnn_attn_r': _L1_gnn_in['attn_r'], 'L2_gnn_W_Q': _L2_gnn_in['W_Q'], 'L2_gnn_W_K': _L2_gnn_in['W_K'], 'L2_gnn_W_V': _L2_gnn_in['W_V'], 'L2_gnn_W_E': _L2_gnn_in['W_E'], 'L2_gnn_mu': _L2_gnn_in['mu'], 'L2_gnn_Wo': _L2_gnn_in['Wo'], 'L2_gnn_bo': _L2_gnn_in['bo'], 'L2_gnn_ln1_g': _L2_gnn_in['ln1_g'], 'L2_gnn_ln1_b': _L2_gnn_in['ln1_b'], 'L2_gnn_ln2_g': _L2_gnn_in['ln2_g'], 'L2_gnn_ln2_b': _L2_gnn_in['ln2_b'], 'L2_gnn_w1': _L2_gnn_in['w1'], 'L2_gnn_b1': _L2_gnn_in['b1'], 'L2_gnn_w2': _L2_gnn_in['w2'], 'L2_gnn_b2': _L2_gnn_in['b2'], 'L2_gnn_out_g': _L2_gnn_in['out_g'], 'L2_gnn_out_b': _L2_gnn_in['out_b'], 'L3_gnn_W1': _L3_gnn_in['W1'], 'L3_gnn_b1': _L3_gnn_in['b1'], 'L3_gnn_gamma': _L3_gnn_in['gamma'], 'L3_gnn_beta': _L3_gnn_in['beta'], 'L3_gnn_W2': _L3_gnn_in['W2'], 'L3_gnn_b2': _L3_gnn_in['b2']}

def reference(x, src, dst, edge_type_3, node_type_4, L0_gnn_Wl0, L0_gnn_Wr0, L0_gnn_att0, L0_gnn_b0, L0_gnn_Wl1, L0_gnn_Wr1, L0_gnn_att1, L0_gnn_b1, L1_gnn_W, L1_gnn_attn_l, L1_gnn_attn_r, L2_gnn_W_Q, L2_gnn_W_K, L2_gnn_W_V, L2_gnn_W_E, L2_gnn_mu, L2_gnn_Wo, L2_gnn_bo, L2_gnn_ln1_g, L2_gnn_ln1_b, L2_gnn_ln2_g, L2_gnn_ln2_b, L2_gnn_w1, L2_gnn_b1, L2_gnn_w2, L2_gnn_b2, L2_gnn_out_g, L2_gnn_out_b, L3_gnn_W1, L3_gnn_b1, L3_gnn_gamma, L3_gnn_beta, L3_gnn_W2, L3_gnn_b2):
    import jax
    import jax.numpy as jnp

    def _L0_gnn_ref(x, edge_index, Wl0, Wr0, att0, b0, Wl1, Wr1, att1, b1):
        import jax, jax.numpy as jnp
        import numpy as np
        N, E, C_IN = (50000, 25000, 256)
        H = 2
        C1 = 64
        C2 = 128
        NEG_SLOPE = 0.2

        def glorot(key, shape):
            fan_in, fan_out = (shape[0], shape[1])
            lim = jnp.sqrt(6.0 / (fan_in + fan_out))
            return jax.random.uniform(key, shape, jnp.float32, -lim, lim)

        def gatv2_conv(x, src, dst, Wl, Wr, att, b, heads, c_out):
            n = x.shape[0]
            xl = (x @ Wl).reshape(n, heads, c_out)
            xr = (x @ Wr).reshape(n, heads, c_out)
            e = jax.nn.leaky_relu(xl[src] + xr[dst], NEG_SLOPE)
            logit = jnp.einsum('ehc,hc->eh', e, att)
            m = jax.ops.segment_max(logit, dst, num_segments=n)
            a = jnp.exp(logit - m[dst])
            denom = jax.ops.segment_sum(a, dst, num_segments=n)
            alpha = a / denom[dst]
            out = jax.ops.segment_sum(alpha[:, :, None] * xl[src], dst, num_segments=n)
            return out.reshape(n, heads * c_out) + b
        n = x.shape[0]
        loops = jnp.arange(n, dtype=edge_index.dtype)
        src = jnp.concatenate([edge_index[0], loops])
        dst = jnp.concatenate([edge_index[1], loops])
        h = gatv2_conv(x, src, dst, Wl0, Wr0, att0, b0, H, C1)
        h = jax.nn.relu(h)
        out = gatv2_conv(h, src, dst, Wl1, Wr1, att1, b1, H, C2)
        return out

    def _L1_gnn_ref(x, edge_index, W, attn_l, attn_r):
        import jax, jax.numpy as jnp
        import numpy as np
        N = 50000
        IN_CH = 256
        HEADS = 8
        OUT_CH = 32
        E = 25000
        num_nodes = x.shape[0]
        xp = (x @ W.T).reshape(num_nodes, HEADS, OUT_CH).astype(jnp.float32)
        loops = jnp.arange(num_nodes, dtype=edge_index.dtype)
        src = jnp.concatenate([edge_index[0], loops])
        dst = jnp.concatenate([edge_index[1], loops])
        alpha_l = (xp * attn_l).sum(-1)[src]
        alpha_r = (xp * attn_r).sum(-1)[dst]
        alpha = jax.nn.leaky_relu(alpha_l + alpha_r, negative_slope=0.2)
        alpha = jnp.exp(alpha - alpha.max(axis=0, keepdims=True))
        alpha_sum = jax.ops.segment_sum(alpha, dst, num_segments=num_nodes)
        alpha = alpha / jnp.maximum(alpha_sum[dst], 1e-06)
        msgs = alpha[:, :, None] * xp[src]
        out = jax.ops.segment_sum(msgs, dst, num_segments=num_nodes)
        return out.reshape(num_nodes, HEADS * OUT_CH)

    def _L2_gnn_ref(x, edge_index, edge_type, node_type, W_Q, W_K, W_V, W_E, mu, Wo, bo, ln1_g, ln1_b, ln2_g, ln2_b, w1, b1, w2, b2, out_g, out_b):
        import jax, jax.numpy as jnp
        import numpy as np
        import math
        L, H, HD, D = (3, 8, 32, 256)
        TN, TE = (4, 3)

        def _layer_norm(x, g, b, eps=1e-05):
            m = jnp.mean(x, axis=-1, keepdims=True)
            v = jnp.var(x, axis=-1, keepdims=True)
            return (x - m) / jnp.sqrt(v + eps) * g + b

        def _typed_transform(xh, W, types):
            out = jnp.zeros_like(xh)
            for t in range(W.shape[0]):
                y = jnp.einsum('mhd,hde->mhe', xh, W[t])
                out = jnp.where((types == t)[:, None, None], y, out)
            return out
        N = x.shape[0]
        src, dst = (edge_index[0], edge_index[1])
        scale = math.sqrt(HD)
        for l in range(L):
            xh = x.reshape(N, H, HD)
            Q = _typed_transform(xh, W_Q[l], node_type)
            K = _typed_transform(xh, W_K[l], node_type)
            V = _typed_transform(xh, W_V[l], node_type)
            q_dst = Q[dst]
            kt = _typed_transform(K[src], W_E[l], edge_type)
            scores = jnp.sum(q_dst * kt, axis=-1) / scale
            scores = scores * mu[l].T[edge_type]
            m = jax.ops.segment_max(scores, dst, num_segments=N)
            m = jnp.maximum(m, -1000000000.0)
            e = jnp.exp(scores - m[dst])
            s = jax.ops.segment_sum(e, dst, num_segments=N)
            w = e / (s[dst] + 1e-10)
            agg = jax.ops.segment_sum(V[src] * w[..., None], dst, num_segments=N)
            attn = agg.reshape(N, D) @ Wo[l] + bo[l]
            x = _layer_norm(x + attn, ln1_g[l], ln1_b[l])
            h = jax.nn.gelu(x @ w1[l] + b1[l], approximate=False) @ w2[l] + b2[l]
            x = _layer_norm(x + h, ln2_g[l], ln2_b[l])
        return _layer_norm(x, out_g, out_b)

    def _L3_gnn_ref(x, edge_index, W1, b1, gamma, beta, W2, b2):
        import jax, jax.numpy as jnp
        import numpy as np
        N_NODES = 3125
        N_EDGES = 10000
        D_IN, D_HID, D_OUT = (256, 1024, 256)
        BN_EPS = 1e-05
        src, dst = (edge_index[0], edge_index[1])
        agg = jax.ops.segment_sum(x[src], dst, num_segments=x.shape[0])
        h = agg + x
        h1 = h @ W1 + b1
        mean = jnp.mean(h1, axis=0)
        var = jnp.mean(jnp.square(h1 - mean), axis=0)
        h1 = (h1 - mean) * jax.lax.rsqrt(var + BN_EPS) * gamma + beta
        h1 = jax.nn.relu(h1)
        out = jax.nn.relu(h1 @ W2 + b2)
        return out
    edge_index = jnp.stack([src, dst])
    x = _layernorm(x + _L0_gnn_ref(x, edge_index, L0_gnn_Wl0, L0_gnn_Wr0, L0_gnn_att0, L0_gnn_b0, L0_gnn_Wl1, L0_gnn_Wr1, L0_gnn_att1, L0_gnn_b1), axis=-1)
    x = _layernorm(x + _L1_gnn_ref(x, edge_index, L1_gnn_W, L1_gnn_attn_l, L1_gnn_attn_r), axis=-1)
    x = _layernorm(x + _L2_gnn_ref(x, edge_index, edge_type_3, node_type_4, L2_gnn_W_Q, L2_gnn_W_K, L2_gnn_W_V, L2_gnn_W_E, L2_gnn_mu, L2_gnn_Wo, L2_gnn_bo, L2_gnn_ln1_g, L2_gnn_ln1_b, L2_gnn_ln2_g, L2_gnn_ln2_b, L2_gnn_w1, L2_gnn_b1, L2_gnn_w2, L2_gnn_b2, L2_gnn_out_g, L2_gnn_out_b), axis=-1)
    x = _layernorm(x + _L3_gnn_ref(x, edge_index, L3_gnn_W1, L3_gnn_b1, L3_gnn_gamma, L3_gnn_beta, L3_gnn_W2, L3_gnn_b2), axis=-1)
    return x

_drawn_inputs = setup_inputs


def setup_inputs(seed=0):
    import zlib

    import numpy as np

    out = dict(_drawn_inputs(seed))
    spreads = {'L0_gnn_b0': (0.0, 0.1),
     'L0_gnn_b1': (0.0, 0.1),
     'L2_gnn_mu': (1.0, 0.6),
     'L2_gnn_bo': (0.0, 0.1),
     'L2_gnn_ln1_g': (1.0, 0.2),
     'L2_gnn_ln1_b': (0.0, 0.1),
     'L2_gnn_ln2_g': (1.0, 0.2),
     'L2_gnn_ln2_b': (0.0, 0.1),
     'L2_gnn_b1': (0.0, 0.1),
     'L2_gnn_b2': (0.0, 0.1),
     'L2_gnn_out_g': (1.0, 0.2),
     'L2_gnn_out_b': (0.0, 0.1),
     'L3_gnn_b1': (0.0, 0.8),
     'L3_gnn_gamma': (1.0, 0.2),
     'L3_gnn_beta': (0.0, 0.1),
     'L3_gnn_b2': (0.0, 0.1)}
    factors = {'L0_gnn_Wr1': 8.0,
     'L0_gnn_att1': 2.742,
     'L2_gnn_W_Q': 8.0,
     'L2_gnn_W_K': 8.0,
     'L2_gnn_W_V': 4.651,
     'L2_gnn_W_E': 8.0,
     'L2_gnn_Wo': 4.798}
    for name, (base, spread) in spreads.items():
        noise = np.random.default_rng([zlib.crc32(name.encode()), seed]).standard_normal(out[name].shape)
        drawn = base * np.exp(spread * noise) if base else spread * noise
        out[name] = jnp.asarray(drawn.astype(out[name].dtype))
    for name, factor in factors.items():
        out[name] = (out[name] * factor).astype(out[name].dtype)
    return out
```

```python
from contextlib import ExitStack

import concourse.bass as bass
from concourse import mybir

F32 = mybir.dt.float32
I32 = mybir.dt.int32
ALU = mybir.AluOpType
ACT = mybir.ActivationFunctionType
AX = mybir.AxisListType.X
RMAX = bass.bass_isa.ReduceOp.max

P = 128
N, D, E = 3125, 256, 50000
NT = -(-N // P)
NLAST = N - (NT - 1) * P
NP = NT * P
GT = 2
GRP = (E + N + NT * (GT * P - 1)) // (GT * P)
BT = 16
BG = BT // GT
NB = -(-GRP // BG)
T = NB * BT
H = 8
EC = -(-E // P)
RC = EC + NT
SC = 16
SU = 17
BIG = 2.0 ** 100
PADSEG, PADLOC, PADDST = 9999.0, 999.0, 4000
LH = 64
assert EC % SU == 0 and NB % 2 == 1 and NT % 2 == 1 and GRP <= NB * BG


class Signal:

    def __init__(self, handle):
        self.sem, self.base = handle, 0

    def at(self, n):
        return self.base + n


def ds(start, n):
    return bass.ds(start, n)


def wait(eng, signal, n):
    if not isinstance(n, int) or n > 0:
        eng.wait_ge(signal.sem, signal.at(n))


def gnn_kernel(nc, A, out):
    ctx = ExitStack()
    with ctx:
        def sb(name, shape, dt=F32):
            return ctx.enter_context(nc.sbuf_tensor(name, shape, dt))

        def sig(name):
            return Signal(ctx.enter_context(nc.semaphore(name)))

        def dram(name, shape, dt=F32):
            return nc.dram_tensor(name, shape, dt, kind="Internal").ap()

        tab_l0a, tab_l0b, tab_l1 = dram("tab_l0a", (NP, 128)), dram("tab_l0b", (NP, D)), dram("tab_l1", (NP, D + H))
        tab_l2, tab_l3 = dram("tab_l2", (3 * NP, 2 * D)), dram("tab_l3", (NP, D))
        residual = dram("residual", (NP, D))
        base_dram = dram("base_dram", (LH * LH, 1))
        rec_dram = dram("rec_dram", (P * T, 8), I32)
        seg_dram = dram("seg_dram", (1, T * P + 2))
        hid_dram = dram("hid_dram", (8, P, NP))

        ident = sb("ident", [P, P])
        ones = sb("ones", [P, P])
        iota_row = sb("iota_row", [P, P])
        lane_mask = sb("lane_mask", [P, 16])
        same_head = sb("same_head", [P, P])
        head_col = sb("head_col", [P, H])
        slot_src = sb("slot_src", [P, T], I32)
        slot_typed = sb("slot_typed", [P, T], I32)
        slot_loc = sb("slot_loc", [P, T])
        slot_bar = sb("slot_bar", [P, T])
        border = sb("border", [P, NB * (P + 1)])
        tile_border = sb("tile_border", [P, NB * 33])
        straddle = sb("straddle", [P, NB])
        block_of = sb("block_of", [1, GRP + 8], I32)
        type_of = sb("type_of", [P, NT])
        X = sb("X", [P, NT, D])
        acc = sb("acc", [P, NT, 272])
        arena = sb("arena", [P, 24640])
        QTAB = 2 * BT * 512
        qtab = arena[:, QTAB:QTAB + NT * D].rearrange("p (j c) -> p j c", j=NT)
        small = sb("small", [P, 256])

        PS = [ctx.enter_context(nc.psum_tensor(f"bank{i}", [P, 512], F32)) for i in range(8)]

        loaded = sig("loaded")
        step = sig("step")
        made = sig("made")
        converted = sig("converted")
        tick = sig("tick")
        multiplied = sig("multiplied")

        def constants():
            ii = arena[:, 0:P].bitcast(I32)
            pi = arena[:, P:P + 1].bitcast(I32)
            w = arena[:, 2 * P:3 * P].bitcast(I32)
            v = arena[:, 3 * P:4 * P].bitcast(I32)
            pf = arena[:, 4 * P:4 * P + 4]
            cf = arena[:, 5 * P:6 * P]
            with nc.Block() as block:
                @block.gpsimd
                def _(pool):
                    pool.iota(ii, pattern=[[1, P]], base=0, channel_multiplier=0).then_inc(made.sem, 1)
                    pool.iota(pi, pattern=[[1, 1]], base=0, channel_multiplier=1).then_inc(made.sem, 1)

                @block.vector
                def _(dve):
                    n = 0

                    def link(op):
                        nonlocal n
                        n += 1
                        op.then_inc(step.sem, 1)
                        dve.wait_ge(step.sem, step.at(n))

                    dve.wait_ge(made.sem, made.at(2))
                    link(dve.memset(ones[:, :], 1.0))
                    link(dve.tensor_copy(iota_row[:, :], ii))
                    link(dve.tensor_copy(pf[:, 0:1], pi))
                    link(dve.tensor_scalar(ident[:, :], iota_row[:, :], pf[:, 0:1], None, ALU.is_equal))
                    link(dve.tensor_scalar(w[:, 0:1], pi, 15, None, ALU.bitwise_and))
                    link(dve.tensor_scalar(v[:, 0:1], pi, 4, None, ALU.logical_shift_right))
                    link(dve.tensor_copy(pf[:, 1:2], w[:, 0:1]))
                    link(dve.tensor_copy(pf[:, 2:3], v[:, 0:1]))
                    link(dve.tensor_scalar(lane_mask[:, :], iota_row[:, 0:16], pf[:, 1:2], None, ALU.is_equal))
                    link(dve.tensor_scalar(head_col[:, :], iota_row[:, 0:H], pf[:, 2:3], None, ALU.is_equal))
                    link(dve.tensor_scalar(w, ii, 4, None, ALU.logical_shift_right))
                    link(dve.tensor_copy(cf, w))
                    link(dve.tensor_scalar(same_head[:, :], cf, pf[:, 2:3], None, ALU.is_equal))
                    step.base += n
            made.base += 2

        hi, lo = arena[:, 0:EC], arena[:, RC:RC + EC]
        pos = arena[:, 2 * RC:3 * RC]
        dst_i = arena[:, 3 * RC:3 * RC + EC].bitcast(I32)
        src_i = arena[:, 4 * RC:4 * RC + EC].bitcast(I32)
        typ_i = arena[:, 5 * RC:5 * RC + EC].bitcast(I32)
        recf = arena[:, 6 * RC:14 * RC].rearrange("p (c f) -> p c f", f=8)
        rec = arena[:, 6 * RC:14 * RC].bitcast(I32).rearrange("p (c f) -> p c f", f=8)
        row_f, row_i = arena[:, 14 * RC:15 * RC], arena[:, 15 * RC:16 * RC].bitcast(I32)
        row_i2 = arena[:, 16 * RC:17 * RC].bitcast(I32)
        W0 = 17 * RC
        slots = arena[:, 13312:13312 + 8 * T].rearrange("p (t f) -> p t f", f=8)
        slots_i = arena[:, 13312:13312 + 8 * T].bitcast(I32).rearrange("p (t f) -> p t f", f=8)
        seg_lane = arena[:, 17024:17024 + NB * (P + 2)].rearrange("p (b s) -> p b s", b=NB)
        differs = arena[:, 20800:24640]

        def view(off, n):
            return arena[:, W0 + off:W0 + off + n]

        oh_hi = view(0, SU * LH).rearrange("p (u c) -> p u c", u=SU)
        oh_lo = view(SU * LH, SU * LH).rearrange("p (u c) -> p u c", u=SU)
        hiT = view(2 * SU * LH, 2 * P).rearrange("p (u c) -> p u c", u=2)
        before = view(2 * SU * LH + 2 * P, 2 * P).rearrange("p (u c) -> p u c", u=2)
        next_slot = view(2 * SU * LH + 4 * P, SU * LH).rearrange("p (u c) -> p u c", u=SU)
        picked = view(3 * SU * LH + 4 * P, 2 * LH).rearrange("p (u c) -> p u c", u=2)
        pos17 = view(3 * SU * LH + 6 * P, SU)
        V1 = 3 * SU * LH + 6 * P + 32
        tri = view(V1, P)
        scr = [view(V1 + P + LH * i, LH) for i in range(12)]
        V2 = V1 + P + 12 * LH
        self_pos = view(V2, NT)
        group_f = view(V2 + 32, GRP)
        block_f = view(V2 + 32 + GRP, GRP)
        pads = acc[:, :, :].rearrange("p a b -> p (a b)")[:, 0:T * 8].rearrange("p (t f) -> p t f", f=8)
        V3 = V2 + 32 + 2 * GRP
        stage_rec = view(V3, 2 * SC * 8).bitcast(I32).rearrange("p (a u f) -> p a u f", a=2, u=SC)
        stage_row = view(V3 + 2 * SC * 8, 2 * SC).bitcast(I32).rearrange("p (a u) -> p a u", a=2)
        assert W0 + V3 + 18 * SC <= 13312

        onehot = sig("onehot")
        turned = sig("turned")
        turned_sb = sig("turned_sb")
        paired = sig("paired")
        masked = sig("masked")
        ranked = sig("ranked")
        taken = sig("taken")
        counted = sig("counted")
        kept = sig("kept")
        scattered = sig("scattered")

        def load_edges():
            with nc.Block() as block:
                @block.vector
                def _(dve):
                    dve.memset(dst_i, PADDST).then_inc(step.sem, 1)
                    dve.memset(src_i, 0).then_inc(step.sem, 1)
                    dve.memset(typ_i, 0).then_inc(step.sem, 1)
                    dve.memset(X[:, NT - 1, :], 0.0).then_inc(step.sem, 1)
                    dve.memset(type_of[:, :], 0.0).then_inc(step.sem, 1)
                    dve.memset(pads[:, :, 0:2], 0.0).then_inc(step.sem, 1)
                    dve.memset(pads[:, :, 2:3], PADSEG).then_inc(step.sem, 1)
                    dve.memset(pads[:, :, 3:4], PADLOC).then_inc(step.sem, 1)
                    dve.memset(pads[:, :, 4:8], 0.0).then_inc(step.sem, 1)

                @block.sync
                def _(sp):
                    sp.wait_ge(step.sem, step.at(9))
                    full, rest = (P - 1) * EC, E - (P - 1) * EC
                    for tile, name in ((dst_i, "dst"), (src_i, "src"), (typ_i, "edge_type_3")):
                        sp.dma_start(tile[0:P - 1, :], A[name][0:full].rearrange("(p c) -> p c", c=EC))\
                          .then_inc(loaded.sem, 16)
                        sp.dma_start(tile[P - 1:P, 0:rest], A[name][full:E].rearrange("(p c) -> p c", p=1))\
                          .then_inc(loaded.sem, 16)
                    sp.dma_start(X[:, 0:NT - 1, :], A["x"][0:(NT - 1) * P, :].rearrange("(j p) c -> p j c", p=P))\
                      .then_inc(loaded.sem, 16)
                    sp.dma_start(X[0:NLAST, NT - 1, :], A["x"][(NT - 1) * P:N, :]).then_inc(loaded.sem, 16)
                    sp.dma_start(rec_dram[:, :].rearrange("(p t) f -> p (t f)", p=P),
                                 pads[:, :, :].rearrange("p t f -> p (t f)").bitcast(I32)).then_inc(loaded.sem, 16)
                    sp.wait_ge(loaded.sem, loaded.at(16 * 9))

                @block.gpsimd
                def _(pool):
                    pool.wait_ge(step.sem, step.at(5))
                    with nc.allow_non_contiguous_dma(reason="3125 node types, once"):
                        pool.dma_start(type_of[:, 0:NT - 1],
                                       A["node_type_4"][0:(NT - 1) * P].rearrange("(j p) -> p j", p=P))\
                            .then_inc(converted.sem, 16)
                        pool.dma_start(type_of[0:NLAST, NT - 1:NT],
                                       A["node_type_4"][(NT - 1) * P:N].rearrange("(p a) -> p a", a=1))\
                            .then_inc(converted.sem, 16)
                    pool.wait_ge(converted.sem, converted.at(32))
            step.base += 9
            loaded.base += 16 * 9
            converted.base += 32

        def histogram():
            with nc.Block() as block:
                @block.vector
                def _(dve):
                    n = 0

                    def link(op):
                        nonlocal n
                        n += 1
                        op.then_inc(step.sem, 1)
                        dve.wait_ge(step.sem, step.at(n))

                    link(dve.tensor_scalar(row_i[:, 0:EC], dst_i, 6, None, ALU.logical_shift_right))
                    link(dve.tensor_copy(hi, row_i[:, 0:EC]))
                    link(dve.tensor_scalar(row_i[:, 0:EC], dst_i, LH - 1, None, ALU.bitwise_and))
                    link(dve.tensor_copy(lo, row_i[:, 0:EC]))

                    def body(i):
                        for u in range(SU):
                            if not (isinstance(i, int) and i == 0):
                                dve.wait_ge(counted.sem, counted.at(SU * i + u - SU + 1))
                            c = SU * i + u
                            dve.tensor_scalar(oh_hi[:, u, :], iota_row[:, 0:LH], hi[:, ds(c, 1)], None, ALU.is_equal)\
                               .then_inc(kept.sem, 1)
                            dve.tensor_scalar(oh_lo[:, u, :], iota_row[:, 0:LH], lo[:, ds(c, 1)], None, ALU.is_equal)\
                               .then_inc(onehot.sem, 1)

                    body(0)
                    with dve.Fori(1, EC // SU - 1) as i:
                        body(i)
                    body(EC // SU - 1)
                    step.base += n

                @block.tensor
                def _(pe):
                    def body(i, first=False, last=False):
                        for u in range(SU):
                            pe.wait_ge(onehot.sem, onehot.at(SU * i + u + 1))
                            pe.matmul(PS[0][0:LH, 0:LH], oh_hi[:, u, :], oh_lo[:, u, :], start=first and u == 0,
                                      stop=last and u == SU - 1).then_inc(counted.sem, 1)

                    body(0, first=True)
                    with pe.Fori(1, EC // SU - 1) as i:
                        body(i)
                    body(EC // SU - 1, last=True)
            onehot.base += EC
            kept.base += EC
            counted.base += EC

        def place_nodes():
            rows = iota_row[0:LH, 0:LH]
            pcol, chalf, codd, q, cnt, run, zero, m_pair, m_before, m_prev, itf, it2f = [s[0:LH, :] for s in scr]
            it, it2 = itf.bitcast(I32), it2f.bitcast(I32)
            with nc.Block() as block:
                @block.vector
                def _(dve):
                    n = 0

                    def link(op):
                        nonlocal n
                        n += 1
                        op.then_inc(step.sem, 1)
                        dve.wait_ge(step.sem, step.at(n))

                    link(dve.tensor_tensor(small[:, 128:256], ident[:, :], iota_row[:, :], ALU.mult))
                    link(dve.tensor_reduce(small[:, 0:1], small[:, 128:256], AX, ALU.add))
                    link(dve.tensor_scalar(tri, iota_row[:, :], small[:, 0:1], None, ALU.is_gt))
                    link(dve.tensor_copy(it[:, 0:1], small[0:LH, 0:1]))
                    link(dve.tensor_scalar(it[:, 1:2], it[:, 0:1], 1, None, ALU.logical_shift_right))
                    link(dve.tensor_scalar(it[:, 2:3], it[:, 0:1], 1, None, ALU.bitwise_and))
                    link(dve.tensor_copy(pcol[:, 0:3], it[:, 0:3]))
                    link(dve.tensor_copy(it, rows))
                    link(dve.tensor_scalar(it2, it, 1, None, ALU.logical_shift_right))
                    link(dve.tensor_copy(chalf, it2))
                    link(dve.tensor_scalar(it2, it, 1, None, ALU.bitwise_and))
                    link(dve.tensor_copy(codd, it2))
                    link(dve.tensor_scalar(m_pair, chalf, pcol[:, 1:2], None, ALU.is_equal))
                    link(dve.tensor_scalar(q[:, 0:1], pcol[:, 2:3], -1.0, 1.0, ALU.mult, ALU.add))
                    link(dve.tensor_scalar(m_before, chalf, pcol[:, 1:2], q[:, 0:1], ALU.is_gt, ALU.mult))
                    link(dve.tensor_tensor(m_prev, m_pair, codd, ALU.mult))
                    link(dve.tensor_scalar(m_prev, m_prev, q[:, 0:1], None, ALU.mult))
                    link(dve.tensor_scalar(q[:, 1:2], pcol[:, 0:1], float(LH), None, ALU.mult))
                    link(dve.tensor_scalar(run, rows, q[:, 1:2], float(N), ALU.add, ALU.is_lt))
                    link(dve.tensor_tensor(cnt, PS[0][0:LH, 0:LH], run, ALU.add))
                    link(dve.tensor_reduce(q[:, 2:3], cnt, AX, ALU.add))
                    dve.sem_inc(rows_summed.sem, 1)
                    dve.wait_ge(multiplied.sem, multiplied.at(2))
                    link(dve.tensor_scalar(q[:, 3:4], PS[1][0:LH, 0:1], float(GT * P - 1), None, ALU.add))
                    link(dve.tensor_copy(it[:, 0:1], q[:, 3:4]))
                    link(dve.tensor_scalar(it[:, 1:2], it[:, 0:1], (GT * P).bit_length() - 1, None,
                                           ALU.logical_shift_right))
                    link(dve.tensor_copy(q[:, 4:5], it[:, 1:2]))
                    dve.sem_inc(rows_summed.sem, 1)
                    dve.wait_ge(multiplied.sem, multiplied.at(3))
                    link(dve.tensor_copy(q[:, 5:6], PS[3][0:LH, 0:1]))
                    link(dve.tensor_copy(q[:, 8:9], PS[2][0:LH, 0:1]))
                    link(dve.tensor_scalar(q[:, 6:7], q[:, 5:6], float(GT * P), q[:, 8:9], ALU.mult, ALU.add))
                    link(dve.memset(zero, 0.0))
                    link(dve.tensor_tensor_scan(run, zero, cnt, 0.0, ALU.add, ALU.add))
                    link(dve.tensor_tensor(run, run, cnt, ALU.subtract))
                    link(dve.tensor_scalar(run, run, q[:, 6:7], None, ALU.add))
                    dve.sem_inc(placed.sem, 1)
                    link(dve.tensor_scalar(next_slot[0:LH, 0, :], run, 1.0, None, ALU.add))
                    link(dve.tensor_scalar(q[:, 7:8], pcol[:, 0:1], float(2 * NT), q[:, 0:1], ALU.is_lt, ALU.mult))
                    dve.wait_ge(made.sem, made.at(1))
                    link(dve.tensor_scalar(block_f[0:LH, :], group_f[0:LH, :], q[:, 5:6], q[:, 7:8],
                                           ALU.is_ge, ALU.mult))
                    dve.sem_inc(rows_summed.sem, 1)
                    dve.wait_ge(multiplied.sem, multiplied.at(4))
                    link(dve.tensor_scalar(block_f, PS[4][:, 0:GRP], -1.0, None, ALU.add))
                    link(dve.memset(block_of[:, :], 0))
                    link(dve.tensor_copy(block_of[0:1, 0:GRP], block_f[0:1, :]))
                    marks["step"] = n

                @block.gpsimd
                def _(pool):
                    pool.iota(group_f, pattern=[[1, GRP]], base=0, channel_multiplier=0,
                              allow_small_or_imprecise_dtypes=True).then_inc(made.sem, 1)

                @block.tensor
                def _(pe):
                    pe.wait_ge(rows_summed.sem, rows_summed.at(1))
                    pe.matmul(PS[1][0:LH, 0:1], m_pair, q[:, 2:3], start=True, stop=True).then_inc(multiplied.sem, 1)
                    pe.matmul(PS[2][0:LH, 0:1], m_prev, q[:, 2:3], start=True, stop=True).then_inc(multiplied.sem, 1)
                    pe.wait_ge(rows_summed.sem, rows_summed.at(2))
                    pe.matmul(PS[3][0:LH, 0:1], m_before, q[:, 4:5], start=True, stop=True)\
                      .then_inc(multiplied.sem, 1)
                    pe.wait_ge(rows_summed.sem, rows_summed.at(3))
                    pe.matmul(PS[4][:, 0:GRP], ones[0:LH, :], block_f[0:LH, :], start=True, stop=True)\
                      .then_inc(multiplied.sem, 1)

                @block.sync
                def _(sp):
                    sp.wait_ge(placed.sem, placed.at(1))
                    sp.dma_start(base_dram[:, :].rearrange("(h l) a -> h (l a)", h=LH), run).then_inc(loaded.sem, 16)
                    sp.wait_ge(loaded.sem, loaded.at(16))
                    with nc.allow_non_contiguous_dma(reason="one number for each node, once"):
                        sp.dma_start(self_pos, base_dram[0:NP, :].rearrange("(j p) a -> p (j a)", p=P))\
                          .then_inc(loaded.sem, 16)
                    sp.wait_ge(loaded.sem, loaded.at(32))
            step.base += marks["step"]
            made.base += 1
            loaded.base += 32
            multiplied.base += 4
            rows_summed.base += 3
            placed.base += 1

        rows_summed, placed, added = sig("rows_summed"), sig("placed"), sig("added")
        marks = {}

        def rank_edges():
            def two_deep(i, u):
                return SU * i + (u - 1 if u >= 2 else -u)

            def every(eng, body):
                body(0)
                with eng.Fori(1, EC // SU) as i:
                    body(i)

            with nc.Block() as block:
                @block.vector
                def _(dve):
                    def body(i):
                        for v in range(SU + 4):
                            if v < SU:
                                u, c = v, SU * i + v
                                wait(dve, ranked, c - SU + 1)
                                dve.tensor_scalar(oh_hi[:, u, :], iota_row[:, 0:LH], hi[:, ds(c, 1)], None,
                                                  ALU.is_equal).then_inc(kept.sem, 1)
                                wait(dve, masked, c - SU + 1)
                                dve.tensor_scalar(oh_lo[:, u, :], iota_row[:, 0:LH], lo[:, ds(c, 1)], None,
                                                  ALU.is_equal).then_inc(onehot.sem, 1)
                            if 0 <= v - 2 < SU:
                                u, c = v - 2, SU * i + v - 2
                                wait(dve, paired, c + 1)
                                wait(dve, ranked, two_deep(i, u))
                                dve.tensor_tensor(before[:, u % 2, :], PS[2 + u % 2][:, 0:P], tri,
                                                  ALU.mult).then_inc(kept.sem, 1)
                                wait(dve, added, c)
                                wait(dve, ranked, c + 2 - SU)
                                dve.tensor_tensor(next_slot[0:LH, (u + 1) % SU, :], next_slot[0:LH, u, :],
                                                  PS[2 + u % 2][0:LH, P:P + LH], ALU.add)\
                                   .then_inc(added.sem, 1)
                            if 0 <= v - 4 < SU:
                                u, c = v - 4, SU * i + v - 4
                                wait(dve, ranked, c + 1)
                                wait(dve, masked, two_deep(i, u))
                                dve.tensor_tensor(picked[:, u % 2, :], PS[4 + u % 2][:, 0:LH],
                                                  oh_lo[:, u, :], ALU.mult).then_inc(taken.sem, 1)
                                wait(dve, taken, c + 1)
                                if u == 0:
                                    wait(dve, counted, i)
                                dve.tensor_reduce(pos17[:, u:u + 1], picked[:, u % 2, :], AX, ALU.add)\
                                   .then_inc(masked.sem, 1)
                        wait(dve, masked, SU * i + SU)
                        dve.tensor_copy(pos[:, ds(SU * i, SU)], pos17).then_inc(counted.sem, 1)

                    every(dve, body)

                @block.tensor
                def _(pe):
                    def body(i):
                        for v in range(SU + 3):
                            if v < SU:
                                u, c = v, SU * i + v
                                wait(pe, onehot, c + 1)
                                wait(pe, turned_sb, two_deep(i, u))
                                pe.matmul(PS[u % 2][0:LH, 0:P], oh_hi[:, u, :], ident[:, :],
                                          start=True, stop=True).then_inc(turned.sem, 1)
                            if 0 <= v - 3 < SU:
                                u, c = v - 3, SU * i + v - 3
                                wait(pe, added, c + 1)
                                wait(pe, taken, two_deep(i, u))
                                pe.matmul(PS[4 + u % 2][:, 0:LH], hiT[0:LH, u % 2, :],
                                          next_slot[0:LH, u, :], start=True, stop=False)
                                pe.matmul(PS[4 + u % 2][:, 0:LH], before[:, u % 2, :], oh_lo[:, u, :],
                                          start=False, stop=True).then_inc(ranked.sem, 1)
                            if 0 <= v - 1 < SU:
                                u, c = v - 1, SU * i + v - 1
                                wait(pe, turned_sb, c + 1)
                                wait(pe, added, two_deep(i, u))
                                pe.matmul(PS[2 + u % 2][0:LH, P:P + LH], oh_hi[:, u, :], oh_lo[:, u, :],
                                          start=True, stop=True)
                                pe.matmul(PS[2 + u % 2][:, 0:P], hiT[0:LH, u % 2, :], hiT[0:LH, u % 2, :],
                                          start=True, stop=True).then_inc(paired.sem, 1)

                    every(pe, body)

                @block.scalar
                def _(act):
                    def body(i):
                        for u in range(SU):
                            wait(act, turned, SU * i + u + 1)
                            wait(act, ranked, two_deep(i, u))
                            act.activation(hiT[0:LH, u % 2, :], PS[u % 2][0:LH, 0:P], ACT.Copy)\
                               .then_inc(turned_sb.sem, 1)

                    every(act, body)
            for s in (onehot, turned, turned_sb, paired, added, ranked, taken, masked):
                s.base += EC
            kept.base += 2 * EC
            counted.base += EC // SU

        def own_wait(eng, signal, n):
            if not isinstance(n, int) or n > 0:
                eng.wait_ge(signal.sem, signal.at(n))
                eng.sem_inc(tick.sem, 1)

        staged, sent = sig("staged"), [sig("sent0"), sig("sent1")]

        def scatter_records():
            with nc.Block() as block:
                @block.vector
                def _(dve):
                    n = 0

                    def link(op):
                        nonlocal n
                        n += 1
                        op.then_inc(step.sem, 1)
                        dve.wait_ge(step.sem, step.at(n))

                    ed, se = slice(0, EC), slice(EC, RC)
                    nowhere = arena[:, 0:RC]
                    link(dve.memset(recf, 0.0))
                    link(dve.tensor_copy(rec[:, ed, 0], src_i))
                    link(dve.tensor_copy(row_f[:, ed], src_i))
                    link(dve.tensor_copy(recf[:, ed, 4], typ_i))
                    link(dve.scalar_tensor_tensor(rec[:, ed, 1], recf[:, ed, 4], float(NP), row_f[:, ed],
                                                  ALU.mult, ALU.add))
                    link(dve.memset(recf[:, ed, 4], 0.0))
                    link(dve.tensor_copy(recf[:, ed, 2], dst_i))
                    link(dve.tensor_scalar(row_i[:, ed], dst_i, P - 1, None, ALU.bitwise_and))
                    link(dve.tensor_copy(recf[:, ed, 3], row_i[:, ed]))
                    link(dve.tensor_scalar(nowhere[:, ed], recf[:, ed, 2], float(PADDST), 2.0 ** 20,
                                           ALU.is_ge, ALU.mult))
                    link(dve.tensor_scalar(recf[:, se, 2], iota_row[:, 0:NT], float(P), small[:, 0:1],
                                           ALU.mult, ALU.add))
                    link(dve.tensor_copy(rec[:, se, 0], recf[:, se, 2]))
                    link(dve.tensor_copy(rec[:, se, 1], recf[:, se, 2]))
                    link(dve.memset(recf[:, se, 4], 0.0))
                    link(dve.tensor_scalar(recf[:, se, 3], recf[:, se, 4], small[:, 0:1], None, ALU.add))
                    link(dve.memset(recf[:, se, 4], -BIG))
                    link(dve.tensor_scalar(nowhere[:, se], recf[:, se, 2], float(N), 2.0 ** 20, ALU.is_ge, ALU.mult))
                    link(dve.tensor_copy(pos[:, se], self_pos))
                    link(dve.tensor_copy(row_i, pos))
                    link(dve.tensor_scalar(row_i2, row_i, P - 1, None, ALU.bitwise_and))
                    link(dve.tensor_copy(row_f, row_i2))
                    link(dve.tensor_scalar(row_i2, row_i, 7, None, ALU.logical_shift_right))
                    link(dve.tensor_copy(pos, row_i2))
                    link(dve.tensor_tensor(nowhere, nowhere, pos, ALU.add))
                    link(dve.scalar_tensor_tensor(row_i, row_f, float(T), nowhere, ALU.mult, ALU.add))
                    marks["step"] = n

                    def body(k, a, use):
                        wait(dve, sent[a], 16 * SC * use)
                        dve.tensor_copy(stage_row[:, a, :], row_i[:, ds(SC * k, SC)]).then_inc(kept.sem, 1)
                        dve.tensor_copy(stage_rec[:, a, :, :], rec[:, ds(SC * k, SC), :]).then_inc(staged.sem, 1)

                    body(0, 0, 0)
                    body(1, 1, 0)
                    with dve.Fori(1, RC // SC // 2) as i:
                        body(2 * i, 0, i)
                        body(2 * i + 1, 1, i)

                @block.gpsimd
                def _(pool):
                    def body(k, a):
                        own_wait(pool, staged, k + 1)
                        for u in range(SC):
                            pool.indirect_dma_start(
                                out=rec_dram[:, :], out_offset=bass.IndirectOffsetOnAxis(ap=stage_row[:, a, u:u + 1], axis=0),
                                in_=stage_rec[:, a, u, :], in_offset=None,
                                bounds_check=P * T - 1, oob_is_err=False).then_inc(sent[a].sem, 16)

                    with pool.Fori(0, RC // SC // 2) as i:
                        body(2 * i, 0)
                        body(2 * i + 1, 1)
                    for a in range(2):
                        own_wait(pool, sent[a], 16 * SC * (RC // SC // 2))
            step.base += marks["step"]
            kept.base += RC // SC
            staged.base += RC // SC
            for a in range(2):
                sent[a].base += 16 * SC * (RC // SC // 2)

        def load_slots():
            q4 = T // 4
            segT = arena[0:q4, 0:4 * P].rearrange("p (q s) -> p q s", q=4)
            with nc.Block() as block:
                @block.sync
                def _(sp):
                    sp.dma_start(slots_i.rearrange("p t f -> p (t f)"),
                                 rec_dram[:, :].rearrange("(p t) f -> p (t f)", p=P)).then_inc(loaded.sem, 16)
                    sp.wait_ge(placed.sem, placed.at(2))
                    for q in range(4):
                        sp.dma_start(seg_dram[0, 1 + q * q4 * P:1 + (q + 1) * q4 * P].rearrange("(t s) -> t s", s=P),
                                     segT[:, q, :]).then_inc(loaded.sem, 16)
                    sp.dma_start(seg_dram[0:1, 0:1], small[0:1, 1:2]).then_inc(loaded.sem, 16)
                    sp.dma_start(seg_dram[0:1, T * P + 1:T * P + 2], small[0:1, 1:2]).then_inc(loaded.sem, 16)
                    sp.wait_ge(loaded.sem, loaded.at(16 * 7))

                @block.vector
                def _(dve):
                    dve.memset(small[:, 1:2], -1.0).then_inc(step.sem, 1)
                    dve.wait_ge(loaded.sem, loaded.at(16))
                    dve.tensor_copy(slot_src[:, :], slots_i[:, :, 0]).then_inc(step.sem, 1)
                    dve.tensor_copy(slot_typed[:, :], slots_i[:, :, 1]).then_inc(step.sem, 1)
                    dve.tensor_copy(slot_loc[:, :], slots[:, :, 3]).then_inc(step.sem, 1)
                    dve.tensor_copy(slot_bar[:, :], slots[:, :, 4]).then_inc(step.sem, 1)
                    dve.wait_ge(multiplied.sem, multiplied.at(4))
                    dve.tensor_copy(segT, PS[0][0:q4, :].rearrange("p (q s) -> p q s", q=4)).then_inc(placed.sem, 1)
                    dve.wait_ge(step.sem, step.at(5))
                    dve.wait_ge(placed.sem, placed.at(1))
                    dve.sem_inc(placed.sem, 1)

                @block.tensor
                def _(pe):
                    pe.wait_ge(loaded.sem, loaded.at(16))
                    for q in range(4):
                        pe.transpose(PS[0][0:q4, q * P:q * P + P], slots[:, q * q4:(q + 1) * q4, 2], ident[:, :])\
                          .then_inc(multiplied.sem, 1)
            loaded.base += 16 * 7
            step.base += 5
            placed.base += 2
            multiplied.base += 4

        def find_borders():
            ends = arena[0:1, 0:2 * T].rearrange("p (k t) -> p k t", k=2)
            tb = tile_border[:, :].rearrange("p (b c) -> p b c", c=33)
            lane, late, early = small[:, 2:3], differs[:, 3744:3744 + 16], differs[:, 3760:3760 + 16]
            firsts, lasts = seg_lane[:, :, 1], seg_lane[:, :, P]
            last_of = PS[0][:, 0:T].rearrange("p (b t) -> p b t", t=BT)
            first_of = PS[1][:, 0:T].rearrange("p (b t) -> p b t", t=BT)
            with nc.Block() as block:
                @block.sync
                def _(sp):
                    seg = seg_dram.tensor
                    for h in range(H):
                        sp.dma_start(seg_lane[16 * h:16 * h + 16, :, :],
                                     bass.AP(tensor=seg, offset=0, ap=[[P, 16], [BT * P, NB], [1, P + 2]]))\
                          .then_inc(loaded.sem, 16)
                    with nc.allow_non_contiguous_dma(reason="a number for each tile, once"):
                        for k, off in ((0, P), (1, 1)):
                            sp.dma_start(ends[:, k, :], bass.AP(tensor=seg, offset=off, ap=[[T * P, 1], [P, T]]))\
                              .then_inc(loaded.sem, 16)
                    sp.wait_ge(loaded.sem, loaded.at(160))

                @block.tensor
                def _(pe):
                    pe.wait_ge(loaded.sem, loaded.at(160))
                    for k in range(2):
                        pe.matmul(PS[k][:, 0:T], ones[0:1, :], ends[:, k, :], start=True, stop=True)\
                          .then_inc(multiplied.sem, 1)

                @block.vector
                def _(dve):
                    n = 0

                    def link(op):
                        nonlocal n
                        n += 1
                        op.then_inc(step.sem, 1)
                        dve.wait_ge(step.sem, step.at(n))

                    link(dve.tensor_tensor(late, lane_mask[:, :], iota_row[:, 0:16], ALU.mult))
                    link(dve.tensor_reduce(lane, late, AX, ALU.add))
                    link(dve.tensor_scalar(late, iota_row[:, 0:16], lane, None, ALU.is_ge))
                    link(dve.tensor_scalar(early, iota_row[:, 0:16], lane, None, ALU.is_le))
                    dve.wait_ge(loaded.sem, loaded.at(160))
                    dif = differs[:, 0:NB * (P + 1)].rearrange("p (b s) -> p b s", b=NB)
                    link(dve.tensor_tensor(dif, seg_lane[:, :, 1:P + 2], seg_lane[:, :, 0:P + 1], ALU.not_equal))
                    link(dve.tensor_scalar(border[:, :], differs[:, 0:NB * (P + 1)], -BIG, None, ALU.mult))
                    dve.wait_ge(multiplied.sem, multiplied.at(2))
                    across = [P, NB, BT]
                    link(dve.tensor_tensor(tb[:, :, 0:16], last_of, firsts.unsqueeze(2).to_broadcast(across),
                                           ALU.not_equal))
                    link(dve.tensor_tensor(tb[:, :, 0:16], tb[:, :, 0:16], late.unsqueeze(1).to_broadcast(across),
                                           ALU.max))
                    link(dve.tensor_tensor(tb[:, :, 17:33], first_of, lasts.unsqueeze(2).to_broadcast(across),
                                           ALU.not_equal))
                    link(dve.tensor_tensor(tb[:, :, 17:33], tb[:, :, 17:33], early.unsqueeze(1).to_broadcast(across),
                                           ALU.max))
                    link(dve.memset(tb[:, 0:1, 16:17], 1.0))
                    link(dve.tensor_tensor(tb[:, 1:NB, 16], last_of[:, 0:NB - 1, BT - 1], firsts[:, 1:NB],
                                           ALU.not_equal))
                    link(dve.tensor_scalar(tile_border[:, :], tile_border[:, :], -BIG, None, ALU.mult))
                    loc, same = differs[:, 0:NB], differs[:, 32:32 + NB]
                    link(dve.tensor_scalar(loc, block_f[:, 0:(NB - 1) * BG + 1:BG], -float(P), None, ALU.mult))
                    link(dve.tensor_tensor(loc, first_of[:, :, 0], loc, ALU.add))
                    link(dve.tensor_scalar(loc, loc, small[:, 0:1], None, ALU.is_equal))
                    link(dve.tensor_copy(differs[:, 64:64 + NB], last_of[:, :, BT - 1]))
                    link(dve.memset(same, 0.0))
                    link(dve.tensor_tensor(same[:, 1:NB], first_of[:, 1:NB, 0], differs[:, 64:64 + NB - 1],
                                           ALU.is_equal))
                    link(dve.tensor_tensor(straddle[:, :], loc, same, ALU.mult))
                    marks["step"] = n
            loaded.base += 160
            multiplied.base += 2
            step.base += marks["step"]

        rows_sb = arena[:, 0:QTAB].rearrange("p (a t c) -> p a t c", a=2, t=BT)
        TAIL = QTAB + NT * D
        weighted = arena[:, TAIL:TAIL + 4 * 272].rearrange("p (a t c) -> p a t c", a=2, t=GT)
        seg_a, seg_b, shifted, powers, final_max, logits = [arena[:, TAIL + 1088 + P * i:TAIL + 1088 + P * i + P]
                                                    for i in range(6)]
        onehots = sb("onehots", [P, 2, BT, P])
        spreads = sb("spreads", [P, 2, GT * P])
        raw = sb("raw", [P, 2, BT * H])
        bars = sb("bars", [P, P + 1])
        seg_max = sb("seg_max", [P, 2, P])
        spread_cols = sb("spread_cols", [P, 33])
        carried = sb("carried", [P, 33])
        carry = sb("carry", [P, 4])
        head_rhs = sb("head_rhs", [P, H])
        rescale = sb("rescale", [P, 2 * H])
        att = sb("att", [P, 2 * D])
        idx = sb("idx", [P, 2, BT], I32)

        names = ("oh_made", "oh_turned", "spread_made", "target_spread", "activated", "leaked", "multiplied_rows", "raw_made",
                 "logits_made", "logits_turned", "mid", "cols_made", "cols_spread", "shifted_made", "powers_made",
                 "powers_turned", "powers_kept", "scale_rhs", "scale_spread", "scale_in", "scale_made", "weighted_made",
                 "denominator_made", "summed", "added_up", "idx_made", "distance")
        S = {n: sig(n) for n in names}
        arrived = [[sig(f"arrived{a}{k}") for k in range(BG)] for a in range(2)]

        def edge_pass(kind, table, width):
            gin, gatv2, gat, hgt = (kind == k for k in ("gin", "gatv2", "gat", "hgt"))
            cw = {"gatv2": width, "gat": H, "hgt": D, "gin": 0}[kind]
            C = width // H if gatv2 else D // H
            v0 = D if hgt else 0
            wc = D if gin else H * (C + (2 if gat else 1))
            loc = slot_loc
            index = slot_typed if hgt else slot_src
            pot = [PS[0][:, 0:GT * P], PS[1][:, 0:GT * P]]
            z = [PS[2][:, :].rearrange("p (t c) -> p t c", t=GT), PS[3][:, :].rearrange("p (t c) -> p t c", t=GT)]
            sums = [PS[4][:, 0:wc], PS[5][:, 0:wc]]
            plt, pcols, pscale = PS[6][:, 0:P], PS[6][:, P:P + 33], PS[6][:, 192:192 + H]
            pat = PS[7][:, 0:P].rearrange("p (h t) -> p h t", h=H)
            powers_sb = stats[:, 0:P].rearrange("p (h t) -> p h t", h=H)
            max_sb = stats[:, P:2 * P].rearrange("p (h t) -> p h t", h=H)
            SLOTS_V = BG + 6

            oh_dve = gatv2 or gin
            w_dve = gat or hgt

            def one_hots(dve, s, a, k, g):
                wait(dve, S["summed"], g - 2 * BG + 1)
                for t in (GT * k, GT * k + 1):
                    op = dve.tensor_scalar(onehots[:, a, t, :], iota_row[:, :], loc[:, ds(BT * s + t, 1)], None,
                                           ALU.is_equal)
                op.then_inc(S["oh_made"].sem, 1)

            def one_hots_act(act, s, a, k, g):
                wait(act, S["summed"], g - 2 * BG + 1)
                for t in (GT * k, GT * k + 1):
                    act.activation(onehots[:, a, t, :], iota_row[:, :], ACT.Abs, scale=-1.0,
                                   bias=loc[:, ds(BT * s + t, 1)]).then_inc(S["distance"].sem, 1)
                wait(act, S["distance"], 2 * g + 2)
                act.activation(onehots[:, a, GT * k:GT * k + GT, :], onehots[:, a, GT * k:GT * k + GT, :], ACT.Relu,
                               scale=-1.0, bias=1.0).then_inc(S["oh_made"].sem, 1)

            def lane_split(ap, c):
                return ap.rearrange("p t (h c) -> p t h c", c=c)

            def blocks_of_batch(engine, s):
                return nc.values_load_multi_w_load_instructions(
                    block_of[0:1, ds(BG * s, BG)], engines=[engine], min_val=0, max_val=NT - 1)[1]

            with nc.Block() as block:
                def steps(eng, step_fn):
                    step_fn(0, 0, 0, True, False)
                    step_fn(1, 1, 0, True, True)
                    with eng.Fori(1, (NB - 1) // 2) as i:
                        step_fn(2 * i, 0, i, True, True)
                        step_fn(2 * i + 1, 1, i, True, True)
                    step_fn(NB - 1, 0, (NB - 1) // 2, True, True)
                    step_fn(NB, 1, (NB - 1) // 2, False, True)

                @block.gpsimd
                def _(pool):
                    freed = S["summed"] if gin else S["weighted_made"]

                    def step_fn(s, a, use, A_, B_):
                        if not A_:
                            return
                        for k in range(BG):
                            own_wait(pool, arrived[a][k], 32 * use)
                        pool.tensor_copy(idx[:, a, :], index[:, ds(BT * s, BT)]).then_inc(S["idx_made"].sem, 1)
                        own_wait(pool, S["idx_made"], s + 1)
                        for k in range(BG):
                            own_wait(pool, freed, BG * (s - 2) + k + 1)
                            if not gin:
                                own_wait(pool, S["raw_made"], BG * (s - 2) + k + 1)
                            for t in (GT * k, GT * k + 1):
                                pool.indirect_dma_start(
                                    out=rows_sb[:, a, t, 0:width], out_offset=None, in_=table[:, :],
                                    in_offset=bass.IndirectOffsetOnAxis(ap=idx[:, a, t:t + 1], axis=0),
                                    bounds_check=table.shape[0] - 1, oob_is_err=False)\
                                    .then_inc(arrived[a][k].sem, 16)

                    steps(pool, step_fn)

                @block.tensor
                def _(pe):
                    def step_fn(s, a, use, A_, B_):
                        g0 = BG * s
                        if A_ and not gin:
                            block_no = blocks_of_batch(mybir.EngineType.PE, s)
                        for v in range(SLOTS_V):
                            if B_ and v == 0 and not gin:
                                wait(pe, S["logits_made"], s)
                                wait(pe, S["scale_in"], s - 1)
                                pe.transpose(plt, logits[:, :], ident[:, :]).then_inc(S["logits_turned"].sem, 1)
                            if A_ and not gin and v < BG:
                                k, g = v, g0 + v
                                wait(pe, S["oh_made"], g + 1)
                                wait(pe, S["spread_made"], g - 1)
                                pe.transpose(pot[k % 2][:, 0:P], onehots[:, a, GT * k, :], ident[:, :])
                                pe.transpose(pot[k % 2][:, P:2 * P], onehots[:, a, GT * k + 1, :], ident[:, :])\
                                  .then_inc(S["oh_turned"].sem, 1)
                            if A_ and not gin and 1 <= v < BG + 1:
                                k, g = v - 1, g0 + v - 1
                                j = block_no[k]
                                wait(pe, S["spread_made"], g + 1)
                                wait(pe, S["raw_made"], g - 1)
                                if gatv2:
                                    wait(pe, arrived[a][k], 32 * (use + 1))
                                for t in range(GT):
                                    mm = pe.matmul(z[k % 2][:, t, 0:cw], spreads[:, k % 2, t * P:t * P + P],
                                                   qtab[:, j, 0:cw], start=True, stop=not gatv2)
                                    if gatv2:
                                        mm = pe.matmul(z[k % 2][:, t, 0:cw], ident[:, :],
                                                       rows_sb[:, a, GT * k + t, 0:cw], start=False, stop=True)
                                mm.then_inc(S["target_spread"].sem, 1)
                            if B_ and v == 2 and not gin:
                                wait(pe, S["cols_made"], s)
                                pe.matmul(pcols, same_head[:, :], spread_cols[:, :], start=True, stop=True)\
                                  .then_inc(S["cols_spread"].sem, 1)
                            if B_ and v == 4 and not gin:
                                wait(pe, S["scale_rhs"], s)
                                pe.matmul(pscale, ones[:, :], head_rhs[:, :], start=True, stop=True)\
                                  .then_inc(S["scale_spread"].sem, 1)
                                wait(pe, S["powers_made"], s)
                                wait(pe, S["weighted_made"], BG * (s - 1))
                                if gat:
                                    pe.transpose(PS[7][:, P:2 * P], final_max[:, :], ident[:, :])
                                pe.transpose(PS[7][:, 0:P], powers[:, :], ident[:, :])\
                                  .then_inc(S["powers_turned"].sem, 1)
                            if B_ and 6 <= v < BG + 6:
                                k, g = v - 6, g0 - BG + v - 6
                                if gin:
                                    wait(pe, S["oh_made"], g + 1)
                                    wait(pe, arrived[1 - a][k], 32 * (use + (1 if a else 0)))
                                else:
                                    wait(pe, S["weighted_made"], g + 1)
                                    wait(pe, S["denominator_made"], g + 1)
                                wait(pe, S["added_up"], g - 1)
                                for t in range(GT):
                                    rhs = rows_sb[:, 1 - a, GT * k + t, 0:wc] if gin else weighted[:, k % 2, t, 0:wc]
                                    mm = pe.matmul(sums[k % 2], onehots[:, 1 - a, GT * k + t, :], rhs,
                                                   start=t == 0, stop=t == GT - 1)
                                mm.then_inc(S["summed"].sem, 1)

                    steps(pe, step_fn)

                @block.scalar
                def _(act):
                    def step_fn(s, a, use, A_, B_):
                        g0 = BG * s
                        for v in range(SLOTS_V):
                            if A_ and not oh_dve:
                                for k in ((0, 1) if v == 0 else (v + 1,) if v + 1 < BG else ()):
                                    one_hots_act(act, s, a, k, g0 + k)
                            if A_ and v < BG:
                                k, g = v, g0 + v
                                wait(act, S["oh_turned"], g + 1)
                                wait(act, S["target_spread"], g - 1)
                                act.activation(spreads[:, k % 2, :], pot[k % 2], ACT.Copy)\
                                   .then_inc(S["spread_made"].sem, 1)
                            if A_ and gatv2 and 1 <= v < BG + 1:
                                k, g = v - 1, g0 + v - 1
                                wait(act, S["target_spread"], g + 1)
                                act.activation(rows_sb[:, a, GT * k:GT * k + GT, D:D + cw], z[k % 2][:, :, 0:cw],
                                               ACT.Copy, scale=0.2)\
                                   .then_inc(S["activated"].sem, 1)
                            if B_ and v == 3:
                                wait(act, S["shifted_made"], s)
                                wait(act, S["powers_turned"], s - 1)
                                act.activation(powers[:, :], shifted[:, :], ACT.Exp).then_inc(S["powers_made"].sem, 1)
                            if B_ and v == 5:
                                wait(act, S["scale_in"], s)
                                act.activation(rescale[:, H:2 * H], rescale[:, 0:H], ACT.Exp)\
                                   .then_inc(S["scale_made"].sem, 1)
                                wait(act, S["powers_turned"], s)
                                wait(act, S["denominator_made"], BG * (s - 1))
                                act.activation(stats[:, 0:(2 if gat else 1) * P], PS[7][:, 0:(2 if gat else 1) * P],
                                               ACT.Copy).then_inc(S["powers_kept"].sem, 1)
                            if B_ and 5 <= v < BG + 5:
                                k, g = v - 5, g0 - BG + v - 5
                                wait(act, S["powers_kept"], s)
                                wait(act, S["summed"], g - 1)
                                w = lane_split(weighted[:, k % 2, :, 0:wc], wc // H)
                                if gat:
                                    act.activation(w[:, :, :, C + 1],
                                                   max_sb[:, :, GT * k:GT * k + GT].rearrange("p h t -> p t h"),
                                                   ACT.Copy).then_inc(kept.sem, 1)
                                if gatv2:
                                    wait(act, arrived[1 - a][k], 32 * (use + (1 if a else 0)))
                                    for t in range(GT):
                                        for h in range(2):
                                            lanes = slice(h * H // 2, (h + 1) * H // 2)
                                            op = act.activation(
                                                w[:, t, lanes, 0:C],
                                                rows_sb[:, 1 - a, GT * k + t, h * cw // 2:(h + 1) * cw // 2]
                                                .rearrange("p (r c) -> p r c", r=H // 2),
                                                ACT.Copy, scale=powers_sb[:, h * H // 2, GT * k + t:GT * k + t + 1])
                                    op.then_inc(S["weighted_made"].sem, 1)
                                act.activation(w[:, :, :, C],
                                               powers_sb[:, :, GT * k:GT * k + GT].rearrange("p h t -> p t h"),
                                               ACT.Copy).then_inc(S["denominator_made"].sem, 1)

                    if not gin:
                        steps(act, step_fn)

                @block.vector
                def _(dve):
                    dve.memset(acc[:, :, :], 0.0).then_inc(step.sem, 1)
                    dve.memset(seg_max[:, :, :], 0.0).then_inc(step.sem, 1)
                    dve.wait_ge(step.sem, step.at(2))

                    def step_fn(s, a, use, A_, B_):
                        g0, b = BG * s, 1 - a
                        m = 0

                        def link(op):
                            nonlocal m
                            m += 1
                            op.then_inc(S["mid"].sem, 1)
                            dve.wait_ge(S["mid"].sem, S["mid"].at(MID * (s - 1) + m))

                        for v in range(SLOTS_V):
                            if A_ and v < BG and oh_dve:
                                one_hots(dve, s, a, v, g0 + v)
                            if A_ and not gin and 2 <= v < BG + 2:
                                k, g = v - 2, g0 + v - 2
                                pr = z[k % 2][:, :, 0:cw]
                                if gatv2:
                                    wait(dve, S["activated"], g + 1)
                                    dve.tensor_tensor(pr, pr, rows_sb[:, a, GT * k:GT * k + GT, D:D + cw], ALU.max)\
                                       .then_inc(S["leaked"].sem, 1)
                                else:
                                    wait(dve, S["target_spread"], g + 1)
                                    wait(dve, arrived[a][k], 32 * (use + 1))
                                if hgt:
                                    dve.tensor_tensor(pr, pr, rows_sb[:, a, GT * k:GT * k + GT, 0:D], ALU.mult)\
                                       .then_inc(S["multiplied_rows"].sem, 1)
                            if B_ and v == 1 and not gin:
                                link(dve.tensor_copy(bars[:, :], border[:, ds((P + 1) * (s - 1), P + 1)]))
                                wait(dve, S["logits_turned"], s)
                                link(dve.tensor_tensor_scan(seg_a[:, :], bars[:, 0:P], plt, -BIG, ALU.add, ALU.max))
                                link(dve.tensor_tensor_scan(seg_b[:, ::-1], bars[:, P:0:-1], seg_a[:, ::-1], -BIG,
                                                            ALU.add, ALU.max))
                                link(dve.tensor_scalar(spread_cols[:, 0:16], lane_mask[:, :], seg_b[:, P - 1:P], None,
                                                       ALU.mult))
                                link(dve.tensor_scalar(spread_cols[:, 16:17], lane_mask[:, 15:16],
                                                       seg_max[:, a, P - 1:P], None, ALU.mult))
                                link(dve.tensor_scalar(spread_cols[:, 17:33], lane_mask[:, :], seg_b[:, 0:1], None,
                                                       ALU.mult))
                                dve.sem_inc(S["cols_made"].sem, 1)
                            if B_ and v == 3 and not gin:
                                wait(dve, S["cols_spread"], s)
                                link(dve.tensor_tensor(carried[:, :], pcols, tile_border[:, ds(33 * (s - 1), 33)],
                                                       ALU.add))
                                link(dve.tensor_reduce(carry[:, 0:1], carried[:, 0:17], AX, ALU.max))
                                link(dve.tensor_reduce(carry[:, 1:2], carried[:, 17:33], AX, ALU.max))
                                link(dve.tensor_tensor_scan(seg_a[:, :], bars[:, 0:P], seg_b[:, :], carry[:, 0:1],
                                                            ALU.add, ALU.max))
                                link(dve.tensor_tensor_scan(seg_max[:, b, ::-1], bars[:, P:0:-1], seg_a[:, ::-1],
                                                            carry[:, 1:2], ALU.add, ALU.max))
                                wait(dve, S["powers_made"], s - 1)
                                link(dve.tensor_tensor(shifted[:, :], plt, seg_max[:, b, :], ALU.subtract))
                                if gat:
                                    wait(dve, S["powers_turned"], s - 1)
                                    link(dve.scalar_tensor_tensor(final_max[:, :], bars[:, 1:P + 1], -1.0 / BIG,
                                                                  seg_max[:, b, :], ALU.mult, ALU.mult))
                                dve.sem_inc(S["shifted_made"].sem, 1)
                                link(dve.tensor_scalar(carry[:, 2:3], seg_max[:, b, 0:1], lane_mask[:, 0:1], None,
                                                       ALU.mult))
                                link(dve.scalar_tensor_tensor(carry[:, 3:4], seg_max[:, a, P - 1:P],
                                                              lane_mask[:, 15:16], carry[:, 2:3], ALU.mult,
                                                              ALU.subtract))
                                link(dve.tensor_scalar(head_rhs[:, :], head_col[:, :], carry[:, 3:4], None, ALU.mult))
                                dve.sem_inc(S["scale_rhs"].sem, 1)
                            if B_ and v == 5 and not gin:
                                wait(dve, S["scale_spread"], s)
                                dve.tensor_scalar(rescale[:, 0:H], pscale, straddle[:, ds(s - 1, 1)], None, ALU.mult)\
                                   .then_inc(S["scale_in"].sem, 1)
                            if B_ and w_dve and 5 <= v < BG + 5:
                                k, g = v - 5, g0 - BG + v - 5
                                wait(dve, S["powers_kept"], s)
                                wait(dve, S["summed"], g - 1)
                                w = lane_split(weighted[:, k % 2, :, 0:wc], wc // H)
                                src = rows_sb[:, b, GT * k:GT * k + GT, v0:v0 + H * C]
                                p = pat[:, :, GT * k:GT * k + GT].rearrange("p h t -> p t h")
                                dve.tensor_tensor(w[:, :, :, 0:C], lane_split(src, C),
                                                  p.unsqueeze(3).to_broadcast([P, GT, H, C]), ALU.mult)\
                                   .then_inc(S["weighted_made"].sem, 1)
                            if A_ and not gin and 2 <= v < BG + 2:
                                k, g = v - 2, g0 + v - 2
                                r = raw[:, a, 0:BT * (2 if gatv2 else H)].rearrange("p (t h) -> p t h", t=BT)
                                r = r[:, GT * k:GT * k + GT, :]
                                if gatv2:
                                    wait(dve, S["leaked"], g + 1)
                                    for t in range(GT):
                                        for h in range(2):
                                            ch = slice(cw // 2 * h, cw // 2 * h + cw // 2)
                                            op = dve.tensor_tensor_reduce(
                                                out=z[k % 2][:, t, ch], in0=z[k % 2][:, t, ch], in1=att[:, ch],
                                                scale=1.0, scalar=0.0, op0=ALU.mult, op1=ALU.add,
                                                accum_out=r[:, t, h:h + 1])
                                elif gat:
                                    op = dve.tensor_tensor(r, z[k % 2][:, :, 0:cw],
                                                           rows_sb[:, a, GT * k:GT * k + GT, D:D + H], ALU.add)
                                else:
                                    wait(dve, S["multiplied_rows"], g + 1)
                                    op = dve.tensor_reduce(r, lane_split(z[k % 2][:, :, 0:cw], C), AX, ALU.add)
                                op.then_inc(S["raw_made"].sem, 1)
                            if B_ and v == 6:
                                block_no = blocks_of_batch(mybir.EngineType.DVE, s - 1)
                            if B_ and 6 <= v < BG + 6:
                                k, g = v - 6, g0 - BG + v - 6
                                j = block_no[k]
                                wait(dve, S["added_up"], g)
                                if k == 0 and not gin:
                                    wait(dve, S["scale_made"], s)
                                    link(dve.tensor_tensor(
                                        acc[:, j, 0:wc].rearrange("p (h c) -> p h c", h=H),
                                        acc[:, j, 0:wc].rearrange("p (h c) -> p h c", h=H),
                                        rescale[:, H:2 * H].unsqueeze(2).to_broadcast([P, H, wc // H]), ALU.mult))
                                wait(dve, S["summed"], g + 1)
                                dve.tensor_tensor(acc[:, j, 0:wc], acc[:, j, 0:wc], sums[k % 2], ALU.add)\
                                   .then_inc(S["added_up"].sem, 1)
                        if A_ and not gin:
                            wait(dve, S["raw_made"], g0 + BG)
                            wait(dve, S["logits_turned"], s)
                            out_l = logits[:, :].rearrange("p (h t) -> p h t", h=H)
                            if gatv2:
                                r = raw[:, a, 0:2 * BT].rearrange("p (t h) -> p h t", t=BT)
                                op = dve.tensor_copy(logits[:, :].rearrange("p (h r t) -> p h r t", h=2, r=H // 2),
                                                     r.unsqueeze(2).to_broadcast([P, 2, H // 2, BT]))
                            else:
                                r = raw[:, a, :].rearrange("p (t h) -> p h t", t=BT)
                                if gat:
                                    op = dve.scalar_tensor_tensor(out_l, r, 0.2, r, ALU.mult, ALU.max)
                                else:
                                    op = dve.tensor_tensor(out_l, r, slot_bar[:, ds(BT * s, BT)].unsqueeze(1)
                                                           .to_broadcast([P, H, BT]), ALU.add)
                            op.then_inc(S["logits_made"].sem, 1)

                    MID = 0 if gin else 17 if gat else 16
                    steps(dve, step_fn)
                    step.base += 2
            G = NB * BG
            per_group = ("oh_made", "summed", "added_up")
            if not gin:
                per_group += ("oh_turned", "spread_made", "target_spread", "raw_made", "weighted_made",
                              "denominator_made")
                for n in ("logits_made", "logits_turned", "cols_made", "cols_spread", "shifted_made", "powers_made",
                          "powers_turned", "powers_kept", "scale_rhs", "scale_spread", "scale_in", "scale_made"):
                    S[n].base += NB
                S["mid"].base += NB * (17 if gat else 16)
            if gatv2:
                per_group += ("activated", "leaked")
            if hgt:
                per_group += ("multiplied_rows",)
            if gat or hgt:
                S["distance"].base += 2 * G
            for n in per_group:
                S[n].base += G
            S["idx_made"].base += NB
            if gat:
                kept.base += G
            for a in range(2):
                for k in range(BG):
                    arrived[a][k].base += 32 * ((NB + 1 - a) // 2)

        hbuf = arena[:, 4096:4096 + NT * D].rearrange("p (j c) -> p j c", j=NT)
        stage = arena[:, 10496:10496 + 2 * 3 * 512].rearrange("p (a c) -> p a c", a=2)
        xin = arena[:, 13568:13568 + 2 * D].rearrange("p (a c) -> p a c", a=2)
        tmp = arena[:, 14080:14080 + 2 * D].rearrange("p (a c) -> p a c", a=2)
        vecs = sb("vecs", [P, 4 * D])
        cols = sb("cols", [P, 32])
        stats = sb("stats", [P, 256])
        ln = sb("ln", [P, 6 * NT])
        flat = "p j c -> p (j c)"

        D_ = {n: sig("d_" + n) for n in ("in", "turned", "turned_sb", "product", "act_out", "dve_out", "tmp",
                                         "hidden", "hidden_sb", "keys", "keys_sb", "typed", "values")}
        stored = [sig("stored0"), sig("stored1")]
        straight = sig("straight")

        def sweep(eng, *stages):
            def one(s, a):
                for k, f in enumerate(stages):
                    if f is not None and not (isinstance(s, int) and not 0 <= s - k < NT):
                        f(s - k, (a - k) % 2)

            for s in range(6):
                one(s, s % 2)
            with eng.Fori(3, NT // 2) as i:
                one(2 * i, 0)
                one(2 * i + 1, 1)
            for s in range(NT - 1, NT - 1 + len(stages)):
                one(s, s % 2)

        def load(*pairs, store=False):
            with nc.Block() as block:
                @block.sync
                def _(sp):
                    with nc.allow_non_contiguous_dma(reason="small weights, once"):
                        for dst, src in pairs:
                            sp.dma_start(dst, src).then_inc(loaded.sem, 16)
                    sp.wait_ge(loaded.sem, loaded.at(16 * len(pairs)))
            loaded.base += 16 * len(pairs)

        def vector_phase(f):
            with nc.Block() as block:
                @block.vector
                def _(dve):
                    n = 0

                    def link(op):
                        nonlocal n
                        n += 1
                        op.then_inc(step.sem, 1)
                        dve.wait_ge(step.sem, step.at(n))

                    f(dve, link)
                    marks["step"] = n
            step.base += marks["step"]

        def scalar_phase(*calls):
            with nc.Block() as block:
                @block.scalar
                def _(act):
                    for out_, in_, func in calls:
                        act.activation(out_, in_, func).then_inc(straight.sem, 1)
            straight.base += len(calls)

        def row(ap):
            return bass.AP(tensor=ap.tensor, offset=ap.offset, ap=[[0, P], [1, ap.shape[-1]]])

        def over_blocks(v):
            return v.unsqueeze(1).to_broadcast([P, NT, D])

        def layer_norm(gain=None, bias=None):
            st = stats[:, 0:6 * NT].rearrange("p (j f) -> p j f", f=6)
            mean, var, rs, nm, t1, t2 = [ln[:, i * NT:(i + 1) * NT] for i in range(6)]

            def first(dve, link):
                with dve.Fori(0, NT) as j:
                    dve.bn_stats(out=st[:, j, :], in_=X[:, j, :]).then_inc(kept.sem, 1)
                dve.wait_ge(kept.sem, kept.at(NT))
                kept.base += NT
                link(dve.tensor_tensor(t1, st[:, :, 1], st[:, :, 4], ALU.add))
                link(dve.tensor_scalar(mean, t1, 0.5, None, ALU.mult))
                link(dve.tensor_tensor(t1, st[:, :, 1], st[:, :, 4], ALU.subtract))
                link(dve.tensor_scalar(t1, t1, 0.5, None, ALU.mult))
                link(dve.tensor_tensor(t1, t1, t1, ALU.mult))
                link(dve.tensor_tensor(t2, st[:, :, 2], st[:, :, 5], ALU.add))
                link(dve.tensor_scalar(t2, t2, 1.0 / D, 1e-5, ALU.mult, ALU.add))
                link(dve.tensor_tensor(var, t1, t2, ALU.add))

            def second(dve, link):
                link(dve.reciprocal(rs, t1))
                link(dve.scalar_tensor_tensor(nm, mean, -1.0, rs, ALU.mult, ALU.mult))
                with dve.Fori(0, NT) as j:
                    dve.tensor_scalar(X[:, j, :], X[:, j, :], ln[:, ds(2 * NT + j, 1)], ln[:, ds(3 * NT + j, 1)],
                                      ALU.mult, ALU.add).then_inc(kept.sem, 1)
                dve.wait_ge(kept.sem, kept.at(NT))
                kept.base += NT
                if gain is not None:
                    link(dve.tensor_tensor(X[:, :, :], X[:, :, :], over_blocks(gain), ALU.mult))
                    link(dve.tensor_tensor(X[:, :, :], X[:, :, :], over_blocks(bias), ALU.add))

            vector_phase(first)
            scalar_phase((t1, var, ACT.Sqrt))
            vector_phase(second)

        def project(src, kb, rhs, n, act_out=None, dve_out=None, dve_ops=1, table=None, width=0):
            turned = [PS[0][:, 0:kb * P], PS[1][:, 0:kb * P]]
            xT = spreads
            prod = [PS[2][:, 0:n], PS[3][:, 0:n]]
            with nc.Block() as block:
                @block.vector
                def _(dve):
                    def take(j, a):
                        wait(dve, D_["turned"], j - 1)
                        dve.tensor_copy(xin[:, a, 0:kb * P], src(j)).then_inc(D_["in"].sem, 1)

                    def give(j, a):
                        wait(dve, D_["product"], j + 1)
                        if act_out:
                            wait(dve, D_["act_out"], j + 1)
                        if table is not None:
                            wait_stored(dve, j, a)
                        dve_out(dve, j, a, prod[a])

                    sweep(dve, take, give if dve_out else None)

                @block.tensor
                def _(pe):
                    def turn(j, a):
                        wait(pe, D_["in"], j + 1)
                        wait(pe, D_["turned_sb"], j - 1)
                        for k in range(kb):
                            op = pe.transpose(turned[a][:, k * P:k * P + P], xin[:, a, k * P:k * P + P], ident[:, :])
                        op.then_inc(D_["turned"].sem, 1)

                    def multiply(j, a):
                        wait(pe, D_["turned_sb"], j + 1)
                        if act_out:
                            wait(pe, D_["act_out"], j - 1)
                        if dve_out:
                            wait(pe, D_["dve_out"], dve_ops * (j - 1))
                        for k in range(kb):
                            op = pe.matmul(prod[a], xT[:, a, k * P:k * P + P], rhs[:, k, 0:n], start=k == 0,
                                           stop=k == kb - 1)
                        op.then_inc(D_["product"].sem, 1)

                    sweep(pe, turn, multiply)

                @block.scalar
                def _(act):
                    def turn(j, a):
                        wait(act, D_["turned"], j + 1)
                        wait(act, D_["product"], j - 1)
                        act.activation(xT[:, a, 0:kb * P], turned[a], ACT.Copy).then_inc(D_["turned_sb"].sem, 1)

                    def give(j, a):
                        wait(act, D_["product"], j + 1)
                        if table is not None:
                            wait_stored(act, j, a)
                        act_out(act, j, a, prod[a]).then_inc(D_["act_out"].sem, 1)

                    sweep(act, turn, give if act_out else None)

                if table is not None:
                    @block.sync
                    def _(sp):
                        def store(j, a):
                            if act_out:
                                own_wait(sp, D_["act_out"], j + 1)
                            if dve_out:
                                own_wait(sp, D_["dve_out"], dve_ops * (j + 1))
                            sp.dma_start(table[ds(P * j, P), :], stage[:, a, 0:width]).then_inc(stored[a].sem, 16)

                        sweep(sp, store)
                        for a in range(2):
                            own_wait(sp, stored[a], 16 * ((NT + 1 - a) // 2))
            for n_ in ("in", "turned", "turned_sb", "product"):
                D_[n_].base += NT
            if act_out:
                D_["act_out"].base += NT
            if dve_out:
                D_["dve_out"].base += NT * dve_ops
            if table is not None:
                for a in range(2):
                    stored[a].base += 16 * ((NT + 1 - a) // 2)

        def wait_stored(eng, j, a):
            wait(eng, stored[a], 8 * (j - a))

        def normalised(lanes, C, denominator):
            def f(dve, link):
                av = acc[:, :, 0:H * lanes].rearrange("p j (h c) -> p j h c", h=H)
                inv = stats[:, 0:NT * H].rearrange("p (j h) -> p j h", j=NT)
                denominator(dve, link, av, inv)
                hv = hbuf[:, :, 0:H * C].rearrange("p j (h c) -> p j h c", h=H)
                for h in range(H):
                    op = dve.tensor_tensor(hv[:, :, h, :], av[:, :, h, 0:C],
                                           inv[:, :, h:h + 1].to_broadcast([P, NT, C]), ALU.mult)
                    link(op)
            return f

        def layer_0():
            w = arena[:, 0:4096].rearrange("p (k n) -> p k n", k=2)
            load(*[(w[:, k, 0:128], A["L0_gnn_Wl0"][k * P:k * P + P, :]) for k in range(2)],
                 *[(w[:, k, 128:256], A["L0_gnn_Wr0"][k * P:k * P + P, :]) for k in range(2)],
                 (w[:, 0, 256:512], A["L0_gnn_Wl1"][:, :]), (w[:, 0, 512:768], A["L0_gnn_Wr1"][:, :]),
                 (att[:, 0:128], row(A["L0_gnn_att0"].rearrange("h c -> (h c)"))),
                 (att[:, 256:512], row(A["L0_gnn_att1"].rearrange("h c -> (h c)"))),
                 (vecs[:, 0:128], row(A["L0_gnn_b0"])), (vecs[:, 256:512], row(A["L0_gnn_b1"])))
            project(lambda j: X[:, j, :], 2, w[:, :, 0:256], 256,
                    act_out=lambda act, j, a, ps: act.activation(stage[:, a, 0:128], ps[:, 0:128], ACT.Copy),
                    dve_out=lambda dve, j, a, ps: dve.tensor_copy(qtab[:, j, 0:128], ps[:, 128:256])
                    .then_inc(D_["dve_out"].sem, 1), table=tab_l0a, width=128)
            edge_pass("gatv2", tab_l0a, 128)

            def denominator(C):
                def f(dve, link, av, inv):
                    link(dve.tensor_scalar(inv, av[:, :, :, C], 1e-30, None, ALU.max))
                    link(dve.reciprocal(inv, inv))
                return f

            def relu(dve, link):
                normalised(17, 16, denominator(16))(dve, link)
                hv = hbuf[:, :, 0:128]
                link(dve.tensor_tensor(hv, hv, vecs[:, 0:128].unsqueeze(1).to_broadcast([P, NT, 128]), ALU.add))
                link(dve.tensor_scalar(hv, hv, 0.0, None, ALU.max))
                link(dve.tensor_copy(att[:, 0:256], att[:, 256:512]))

            vector_phase(relu)
            load((w[:, 0, 256:512], A["L0_gnn_Wl1"][:, :]), (w[:, 0, 512:768], A["L0_gnn_Wr1"][:, :]))
            project(lambda j: hbuf[:, j, 0:128], 1, w[:, :, 256:768], 512,
                    act_out=lambda act, j, a, ps: act.activation(stage[:, a, 0:256], ps[:, 0:256], ACT.Copy),
                    dve_out=lambda dve, j, a, ps: dve.tensor_copy(qtab[:, j, :], ps[:, 256:512])
                    .then_inc(D_["dve_out"].sem, 1), table=tab_l0b, width=256)
            edge_pass("gatv2", tab_l0b, 256)

            def close(dve, link):
                normalised(33, 32, denominator(32))(dve, link)
                link(dve.tensor_tensor(hbuf[:, :, :], hbuf[:, :, :], over_blocks(vecs[:, 256:512]), ALU.add))
                link(dve.tensor_tensor(X[:, :, :], X[:, :, :], hbuf[:, :, :], ALU.add))

            vector_phase(close)
            layer_norm()

        def layer_1():
            w_in = arena[:, 0:512].rearrange("p (o n) -> p o n", o=2)
            w = arena[:, 512:1024].rearrange("p (k n) -> p k n", k=2)
            load(*[(w_in[:, o, :], A["L1_gnn_W"][o * P:o * P + P, :]) for o in range(2)],
                 (att[:, 0:256], row(A["L1_gnn_attn_l"].rearrange("a h c -> (a h c)"))),
                 (att[:, 256:512], row(A["L1_gnn_attn_r"].rearrange("a h c -> (a h c)"))))
            with nc.Block() as block:
                @block.tensor
                def _(pe):
                    for k in range(2):
                        for o in range(2):
                            pe.transpose(PS[0][:, k * D + o * P:k * D + o * P + P], w_in[:, o, k * P:k * P + P],
                                         ident[:, :]).then_inc(multiplied.sem, 1)

                @block.vector
                def _(dve):
                    dve.wait_ge(multiplied.sem, multiplied.at(4))
                    dve.tensor_copy(w, PS[0][:, :].rearrange("p (k n) -> p k n", k=2)).then_inc(step.sem, 1)
            multiplied.base += 4
            step.base += 1

            def logit_parts(dve, j, a, ps):
                for k, out_ in ((0, stage[:, a, D:D + H]), (1, qtab[:, j, 0:H])):
                    wait(dve, D_["dve_out"], 2 * j + k)
                    dve.tensor_tensor(tmp[:, 0, :], ps, att[:, k * D:k * D + D], ALU.mult).then_inc(D_["tmp"].sem, 1)
                    wait(dve, D_["tmp"], 2 * j + k + 1)
                    dve.tensor_reduce(out_, tmp[:, 0, :].rearrange("p (h c) -> p h c", h=H), AX, ALU.add)\
                       .then_inc(D_["dve_out"].sem, 1)

            project(lambda j: X[:, j, :], 2, w, 256,
                    act_out=lambda act, j, a, ps: act.activation(stage[:, a, 0:256], ps, ACT.Copy),
                    dve_out=logit_parts, dve_ops=2, table=tab_l1, width=D + H)
            D_["tmp"].base += 2 * NT
            edge_pass("gat", tab_l1, D + H)

            av = acc[:, :, 0:H * 34].rearrange("p j (h c) -> p j h c", h=H)
            top = tmp[:, 0, 0:NT * H].rearrange("p (j h) -> p j h", j=NT)
            factor = tmp[:, 1, 0:NT * H].rearrange("p (j h) -> p j h", j=NT)
            peak, peaks = small[:, 16:24], small[:, 24:32]

            def maxima(dve, link):
                link(dve.tensor_copy(top, av[:, :, :, 33]))
                link(dve.tensor_scalar(small[:, 8:9], small[:, 0:1], float(NLAST), -BIG, ALU.is_ge, ALU.mult))
                link(dve.tensor_scalar(top[:, NT - 1, :], top[:, NT - 1, :], small[:, 8:9], None, ALU.add))
                link(dve.tensor_reduce(peak, top.rearrange("p j h -> p h j"), AX, ALU.max))

            vector_phase(maxima)
            with nc.Block() as block:
                @block.gpsimd
                def _(pool):
                    pool.partition_all_reduce(peaks, peak, P, RMAX).then_inc(made.sem, 1)
            made.base += 1
            vector_phase(lambda dve, link: link(dve.tensor_tensor(
                top, top, peaks.unsqueeze(1).to_broadcast([P, NT, H]), ALU.subtract)))
            scalar_phase((factor, top, ACT.Exp))

            def denominator(dve, link, av, inv):
                link(dve.tensor_tensor(inv, av[:, :, :, 32], factor, ALU.mult))
                link(dve.tensor_scalar(inv, inv, 1e-6, None, ALU.max))
                link(dve.reciprocal(inv, inv))
                link(dve.tensor_tensor(inv, inv, factor, ALU.mult))

            def close(dve, link):
                normalised(34, 32, denominator)(dve, link)
                link(dve.tensor_tensor(X[:, :, :], X[:, :, :], hbuf[:, :, :], ALU.add))

            vector_phase(close)
            layer_norm()

        flat_oh = onehots[:, :, :, :].rearrange("p a t c -> p (a t c)")

        def typed_tables(l):
            w_qv = arena[:, 0:2048].rearrange("p (a k c n) -> p a k c n", a=4, k=2, c=2)
            w_k = arena[:, 2048:3072].rearrange("p (a k n) -> p a k n", a=4, k=2)
            w_e = arena[:, 3072:3840].rearrange("p (k a n) -> p k a n", k=2, a=3)
            mu = small[:, 32:56].rearrange("p (h t) -> p t h", t=3)
            masked_x = flat_oh[:, 0:2048].rearrange("p (a t c) -> p a t c", a=2, t=4)
            turned_x = flat_oh[:, 2048:4096].rearrange("p (a k t c) -> p a k t c", a=2, k=2, t=4)
            is_type = stats[:, 0:4 * NT].rearrange("p (t j) -> p t j", t=4)
            keysT = spreads

            def prepare(dve, link):
                link(dve.memset(arena[:, 0:3840], 0.0))
                for t in range(4):
                    link(dve.tensor_scalar(is_type[:, t, :], type_of[:, :], float(t), None, ALU.is_equal))

            vector_phase(prepare)
            pairs = []
            for hh in range(4):
                q = slice(32 * hh, 32 * hh + 32)
                for k in range(2):
                    h = 4 * k + hh
                    pairs += [(w_qv[q, :, k, 0, q], A["L2_gnn_W_Q"][l, :, h].rearrange("a d e -> d a e")),
                              (w_qv[q, :, k, 1, q], A["L2_gnn_W_V"][l, :, h].rearrange("a d e -> d a e")),
                              (w_k[q, :, k, q], A["L2_gnn_W_K"][l, :, h].rearrange("a d e -> d a e")),
                              (w_e[q, k, :, q], A["L2_gnn_W_E"][l, :, h].rearrange("a d e -> d a e"))]
            mu_ap = A["L2_gnn_mu"]
            pairs.append((small[:, 32:56], bass.AP(tensor=mu_ap.tensor, offset=l * H * 3, ap=[[0, P], [1, 3 * H]])))
            load(*pairs)
            vector_phase(lambda dve, link: link(dve.tensor_scalar(small[:, 32:56], small[:, 32:56],
                                                                  float(32.0 ** -0.5), None, ALU.mult)))
            qv = [PS[2][:, :].rearrange("p (k c n) -> p k c n", k=2, c=2),
                  PS[3][:, :].rearrange("p (k c n) -> p k c n", k=2, c=2)]
            kt = [PS[4][:, 0:D], PS[7][:, 0:D]]
            ke = [PS[5][:, 0:384].rearrange("p (t n) -> p t n", t=3), PS[6][:, 0:384].rearrange("p (t n) -> p t n", t=3)]

            with nc.Block() as block:
                @block.vector
                def _(dve):
                    def mask(j, a):
                        wait(dve, D_["turned"], j - 1)
                        for t in range(4):
                            op = dve.tensor_scalar(masked_x[:, a, t, :], X[:, j, :], is_type_at(t, j), None, ALU.mult)
                        op.then_inc(D_["in"].sem, 1)

                    def is_type_at(t, j):
                        return stats[:, ds(t * NT + j, 1)]

                    def queries(j, a):
                        wait(dve, D_["values"], 3 * (j + 1))
                        dve.tensor_copy(qtab[:, j, :].rearrange("p (k n) -> p k n", k=2), qv[a][:, :, 0, :])\
                           .then_inc(D_["dve_out"].sem, 1)

                    def keys(j, a):
                        wait(dve, D_["typed"], j + 1)
                        wait_stored(dve, j, a)
                        st = stage[:, a, :].rearrange("p (t c) -> p t c", t=3)
                        for k in range(2):
                            dve.tensor_tensor(
                                st[:, :, k * P:k * P + P].rearrange("p t (h e) -> p t h e", e=32),
                                ke[k].rearrange("p t (h e) -> p t h e", e=32),
                                mu[:, :, 4 * k:4 * k + 4].unsqueeze(3).to_broadcast([P, 3, 4, 32]), ALU.mult)\
                               .then_inc(D_["keys"].sem, 1)

                    sweep(dve, mask, None, queries, keys)

                @block.tensor
                def _(pe):
                    def turn(j, a):
                        wait(pe, D_["in"], j + 1)
                        wait(pe, D_["turned_sb"], 2 * j)
                        for k in range(2):
                            for t in range(4):
                                op = pe.transpose(PS[k][:, t * P:t * P + P], masked_x[:, a, t, k * P:k * P + P],
                                                  ident[:, :])
                        op.then_inc(D_["turned"].sem, 1)

                    def transform(j, a):
                        wait(pe, D_["turned_sb"], 2 * j + 2)
                        wait(pe, D_["dve_out"], j - 1)
                        wait(pe, D_["values"], 3 * (j - 1))
                        wait(pe, D_["keys_sb"], j - 1)
                        for k in range(2):
                            for t in range(4):
                                pe.matmul(kt[a][:, k * P:k * P + P], w_k[:, t, k, :], turned_x[:, a, k, t, :],
                                          start=t == 0, stop=t == 3).then_inc(kept.sem, 1)
                        for k in range(2):
                            for t in range(4):
                                op = pe.matmul(qv[a][:, k, :, :].rearrange("p c n -> p (c n)"),
                                               turned_x[:, a, k, t, :],
                                               w_qv[:, t, k, :, :].rearrange("p c n -> p (c n)"),
                                               start=t == 0, stop=t == 3)
                        op.then_inc(D_["product"].sem, 1)

                    def edge_types(j, a):
                        wait(pe, D_["keys_sb"], j + 1)
                        wait(pe, D_["keys"], 2 * j)
                        for k in range(2):
                            op = pe.matmul(ke[k].rearrange("p t n -> p (t n)"), keysT[:, a, k * P:k * P + P],
                                           w_e[:, k, :, :].rearrange("p t n -> p (t n)"), start=True, stop=True)
                        op.then_inc(D_["typed"].sem, 1)

                    sweep(pe, turn, transform, edge_types)

                @block.scalar
                def _(act):
                    def turn(j, a):
                        wait(act, D_["turned"], j + 1)
                        wait(act, D_["product"], j - 1)
                        for k in range(2):
                            act.activation(turned_x[:, a, k, :, :].rearrange("p t c -> p (t c)"), PS[k][:, :], ACT.Copy)\
                               .then_inc(D_["turned_sb"].sem, 1)

                    def keys(j, a):
                        wait(act, D_["product"], j + 1)
                        wait(act, D_["typed"], j - 1)
                        act.activation(keysT[:, a, :], kt[a], ACT.Copy).then_inc(D_["keys_sb"].sem, 1)
                        wait_stored(act, j, a)
                        st = stage[:, a, :].rearrange("p (t c) -> p t c", t=3)
                        for t in range(3):
                            act.activation(st[:, t, D:2 * D].rearrange("p (k n) -> p k n", k=2), qv[a][:, :, 1, :],
                                           ACT.Copy).then_inc(D_["values"].sem, 1)

                    sweep(act, turn, keys)

                @block.sync
                def _(sp):
                    def store(j, a):
                        own_wait(sp, D_["values"], 3 * (j + 1))
                        own_wait(sp, D_["keys"], 2 * (j + 1))
                        sp.dma_start(tab_l2[:, :].rearrange("(t n) c -> n t c", t=3)[ds(P * j, P), :, :],
                                     stage[:, a, :].rearrange("p (t c) -> p t c", t=3)).then_inc(stored[a].sem, 16)

                    sweep(sp, store)
                    for a in range(2):
                        own_wait(sp, stored[a], 16 * ((NT + 1 - a) // 2))
            for n_ in ("in", "turned", "product", "dve_out", "typed", "keys_sb"):
                D_[n_].base += NT
            D_["turned_sb"].base += 2 * NT
            D_["keys"].base += 2 * NT
            D_["values"].base += 3 * NT
            kept.base += 8 * NT
            for a in range(2):
                stored[a].base += 16 * ((NT + 1 - a) // 2)

        def perceptron(up, down, bias, func, scale=None, out_fn=None, hidden_of=None):
            hid = [stage_h[:, 0, :, :], stage_h[:, 1, :, :]]
            turned = [PS[0][:, 0:D], PS[7][:, 0:D]]
            hp = [[PS[1], PS[2]], [PS[3], PS[4]]]
            prod = [PS[5][:, 0:D], PS[6][:, 0:D]]
            with nc.Block() as block:
                @block.vector
                def _(dve):
                    def take(j, a):
                        wait(dve, D_["turned"], j - 1)
                        dve.tensor_copy(xin[:, a, :], X[:, j, :]).then_inc(D_["in"].sem, 1)

                    def give(j, a):
                        wait(dve, D_["product"], j + 1)
                        dve.tensor_tensor(X[:, j, :], X[:, j, :], prod[a], ALU.add).then_inc(D_["dve_out"].sem, 1)

                    sweep(dve, take, None, None, give)

                @block.tensor
                def _(pe):
                    def turn(j, a):
                        wait(pe, D_["in"], j + 1)
                        wait(pe, D_["turned_sb"], j - 1)
                        for k in range(2):
                            op = pe.transpose(turned[a][:, k * P:k * P + P], xin[:, a, k * P:k * P + P], ident[:, :])
                        op.then_inc(D_["turned"].sem, 1)

                    def ups(j, a):
                        wait(pe, D_["turned_sb"], j + 1)
                        wait(pe, D_["hidden_sb"], 8 * (j - 1))
                        for m in range(8):
                            for k in range(2):
                                op = pe.matmul(hp[a][m // 4][:, m % 4 * P:m % 4 * P + P], up[:, k, m * P:m * P + P],
                                               spreads[:, a, k * P:k * P + P], start=k == 0, stop=k == 1)
                            op.then_inc(D_["hidden"].sem, 1)

                    def downs(j, a):
                        wait(pe, D_["hidden_sb"], 8 * (j + 1))
                        wait(pe, D_["dve_out"], j - 1)
                        for m in range(8):
                            op = pe.matmul(prod[a], hid[a][:, m, :], down[:, m, :], start=m == 0, stop=m == 7)
                        op.then_inc(D_["product"].sem, 1)

                    sweep(pe, turn, ups, downs)

                @block.scalar
                def _(act):
                    def turn(j, a):
                        wait(act, D_["turned"], j + 1)
                        wait(act, D_["hidden"], 8 * (j - 1))
                        act.activation(spreads[:, a, :], turned[a], ACT.Copy).then_inc(D_["turned_sb"].sem, 1)

                    def hidden(j, a):
                        wait(act, D_["product"], j - 1)
                        for m in range(8):
                            wait(act, D_["hidden"], 8 * j + m // 4 * 4 + 4)
                            act.activation(hid[a][:, m, :], hp[a][m // 4][:, m % 4 * P:m % 4 * P + P], func,
                                           bias=bias[:, m:m + 1]).then_inc(D_["hidden_sb"].sem, 1)

                    sweep(act, turn, hidden)
            for n_ in ("in", "turned", "turned_sb", "product", "dve_out"):
                D_[n_].base += NT
            D_["hidden"].base += 8 * NT
            D_["hidden_sb"].base += 8 * NT

        stage_h = stage.rearrange("p a c -> p (a c)")[:, 0:2048].rearrange("p (a m c) -> p a m c", a=2, m=8)

        def transformer_layer(l):
            typed_tables(l)
            edge_pass("hgt", tab_l2, 2 * D)

            def denominator(dve, link, av, inv):
                link(dve.tensor_scalar(inv, av[:, :, :, 32], 1e-10, None, ALU.add))
                link(dve.reciprocal(inv, inv))

            vector_phase(normalised(33, 32, denominator))
            w1 = arena[:, 0:2048].rearrange("p (k n) -> p k n", k=2)
            w2 = arena[:, 2048:4096].rearrange("p (m n) -> p m n", m=8)
            wo = flat_oh[:, 0:512].rearrange("p (k n) -> p k n", k=2)
            load((wo, A["L2_gnn_Wo"][l].rearrange("(k p) n -> p k n", p=P)),
                 (w1, A["L2_gnn_w1"][l].rearrange("(k p) n -> p k n", p=P)),
                 (w2, A["L2_gnn_w2"][l].rearrange("(m p) n -> p m n", p=P)),
                 (vecs[:, 0:D], row(A["L2_gnn_bo"][l])), (vecs[:, D:2 * D], row(A["L2_gnn_b2"][l])),
                 (vecs[:, 2 * D:3 * D], row(A["L2_gnn_ln1_g"][l])), (vecs[:, 3 * D:4 * D], row(A["L2_gnn_ln1_b"][l])),
                 (att[:, 0:D], row(A["L2_gnn_ln2_g"][l])), (att[:, D:2 * D], row(A["L2_gnn_ln2_b"][l])),
                 (cols[:, 0:8], A["L2_gnn_b1"][l].rearrange("(m p) -> p m", p=P)))
            project(lambda j: hbuf[:, j, :], 2, wo, 256,
                    dve_out=lambda dve, j, a, ps: dve.tensor_tensor(X[:, j, :], X[:, j, :], ps, ALU.add)
                    .then_inc(D_["dve_out"].sem, 1))
            add_row(vecs[:, 0:D])
            layer_norm(vecs[:, 2 * D:3 * D], vecs[:, 3 * D:4 * D])
            perceptron(w1, w2, cols[:, 0:8], ACT.Gelu)
            add_row(vecs[:, D:2 * D])
            layer_norm(att[:, 0:D], att[:, D:2 * D])

        def add_row(v):
            vector_phase(lambda dve, link: link(dve.tensor_tensor(X[:, :, :], X[:, :, :], over_blocks(v), ALU.add)))

        def layer_2():
            blocks = lambda t: t[:, :].rearrange("(j p) c -> p j c", p=P)
            load((blocks(residual), X[:, :, :]))

            def self_loops(sign):
                vector_phase(lambda dve, link: link(dve.scalar_tensor_tensor(
                    slot_loc[:, :], slot_bar[:, :], -sign * PADLOC / BIG, slot_loc[:, :], ALU.mult, ALU.add)))

            self_loops(1)
            for l in range(3):
                transformer_layer(l)
            self_loops(-1)
            load((vecs[:, 0:D], row(A["L2_gnn_out_g"])), (vecs[:, D:2 * D], row(A["L2_gnn_out_b"])),
                 (hbuf[:, :, :], blocks(residual)))
            layer_norm(vecs[:, 0:D], vecs[:, D:2 * D])
            vector_phase(lambda dve, link: link(dve.tensor_tensor(X[:, :, :], X[:, :, :], hbuf[:, :, :], ALU.add)))
            layer_norm()

        def layer_3():
            w1 = flat_oh[:, 0:2048].rearrange("p (k n) -> p k n", k=2)
            w2 = flat_oh[:, 2048:4096].rearrange("p (m n) -> p m n", m=8)
            load((tab_l3[:, :].rearrange("(j p) c -> p j c", p=P), X[:, :, :]))
            edge_pass("gin", tab_l3, D)
            load((w1, A["L3_gnn_W1"].rearrange("(k p) n -> p k n", p=P)),
                 (w2, A["L3_gnn_W2"].rearrange("(m p) n -> p m n", p=P)),
                 (vecs[:, 0:D], row(A["L3_gnn_b2"])),
                 (cols[:, 0:8], A["L3_gnn_b1"].rearrange("(m p) -> p m", p=P)),
                 (cols[:, 8:16], A["L3_gnn_gamma"].rearrange("(m p) -> p m", p=P)),
                 (cols[:, 16:24], A["L3_gnn_beta"].rearrange("(m p) -> p m", p=P)))
            hid = [arena[:, NP * m:NP * m + NP] for m in range(7)] + [border[:, 0:NP]]
            turned = [PS[0][:, 0:D], PS[7][:, 0:D]]
            hp = [[PS[1], PS[2]], [PS[3], PS[4]]]
            rows_in = vecs[:, D:3 * D].rearrange("p (a c) -> p a c", a=2)
            with nc.Block() as block:
                @block.vector
                def _(dve):
                    def take(j, a):
                        wait(dve, D_["turned"], j - 1)
                        dve.tensor_copy(rows_in[:, a, :], acc[:, j, 0:D]).then_inc(D_["in"].sem, 1)

                    sweep(dve, take)

                @block.tensor
                def _(pe):
                    def turn(j, a):
                        wait(pe, D_["in"], j + 1)
                        wait(pe, D_["turned_sb"], j - 1)
                        for k in range(2):
                            op = pe.transpose(turned[a][:, k * P:k * P + P], rows_in[:, a, k * P:k * P + P],
                                              ident[:, :])
                        op.then_inc(D_["turned"].sem, 1)

                    def ups(j, a):
                        wait(pe, D_["turned_sb"], j + 1)
                        wait(pe, D_["hidden_sb"], 8 * (j - 1))
                        for m in range(8):
                            for k in range(2):
                                op = pe.matmul(hp[a][m // 4][:, m % 4 * P:m % 4 * P + P], w1[:, k, m * P:m * P + P],
                                               spreads[:, a, k * P:k * P + P], start=k == 0, stop=k == 1)
                            op.then_inc(D_["hidden"].sem, 1)

                    sweep(pe, turn, ups)

                @block.scalar
                def _(act):
                    def turn(j, a):
                        wait(act, D_["turned"], j + 1)
                        wait(act, D_["hidden"], 8 * (j - 1))
                        act.activation(spreads[:, a, :], turned[a], ACT.Copy).then_inc(D_["turned_sb"].sem, 1)

                    def keep(j, a):
                        for m in range(8):
                            wait(act, D_["hidden"], 8 * j + m // 4 * 4 + 4)
                            act.activation(hid[m][:, ds(P * j, P)], hp[a][m // 4][:, m % 4 * P:m % 4 * P + P],
                                           ACT.Identity, bias=cols[:, m:m + 1]).then_inc(D_["hidden_sb"].sem, 1)

                    sweep(act, turn, keep)
            for n_ in ("in", "turned", "turned_sb"):
                D_[n_].base += NT
            D_["hidden"].base += 8 * NT
            D_["hidden_sb"].base += 8 * NT

            chunks = [(c, min(512, N - c)) for c in range(0, N, 512)]
            part = acc[:, 0:2, :].rearrange("p a b -> p (a b)")[:, 0:8 * len(chunks) * 6]\
                .rearrange("p (m c f) -> p m c f", m=8, f=6)
            mv = acc[:, 2, 0:16].rearrange("p (m f) -> p m f", f=2)
            sd, sc, bi = acc[:, 3, 0:8], acc[:, 3, 8:16], acc[:, 3, 16:24]

            def batch_stats(dve, link):
                for m in range(8):
                    for c, (c0, n_) in enumerate(chunks):
                        link(dve.bn_stats(out=part[:, m, c, :], in_=hid[m][:, c0:c0 + n_]))
                    link(dve.bn_aggr(out=mv[:, m, :], in_=part[:, m, :, :]))
                link(dve.tensor_scalar(sd, mv[:, :, 1], 1e-5, None, ALU.add))

            vector_phase(batch_stats)
            scalar_phase((sc, sd, ACT.Sqrt))

            def affine(dve, link):
                link(dve.reciprocal(sd, sc))
                link(dve.tensor_tensor(sc, sd, cols[:, 8:16], ALU.mult))
                link(dve.tensor_tensor(bi, mv[:, :, 0], sc, ALU.mult))
                link(dve.tensor_tensor(bi, cols[:, 16:24], bi, ALU.subtract))

            vector_phase(affine)

            hin = acc[:, 4:12, :].rearrange("p a b -> p (a b)")[:, 0:2048].rearrange("p (a m c) -> p a m c", a=2, m=8)
            sums = acc[:, 12, 0:D]
            prod = [PS[5][:, 0:D], PS[6][:, 0:D]]
            with nc.Block() as block:
                @block.scalar
                def _(act):
                    def hidden(j, a):
                        wait(act, D_["product"], j - 1)
                        for m in range(8):
                            act.activation(hin[:, a, m, :], hid[m][:, ds(P * j, P)], ACT.Relu, bias=bi[:, m:m + 1],
                                           scale=sc[:, m:m + 1]).then_inc(D_["hidden_sb"].sem, 1)

                    sweep(act, hidden)

                @block.tensor
                def _(pe):
                    def downs(j, a):
                        wait(pe, D_["hidden_sb"], 8 * (j + 1))
                        wait(pe, D_["tmp"], j - 1)
                        for m in range(8):
                            op = pe.matmul(prod[a], hin[:, a, m, :], w2[:, m, :], start=m == 0, stop=m == 7)
                        op.then_inc(D_["product"].sem, 1)

                    sweep(pe, downs)

                @block.vector
                def _(dve):
                    def give(j, a):
                        wait(dve, D_["product"], j + 1)
                        wait(dve, D_["dve_out"], j)
                        dve.tensor_tensor(sums, prod[a], vecs[:, 0:D], ALU.add).then_inc(D_["tmp"].sem, 1)
                        wait(dve, D_["tmp"], j + 1)
                        dve.scalar_tensor_tensor(X[:, j, :], sums, 0.0, X[:, j, :], ALU.max, ALU.add)\
                           .then_inc(D_["dve_out"].sem, 1)

                    sweep(dve, give)
            D_["hidden_sb"].base += 8 * NT
            for n_ in ("product", "tmp", "dve_out"):
                D_[n_].base += NT
            layer_norm()

        constants()
        load_edges()
        histogram()
        place_nodes()
        rank_edges()
        scatter_records()
        load_slots()
        find_borders()
        layer_0()
        layer_1()
        layer_2()
        layer_3()
        load((out[0:(NT - 1) * P, :].rearrange("(j p) c -> p j c", p=P), X[:, 0:NT - 1, :]),
             (out[(NT - 1) * P:N, :], X[0:NLAST, NT - 1, :]))


def kernel(**inputs):
    import numpy as np
    import concourse.bacc as bacc
    from concourse.bass_utils import run_bass_kernel_spmd

    nc = bacc.Bacc("TRN2", target_bir_lowering=False, num_devices=1)
    arrays = {name: np.ascontiguousarray(a) for name, a in inputs.items()}
    A = {name: nc.dram_tensor(name, a.shape, mybir.dt.from_np(a.dtype), kind="ExternalInput").ap()
         for name, a in arrays.items()}
    out = nc.dram_tensor("out", (N, D), F32, kind="ExternalOutput").ap()
    gnn_kernel(nc, A, out)
    result = run_bass_kernel_spmd(nc, [arrays], core_ids=[0])
    return result.results[0]["out"]
```

```python
from contextlib import ExitStack

import concourse.bass as bass
from concourse import mybir

F32 = mybir.dt.float32
I32 = mybir.dt.int32
BF16 = mybir.dt.bfloat16
ALU = mybir.AluOpType
ACT = mybir.ActivationFunctionType
AX = mybir.AxisListType.X
RMAX = bass.bass_isa.ReduceOp.max

P = 128
N, D, E = 3125, 256, 50000
NT = -(-N // P)
NLAST = N - (NT - 1) * P
NP = NT * P
GT = 2
GRP = (E + N + NT * (GT * P - 1)) // (GT * P)
BT = 16
BG = BT // GT
NB = -(-GRP // BG)
T = NB * BT
H = 8
QC = 4
EC = 2 * QC * -(-E // (2 * QC * P))
RC = EC + NT
SC = 4 * QC
BIG = 2.0 ** 100
PADSEG, PADLOC, PADDST = 9999.0, 999.0, 4000
LH = 64
assert (P - 1) * EC < E and NB % 2 == 1 and NT % 2 == 1 and GRP <= NB * BG


class Signal:

    def __init__(self, handle):
        self.sem, self.base = handle, 0

    def at(self, n):
        return self.base + n


def ds(start, n):
    return bass.ds(start, n)


def needed(n):
    return not isinstance(n, int) or n > 0


def gnn_kernel(nc, A, out):
    ctx = ExitStack()
    with ctx:
        def sb(name, shape, dt=F32):
            return ctx.enter_context(nc.sbuf_tensor(name, shape, dt))

        def sig(name):
            return Signal(ctx.enter_context(nc.semaphore(name)))

        def dram(name, shape, dt=F32):
            return nc.dram_tensor(name, shape, dt, kind="Internal").ap()

        tab_l0a, tab_l0b, tab_l1 = dram("tab_l0a", (NP, 128)), dram("tab_l0b", (NP, D)), dram("tab_l1", (NP, D + H))
        tab_l2, tab_l3 = dram("tab_l2", (3 * NP, 2 * D)), dram("tab_l3", (NP, D))
        residual = dram("residual", (NP, D))
        base_dram = dram("base_dram", (LH * LH, 1))
        rec_dram = dram("rec_dram", (P * T, 8), I32)
        seg_dram = dram("seg_dram", (1, T * P + 2))
        hid_dram = dram("hid_dram", (8, P, NP))

        ident = sb("ident", [P, P])
        ones = sb("ones", [P, P])
        iota_row = sb("iota_row", [P, P])
        lane_mask = sb("lane_mask", [P, 16])
        same_head = sb("same_head", [P, P])
        head_col = sb("head_col", [P, H])
        slot_src = sb("slot_src", [P, T], I32)
        slot_typed = sb("slot_typed", [P, T], I32)
        slot_loc = sb("slot_loc", [P, T])
        slot_bar = sb("slot_bar", [P, T])
        border = sb("border", [P, NB * (P + 1)])
        tile_border = sb("tile_border", [P, NB * 33])
        straddle = sb("straddle", [P, NB])
        block_of = sb("block_of", [1, 2, NB * BG + 16], I32)
        type_of = sb("type_of", [P, NT])
        X = sb("X", [P, NT, D])
        acc = sb("acc", [P, NT, 272])
        arena = sb("arena", [P, 24640])
        QTAB = 2 * BT * 512
        qtab = arena[:, QTAB:QTAB + NT * D].rearrange("p (j c) -> p j c", j=NT)
        small = sb("small", [P, 256])

        PS = [ctx.enter_context(nc.psum_tensor(f"bank{i}", [P, 512], F32)) for i in range(8)]

        loaded = sig("loaded")
        step = sig("step")
        made = sig("made")
        converted = sig("converted")
        tick = sig("tick")
        multiplied = sig("multiplied")

        def constants():
            ii = arena[:, 0:P].bitcast(I32)
            pi = arena[:, P:P + 1].bitcast(I32)
            w = arena[:, 2 * P:3 * P].bitcast(I32)
            v = arena[:, 3 * P:4 * P].bitcast(I32)
            pf = arena[:, 4 * P:4 * P + 4]
            cf = arena[:, 5 * P:6 * P]
            with nc.Block() as block:
                @block.gpsimd
                def _(pool):
                    pool.iota(ii, pattern=[[1, P]], base=0, channel_multiplier=0).then_inc(made.sem, 1)
                    pool.iota(pi, pattern=[[1, 1]], base=0, channel_multiplier=1).then_inc(made.sem, 1)

                @block.vector
                def _(dve):
                    n = 0

                    def link(op):
                        nonlocal n
                        n += 1
                        op.then_inc(step.sem, 1)
                        dve.wait_ge(step.sem, step.at(n))

                    dve.wait_ge(made.sem, made.at(2))
                    link(dve.memset(ones[:, :], 1.0))
                    link(dve.tensor_copy(iota_row[:, :], ii))
                    link(dve.tensor_copy(pf[:, 0:1], pi))
                    link(dve.tensor_scalar(ident[:, :], iota_row[:, :], pf[:, 0:1], None, ALU.is_equal))
                    link(dve.tensor_scalar(w[:, 0:1], pi, 15, None, ALU.bitwise_and))
                    link(dve.tensor_scalar(v[:, 0:1], pi, 4, None, ALU.logical_shift_right))
                    link(dve.tensor_copy(pf[:, 1:2], w[:, 0:1]))
                    link(dve.tensor_copy(pf[:, 2:3], v[:, 0:1]))
                    link(dve.tensor_scalar(lane_mask[:, :], iota_row[:, 0:16], pf[:, 1:2], None, ALU.is_equal))
                    link(dve.tensor_scalar(head_col[:, :], iota_row[:, 0:H], pf[:, 2:3], None, ALU.is_equal))
                    link(dve.tensor_scalar(w, ii, 4, None, ALU.logical_shift_right))
                    link(dve.tensor_copy(cf, w))
                    link(dve.tensor_scalar(same_head[:, :], cf, pf[:, 2:3], None, ALU.is_equal))
                    step.base += n
            made.base += 2

        hi, lo = arena[:, 0:EC], arena[:, RC:RC + EC]
        nowhere = arena[:, 2 * RC:3 * RC]
        dst_i = arena[:, 3 * RC:3 * RC + EC].bitcast(I32)
        src_i = arena[:, 4 * RC:4 * RC + EC].bitcast(I32)
        typ_i = arena[:, 5 * RC:5 * RC + EC].bitcast(I32)
        recf = arena[:, 6 * RC:14 * RC].rearrange("p (c f) -> p c f", f=8)
        rec = arena[:, 6 * RC:14 * RC].bitcast(I32).rearrange("p (c f) -> p c f", f=8)
        row_f, row_i = arena[:, 14 * RC:15 * RC], arena[:, 15 * RC:16 * RC].bitcast(I32)
        row_i2 = arena[:, 16 * RC:17 * RC].bitcast(I32)
        W0 = 17 * RC
        slots = arena[:, 13312:13312 + 8 * T].rearrange("p (t f) -> p t f", f=8)
        slots_i = arena[:, 13312:13312 + 8 * T].bitcast(I32).rearrange("p (t f) -> p t f", f=8)
        seg_lane = arena[:, 17024:17024 + NB * (P + 2)].rearrange("p (b s) -> p b s", b=NB)
        differs = arena[:, 20800:24640]

        def view(off, n):
            return arena[:, W0 + off:W0 + off + n]

        tri = view(0, P)
        scr = [view(P + LH * i, LH) for i in range(12)]
        V2 = P + 12 * LH
        self_pos = view(V2, NT)
        group_f = view(V2 + 32, GRP)
        block_f = view(V2 + 32 + GRP, GRP)
        pads = acc[:, :, :].rearrange("p a b -> p (a b)")[:, 0:T * 8].rearrange("p (t f) -> p t f", f=8)
        assert W0 + V2 + 32 + 2 * GRP <= 13312

        R0 = 13312
        NQ = EC // QC
        RING = 8
        oh_hi = arena[:, R0:R0 + 1024].bitcast(BF16).rearrange("p (q u c) -> p q u c", q=RING, u=QC)
        oh_lo = arena[:, R0 + 1024:R0 + 2048].bitcast(BF16).rearrange("p (q u c) -> p q u c", q=RING, u=QC)
        hiT = arena[0:LH, R0 + 2048:R0 + 3072].rearrange("p (a u c) -> p a u c", a=2, u=QC)
        hiT_b = arena[0:LH, R0 + 3072:R0 + 3584].bitcast(BF16).rearrange("p (a u c) -> p a u c", a=2, u=QC)
        before = arena[:, R0 + 3584:R0 + 4096].bitcast(BF16).rearrange("p (a u c) -> p a u c", a=2, u=QC)
        next_slot = arena[0:LH, R0 + 4096:R0 + 5120].rearrange("p (q u c) -> p q u c", q=4, u=QC)
        picked = arena[:, R0 + 5120:R0 + 5632].rearrange("p (a u c) -> p a u c", a=2, u=QC)
        pos16 = arena[:, R0 + 5632:R0 + 5632 + 2 * SC].rearrange("p (a u) -> p a u", a=2)
        parts_i = arena[:, R0 + 5664:R0 + 5664 + 3 * SC].bitcast(I32).rearrange("p (k u) -> p k u", k=3)
        parts_f = arena[:, R0 + 5712:R0 + 5712 + 3 * SC].rearrange("p (k u) -> p k u", k=3)
        ident_b = arena[:, R0 + 5760:R0 + 5824].bitcast(BF16)
        stage_rec = arena[:, R0 + 5824:R0 + 5824 + 2 * SC * 8].bitcast(I32).rearrange("p (a u f) -> p a u f", a=2, u=SC)
        stage_row = arena[:, R0 + 6080:R0 + 6080 + 2 * SC].bitcast(I32).rearrange("p (a u) -> p a u", a=2)

        onehot = sig("onehot")
        turned = sig("turned")
        turned_sb = sig("turned_sb")
        paired = sig("paired")
        masked = sig("masked")
        ranked = sig("ranked")
        taken = sig("taken")
        counted = sig("counted")
        kept = sig("kept")
        scattered = sig("scattered")

        def load_edges():
            with nc.Block() as block:
                @block.vector
                def _(dve):
                    dve.memset(dst_i, PADDST).then_inc(step.sem, 1)
                    dve.memset(src_i, 0).then_inc(step.sem, 1)
                    dve.memset(typ_i, 0).then_inc(step.sem, 1)
                    dve.memset(X[:, NT - 1, :], 0.0).then_inc(step.sem, 1)
                    dve.memset(type_of[:, :], 0.0).then_inc(step.sem, 1)
                    dve.memset(pads[:, :, 0:2], 0.0).then_inc(step.sem, 1)
                    dve.memset(pads[:, :, 2:3], PADSEG).then_inc(step.sem, 1)
                    dve.memset(pads[:, :, 3:4], PADLOC).then_inc(step.sem, 1)
                    dve.memset(pads[:, :, 4:8], 0.0).then_inc(step.sem, 1)

                @block.sync
                def _(sp):
                    sp.wait_ge(step.sem, step.at(9))
                    full, rest = (P - 1) * EC, E - (P - 1) * EC
                    for tile, name in ((dst_i, "dst"), (src_i, "src"), (typ_i, "edge_type_3")):
                        sp.dma_start(tile[0:P - 1, :], A[name][0:full].rearrange("(p c) -> p c", c=EC))\
                          .then_inc(loaded.sem, 16)
                        sp.dma_start(tile[P - 1:P, 0:rest], A[name][full:E].rearrange("(p c) -> p c", p=1))\
                          .then_inc(loaded.sem, 16)
                    sp.dma_start(X[:, 0:NT - 1, :], A["x"][0:(NT - 1) * P, :].rearrange("(j p) c -> p j c", p=P))\
                      .then_inc(loaded.sem, 16)
                    sp.dma_start(X[0:NLAST, NT - 1, :], A["x"][(NT - 1) * P:N, :]).then_inc(loaded.sem, 16)
                    sp.dma_start(rec_dram[:, :].rearrange("(p t) f -> p (t f)", p=P),
                                 pads[:, :, :].rearrange("p t f -> p (t f)").bitcast(I32)).then_inc(loaded.sem, 16)
                    sp.wait_ge(loaded.sem, loaded.at(16 * 9))

                @block.gpsimd
                def _(pool):
                    pool.wait_ge(step.sem, step.at(5))
                    with nc.allow_non_contiguous_dma(reason="3125 node types, once"):
                        pool.dma_start(type_of[:, 0:NT - 1],
                                       A["node_type_4"][0:(NT - 1) * P].rearrange("(j p) -> p j", p=P))\
                            .then_inc(converted.sem, 16)
                        pool.dma_start(type_of[0:NLAST, NT - 1:NT],
                                       A["node_type_4"][(NT - 1) * P:N].rearrange("(p a) -> p a", a=1))\
                            .then_inc(converted.sem, 16)
                    pool.wait_ge(converted.sem, converted.at(32))
            step.base += 9
            loaded.base += 16 * 9
            converted.base += 32

        def histogram():
            with nc.Block() as block:
                @block.vector
                def _(dve):
                    n = 0

                    def link(op):
                        nonlocal n
                        n += 1
                        op.then_inc(step.sem, 1)
                        dve.wait_ge(step.sem, step.at(n))

                    link(dve.tensor_scalar(row_i[:, 0:EC], dst_i, 6, None, ALU.logical_shift_right))
                    link(dve.tensor_copy(hi, row_i[:, 0:EC]))
                    link(dve.tensor_scalar(row_i[:, 0:EC], dst_i, LH - 1, None, ALU.bitwise_and))
                    link(dve.tensor_copy(lo, row_i[:, 0:EC]))

                    def body(i, first=False):
                        for q in range(RING):
                            if not first:
                                dve.wait_ge(counted.sem, counted.at(RING * i + q - RING + 1))
                            for u in range(QC):
                                for oh, number in ((oh_hi, hi), (oh_lo, lo)):
                                    op = dve.tensor_scalar(oh[:, q, u, :], iota_row[:, 0:LH],
                                                           number[:, ds(QC * (RING * i + q) + u, 1)], None,
                                                           ALU.is_equal)
                            op.then_inc(onehot.sem, 1)
                            if isinstance(i, int) and RING * i + q == NQ - 1:
                                break

                    body(0, first=True)
                    with dve.Fori(1, NQ // RING) as i:
                        body(i)
                    body(NQ // RING)
                    step.base += n

                @block.tensor
                def _(pe):
                    def body(i):
                        for q in range(RING):
                            first, last = [isinstance(i, int) and RING * i + q == x for x in (0, NQ - 1)]
                            pe.wait_ge(onehot.sem, onehot.at(RING * i + q + 1))
                            for u in range(QC):
                                op = pe.matmul(PS[0][0:LH, 0:LH], oh_hi[:, q, u, :], oh_lo[:, q, u, :],
                                               start=first and u == 0, stop=last and u == QC - 1)
                            op.then_inc(counted.sem, 1)
                            if last:
                                break

                    body(0)
                    with pe.Fori(1, NQ // RING) as i:
                        body(i)
                    body(NQ // RING)
            onehot.base += NQ
            counted.base += NQ

        def place_nodes():
            rows = iota_row[0:LH, 0:LH]
            pcol, chalf, codd, q, cnt, run, zero, m_pair, m_before, m_prev, itf, it2f = [s[0:LH, :] for s in scr]
            it, it2 = itf.bitcast(I32), it2f.bitcast(I32)
            with nc.Block() as block:
                @block.vector
                def _(dve):
                    n = 0

                    def link(op):
                        nonlocal n
                        n += 1
                        op.then_inc(step.sem, 1)
                        dve.wait_ge(step.sem, step.at(n))

                    link(dve.tensor_tensor(small[:, 128:256], ident[:, :], iota_row[:, :], ALU.mult))
                    link(dve.tensor_reduce(small[:, 0:1], small[:, 128:256], AX, ALU.add))
                    link(dve.tensor_scalar(tri, iota_row[:, :], small[:, 0:1], None, ALU.is_gt))
                    link(dve.tensor_copy(it[:, 0:1], small[0:LH, 0:1]))
                    link(dve.tensor_scalar(it[:, 1:2], it[:, 0:1], 1, None, ALU.logical_shift_right))
                    link(dve.tensor_scalar(it[:, 2:3], it[:, 0:1], 1, None, ALU.bitwise_and))
                    link(dve.tensor_copy(pcol[:, 0:3], it[:, 0:3]))
                    link(dve.tensor_copy(it, rows))
                    link(dve.tensor_scalar(it2, it, 1, None, ALU.logical_shift_right))
                    link(dve.tensor_copy(chalf, it2))
                    link(dve.tensor_scalar(it2, it, 1, None, ALU.bitwise_and))
                    link(dve.tensor_copy(codd, it2))
                    link(dve.tensor_scalar(m_pair, chalf, pcol[:, 1:2], None, ALU.is_equal))
                    link(dve.tensor_scalar(q[:, 0:1], pcol[:, 2:3], -1.0, 1.0, ALU.mult, ALU.add))
                    link(dve.tensor_scalar(m_before, chalf, pcol[:, 1:2], q[:, 0:1], ALU.is_gt, ALU.mult))
                    link(dve.tensor_tensor(m_prev, m_pair, codd, ALU.mult))
                    link(dve.tensor_scalar(m_prev, m_prev, q[:, 0:1], None, ALU.mult))
                    link(dve.tensor_scalar(q[:, 1:2], pcol[:, 0:1], float(LH), None, ALU.mult))
                    link(dve.tensor_scalar(run, rows, q[:, 1:2], float(N), ALU.add, ALU.is_lt))
                    link(dve.tensor_tensor(cnt, PS[0][0:LH, 0:LH], run, ALU.add))
                    link(dve.tensor_reduce(q[:, 2:3], cnt, AX, ALU.add))
                    dve.sem_inc(rows_summed.sem, 1)
                    dve.wait_ge(multiplied.sem, multiplied.at(2))
                    link(dve.tensor_scalar(q[:, 3:4], PS[1][0:LH, 0:1], float(GT * P - 1), None, ALU.add))
                    link(dve.tensor_copy(it[:, 0:1], q[:, 3:4]))
                    link(dve.tensor_scalar(it[:, 1:2], it[:, 0:1], (GT * P).bit_length() - 1, None,
                                           ALU.logical_shift_right))
                    link(dve.tensor_copy(q[:, 4:5], it[:, 1:2]))
                    dve.sem_inc(rows_summed.sem, 1)
                    dve.wait_ge(multiplied.sem, multiplied.at(3))
                    link(dve.tensor_copy(q[:, 5:6], PS[3][0:LH, 0:1]))
                    link(dve.tensor_copy(q[:, 8:9], PS[2][0:LH, 0:1]))
                    link(dve.tensor_scalar(q[:, 6:7], q[:, 5:6], float(GT * P), q[:, 8:9], ALU.mult, ALU.add))
                    link(dve.memset(zero, 0.0))
                    link(dve.tensor_tensor_scan(run, zero, cnt, 0.0, ALU.add, ALU.add))
                    link(dve.tensor_tensor(run, run, cnt, ALU.subtract))
                    link(dve.tensor_scalar(run, run, q[:, 6:7], None, ALU.add))
                    dve.sem_inc(placed.sem, 1)
                    link(dve.tensor_scalar(next_slot[:, 3, QC - 1, :], run, 1.0, None, ALU.add))
                    link(dve.tensor_scalar(q[:, 7:8], pcol[:, 0:1], float(2 * NT), q[:, 0:1], ALU.is_lt, ALU.mult))
                    dve.wait_ge(made.sem, made.at(1))
                    link(dve.tensor_scalar(block_f[0:LH, :], group_f[0:LH, :], q[:, 5:6], q[:, 7:8],
                                           ALU.is_ge, ALU.mult))
                    dve.sem_inc(rows_summed.sem, 1)
                    dve.wait_ge(multiplied.sem, multiplied.at(4))
                    link(dve.tensor_scalar(block_f, PS[4][:, 0:GRP], -1.0, None, ALU.add))
                    link(dve.memset(block_of[:, :, :], 0))
                    for k in range(2):
                        link(dve.tensor_copy(block_of[0:1, k, 2 * k:2 * k + GRP], block_f[0:1, :]))
                    marks["step"] = n

                @block.gpsimd
                def _(pool):
                    pool.iota(group_f, pattern=[[1, GRP]], base=0, channel_multiplier=0,
                              allow_small_or_imprecise_dtypes=True).then_inc(made.sem, 1)

                @block.tensor
                def _(pe):
                    pe.wait_ge(rows_summed.sem, rows_summed.at(1))
                    pe.matmul(PS[1][0:LH, 0:1], m_pair, q[:, 2:3], start=True, stop=True).then_inc(multiplied.sem, 1)
                    pe.matmul(PS[2][0:LH, 0:1], m_prev, q[:, 2:3], start=True, stop=True).then_inc(multiplied.sem, 1)
                    pe.wait_ge(rows_summed.sem, rows_summed.at(2))
                    pe.matmul(PS[3][0:LH, 0:1], m_before, q[:, 4:5], start=True, stop=True)\
                      .then_inc(multiplied.sem, 1)
                    pe.wait_ge(rows_summed.sem, rows_summed.at(3))
                    pe.matmul(PS[4][:, 0:GRP], ones[0:LH, :], block_f[0:LH, :], start=True, stop=True)\
                      .then_inc(multiplied.sem, 1)

                @block.sync
                def _(sp):
                    sp.wait_ge(placed.sem, placed.at(1))
                    sp.dma_start(base_dram[:, :].rearrange("(h l) a -> h (l a)", h=LH), run).then_inc(loaded.sem, 16)
                    sp.wait_ge(loaded.sem, loaded.at(16))
                    with nc.allow_non_contiguous_dma(reason="one number for each node, once"):
                        sp.dma_start(self_pos, base_dram[0:NP, :].rearrange("(j p) a -> p (j a)", p=P))\
                          .then_inc(loaded.sem, 16)
                    sp.wait_ge(loaded.sem, loaded.at(32))
            step.base += marks["step"]
            made.base += 1
            loaded.base += 32
            multiplied.base += 4
            rows_summed.base += 3
            placed.base += 1

        rows_summed, placed = sig("rows_summed"), sig("placed")
        marks = {}

        staged, sent = sig("staged"), [sig("sent0"), sig("sent1")]

        def make_records():
            def build(dve, link):
                ed, se = slice(0, EC), slice(EC, RC)
                link(dve.memset(recf, 0.0))
                link(dve.tensor_copy(rec[:, ed, 0], src_i))
                link(dve.tensor_copy(row_f[:, ed], src_i))
                link(dve.tensor_copy(recf[:, ed, 4], typ_i))
                link(dve.scalar_tensor_tensor(rec[:, ed, 1], recf[:, ed, 4], float(NP), row_f[:, ed],
                                              ALU.mult, ALU.add))
                link(dve.memset(recf[:, ed, 4], 0.0))
                link(dve.tensor_copy(recf[:, ed, 2], dst_i))
                link(dve.tensor_scalar(row_i[:, ed], dst_i, P - 1, None, ALU.bitwise_and))
                link(dve.tensor_copy(recf[:, ed, 3], row_i[:, ed]))
                link(dve.tensor_scalar(nowhere[:, ed], recf[:, ed, 2], float(PADDST), 2.0 ** 20,
                                       ALU.is_ge, ALU.mult))
                link(dve.tensor_scalar(recf[:, se, 2], iota_row[:, 0:NT], float(P), small[:, 0:1],
                                       ALU.mult, ALU.add))
                link(dve.tensor_copy(rec[:, se, 0], recf[:, se, 2]))
                link(dve.tensor_copy(rec[:, se, 1], recf[:, se, 2]))
                link(dve.memset(recf[:, se, 4], 0.0))
                link(dve.tensor_scalar(recf[:, se, 3], recf[:, se, 4], small[:, 0:1], None, ALU.add))
                link(dve.memset(recf[:, se, 4], -BIG))
                link(dve.tensor_scalar(nowhere[:, se], recf[:, se, 2], float(N), 2.0 ** 20, ALU.is_ge, ALU.mult))
                link(dve.tensor_copy(row_i[:, se], self_pos))
                link(dve.tensor_scalar(row_i2[:, se], row_i[:, se], P - 1, None, ALU.bitwise_and))
                link(dve.tensor_copy(row_f[:, se], row_i2[:, se]))
                link(dve.tensor_scalar(row_i2[:, se], row_i[:, se], 7, None, ALU.logical_shift_right))
                link(dve.tensor_copy(self_pos, row_i2[:, se]))
                link(dve.tensor_tensor(nowhere[:, se], nowhere[:, se], self_pos, ALU.add))
                link(dve.scalar_tensor_tensor(row_i[:, se], row_f[:, se], float(T), nowhere[:, se],
                                              ALU.mult, ALU.add))
                link(dve.tensor_copy(ident_b, ident[:, :]))
            vector_phase(build)

        def sort_edges():
            LAG = dict(one_hots=0, turn=1, place=2, pair=2, mask=3, rank=4, pick=5)
            SCATTER = 9
            turned_hi = [PS[0][0:LH, :], PS[1][0:LH, :]]
            counts = [PS[2][0:LH, 0:QC * LH], PS[3][0:LH, 0:QC * LH]]
            pairs = [PS[4], PS[5]]
            slots_of = [PS[6][:, 0:QC * LH], PS[7][:, 0:QC * LH]]
            NBAT = -(-NQ // 4)
            four = "p (u c) -> p u c"

            def run(eng, slot_fn):
                for w in range(RING):
                    slot_fn(0, w)
                with eng.Fori(1, NQ // RING) as i:
                    for w in range(RING):
                        slot_fn(i, w)
                for q in range(NQ // RING * RING, 4 * NBAT + SCATTER - 3):
                    slot_fn(q // RING, q % RING)

            class Quad:

                def __init__(self, i, w, lag):
                    self.q = RING * i + w - lag
                    self.r, self.a = (w - lag) % RING, (w - lag) % 2
                    self.there = not isinstance(i, int) or 0 <= self.q < NQ
                    self.batch_column = self.r // 4 % 2, self.r % 4 * QC
                    self.batch = 2 * i + (w - lag) // 4

            with nc.Block() as block:
                @block.vector
                def _(dve):
                    linked = 0

                    def slot_fn(i, w):
                        x = Quad(i, w, LAG["one_hots"])
                        if x.there:
                            if needed(x.q - RING + 1):
                                dve.wait_ge(picked_up.sem, picked_up.at(x.q - RING + 1))
                            for u in range(QC):
                                for oh, number in ((oh_hi, hi), (oh_lo, lo)):
                                    op = dve.tensor_scalar(oh[:, x.r, u, :], iota_row[:, 0:LH],
                                                           number[:, ds(QC * x.q + u, 1)], None, ALU.is_equal)
                            op.then_inc(onehot.sem, 1)
                        x = Quad(i, w, LAG["pick"])
                        if x.there:
                            dve.wait_ge(ranked.sem, ranked.at(x.q + 1))
                            if needed(x.q - 1):
                                dve.wait_ge(picked_up.sem, picked_up.at(x.q - 1))
                            dve.tensor_tensor(picked[:, x.a, :, :], slots_of[x.a].rearrange(four, u=QC),
                                              oh_lo[:, x.r, :, :], ALU.mult).then_inc(taken.sem, 1)
                        x = Quad(i, w, LAG["place"])
                        if x.there:
                            dve.wait_ge(turned.sem, turned.at(x.q + 1))
                            if needed(x.q):
                                dve.wait_ge(placed_next.sem, placed_next.at(x.q))
                            if needed(x.q - 3):
                                dve.wait_ge(ranked.sem, ranked.at(x.q - 3))
                            dve.tensor_tensor(
                                next_slot[:, x.r % 4, :, :],
                                next_slot[:, (x.r + 3) % 4, QC - 1:QC, :].to_broadcast([LH, QC, LH]),
                                counts[x.a].rearrange(four, u=QC), ALU.add).then_inc(placed_next.sem, 1)
                        x = Quad(i, w, LAG["pick"])
                        if x.there:
                            dve.wait_ge(taken.sem, taken.at(x.q + 1))
                            a, c = x.batch_column
                            dve.tensor_reduce(pos16[:, a, c:c + QC], picked[:, x.a, :, :], AX, ALU.add)\
                               .then_inc(picked_up.sem, 1)
                        x = Quad(i, w, LAG["mask"])
                        if x.there:
                            dve.wait_ge(paired.sem, paired.at(x.q + 1))
                            if needed(x.q - 1):
                                dve.wait_ge(ranked.sem, ranked.at(x.q - 1))
                            dve.tensor_tensor(before[:, x.a, :, :], pairs[x.a][:, :].rearrange(four, u=QC),
                                              tri.unsqueeze(1).to_broadcast([P, QC, P]), ALU.mult)\
                               .then_inc(masked.sem, 1)
                        x = Quad(i, w, SCATTER)
                        if x.r % 4 == 0 and x.there:
                            a = x.batch_column[0]
                            cols = min(SC, EC - SC * x.batch) if isinstance(i, int) else SC
                            n = 0

                            def link(op):
                                nonlocal n
                                n += 1
                                op.then_inc(step.sem, 1)
                                dve.wait_ge(step.sem, step.at(5 * x.batch + n))

                            pi, pf = parts_i[:, :, 0:cols], parts_f[:, :, 0:cols]
                            if needed(4 * x.batch + cols // QC):
                                dve.wait_ge(picked_up.sem, picked_up.at(4 * x.batch + cols // QC))
                            link(dve.tensor_copy(pi[:, 2, :], pos16[:, a, 0:cols]))
                            dve.tensor_scalar(pi[:, 0, :], pi[:, 2, :], 7, None, ALU.logical_shift_right)
                            link(dve.tensor_scalar(pi[:, 1, :], pi[:, 2, :], P - 1, None, ALU.bitwise_and))
                            link(dve.tensor_copy(pf[:, 0:2, :], pi[:, 0:2, :]))
                            link(dve.tensor_tensor(pf[:, 2, :], pf[:, 0, :], nowhere[:, ds(SC * x.batch, cols)],
                                                   ALU.add))
                            uses = (x.batch - a) // 2 if isinstance(i, int) else i + (w - SCATTER) // 4 // 2
                            if needed(16 * SC * uses):
                                dve.wait_ge(sent[a].sem, sent[a].at(16 * SC * uses))
                            dve.scalar_tensor_tensor(stage_row[:, a, 0:cols], pf[:, 1, :], float(T), pf[:, 2, :],
                                                     ALU.mult, ALU.add)
                            link(dve.tensor_copy(stage_rec[:, a, 0:cols, :], rec[:, ds(SC * x.batch, cols), :]))
                            dve.sem_inc(staged.sem, 1)

                    run(dve, slot_fn)

                @block.tensor
                def _(pe):
                    def slot_fn(i, w):
                        x = Quad(i, w, LAG["turn"])
                        if x.there:
                            pe.wait_ge(onehot.sem, onehot.at(x.q + 1))
                            if needed(2 * (x.q - 1)):
                                pe.wait_ge(turned_sb.sem, turned_sb.at(2 * (x.q - 1)))
                            if needed(x.q - 1):
                                pe.wait_ge(placed_next.sem, placed_next.at(x.q - 1))
                            for u in range(QC):
                                pe.matmul(turned_hi[x.a][:, u * P:u * P + P], oh_hi[:, x.r, u, :], ident_b,
                                          start=True, stop=True)
                            for u in range(QC):
                                for v in range(u + 1):
                                    op = pe.matmul(counts[x.a][:, u * LH:u * LH + LH], oh_hi[:, x.r, v, :],
                                                   oh_lo[:, x.r, v, :], start=v == 0, stop=v == u)
                            op.then_inc(turned.sem, 1)
                        x = Quad(i, w, LAG["rank"])
                        if x.there:
                            pe.wait_ge(placed_next.sem, placed_next.at(x.q + 1))
                            pe.wait_ge(masked.sem, masked.at(x.q + 1))
                            if needed(x.q - 1):
                                pe.wait_ge(taken.sem, taken.at(x.q - 1))
                            for u in range(QC):
                                first = next_slot[:, x.r % 4, u - 1, :] if u else \
                                    next_slot[:, (x.r + 3) % 4, QC - 1, :]
                                out_ = slots_of[x.a][:, u * LH:u * LH + LH]
                                pe.matmul(out_, hiT[:, x.a, u, :], first, start=True, stop=False)
                                op = pe.matmul(out_, before[:, x.a, u, :], oh_lo[:, x.r, u, :], start=False, stop=True)
                            op.then_inc(ranked.sem, 1)
                        x = Quad(i, w, LAG["pair"])
                        if x.there:
                            pe.wait_ge(turned_sb.sem, turned_sb.at(2 * (x.q + 1)))
                            if needed(x.q - 1):
                                pe.wait_ge(masked.sem, masked.at(x.q - 1))
                            for u in range(QC):
                                op = pe.matmul(pairs[x.a][:, u * P:u * P + P], hiT_b[:, x.a, u, :], hiT_b[:, x.a, u, :],
                                               start=True, stop=True)
                            op.then_inc(paired.sem, 1)

                    run(pe, slot_fn)

                @block.scalar
                def _(act):
                    def slot_fn(i, w):
                        x = Quad(i, w, LAG["turn"])
                        if x.there:
                            act.wait_ge(turned.sem, turned.at(x.q + 1))
                            if needed(x.q - 1):
                                act.wait_ge(paired.sem, paired.at(x.q - 1))
                            act.activation(hiT_b[:, x.a, :, :], turned_hi[x.a].rearrange(four, u=QC), ACT.Copy)\
                               .then_inc(turned_sb.sem, 1)
                            if needed(x.q - 1):
                                act.wait_ge(ranked.sem, ranked.at(x.q - 1))
                            act.activation(hiT[:, x.a, :, :], turned_hi[x.a].rearrange(four, u=QC), ACT.Copy)\
                               .then_inc(turned_sb.sem, 1)

                    run(act, slot_fn)

                @block.gpsimd
                def _(pool):
                    def send(row, record, done):
                        pool.indirect_dma_start(
                            out=rec_dram[:, :], out_offset=bass.IndirectOffsetOnAxis(ap=row, axis=0),
                            in_=record, in_offset=None, bounds_check=P * T - 1, oob_is_err=False)\
                            .then_inc(done.sem, 16)

                    for c in range(EC, RC):
                        send(row_i[:, c:c + 1], rec[:, c, :], looped)

                    def body(b, a, cols=SC):
                        pool.wait_ge(staged.sem, staged.at(b + 1))
                        pool.sem_inc(tick.sem, 1)
                        for u in range(cols):
                            send(stage_row[:, a, u:u + 1], stage_rec[:, a, u, :], sent[a])

                    with pool.Fori(0, NBAT // 2) as i:
                        body(2 * i, 0)
                        body(2 * i + 1, 1)
                    if NBAT % 2:
                        body(NBAT - 1, 0, EC - SC * (NBAT - 1))
                    if needed(16 * NT):
                        pool.wait_ge(looped.sem, looped.at(16 * NT))
                        pool.sem_inc(tick.sem, 1)
                    if needed(16 * (EC - SC * (NBAT // 2))):
                        pool.wait_ge(sent[0].sem, sent[0].at(16 * (EC - SC * (NBAT // 2))))
                        pool.sem_inc(tick.sem, 1)
                    if needed(16 * SC * (NBAT // 2)):
                        pool.wait_ge(sent[1].sem, sent[1].at(16 * SC * (NBAT // 2)))
                        pool.sem_inc(tick.sem, 1)
            for s_ in (onehot, turned, paired, placed_next, ranked, taken, masked, picked_up):
                s_.base += NQ
            turned_sb.base += 2 * NQ
            staged.base += NBAT
            step.base += 5 * NBAT
            looped.base += 16 * NT
            sent[0].base += 16 * (EC - SC * (NBAT // 2))
            sent[1].base += 16 * SC * (NBAT // 2)

        placed_next, picked_up, looped = sig("placed_next"), sig("picked_up"), sig("looped")

        def load_slots():
            q4 = T // 4
            segT = arena[0:q4, 0:4 * P].rearrange("p (q s) -> p q s", q=4)
            with nc.Block() as block:
                @block.sync
                def _(sp):
                    sp.dma_start(slots_i.rearrange("p t f -> p (t f)"),
                                 rec_dram[:, :].rearrange("(p t) f -> p (t f)", p=P)).then_inc(loaded.sem, 16)
                    sp.wait_ge(placed.sem, placed.at(2))
                    for q in range(4):
                        sp.dma_start(seg_dram[0, 1 + q * q4 * P:1 + (q + 1) * q4 * P].rearrange("(t s) -> t s", s=P),
                                     segT[:, q, :]).then_inc(loaded.sem, 16)
                    sp.dma_start(seg_dram[0:1, 0:1], small[0:1, 1:2]).then_inc(loaded.sem, 16)
                    sp.dma_start(seg_dram[0:1, T * P + 1:T * P + 2], small[0:1, 1:2]).then_inc(loaded.sem, 16)
                    sp.wait_ge(loaded.sem, loaded.at(16 * 7))

                @block.vector
                def _(dve):
                    dve.memset(small[:, 1:2], -1.0).then_inc(step.sem, 1)
                    dve.wait_ge(loaded.sem, loaded.at(16))
                    dve.tensor_copy(slot_src[:, :], slots_i[:, :, 0]).then_inc(step.sem, 1)
                    dve.tensor_copy(slot_typed[:, :], slots_i[:, :, 1]).then_inc(step.sem, 1)
                    dve.tensor_copy(slot_loc[:, :], slots[:, :, 3]).then_inc(step.sem, 1)
                    dve.tensor_copy(slot_bar[:, :], slots[:, :, 4]).then_inc(step.sem, 1)
                    dve.wait_ge(multiplied.sem, multiplied.at(4))
                    dve.tensor_copy(segT, PS[0][0:q4, :].rearrange("p (q s) -> p q s", q=4)).then_inc(placed.sem, 1)
                    dve.wait_ge(step.sem, step.at(5))
                    dve.wait_ge(placed.sem, placed.at(1))
                    dve.sem_inc(placed.sem, 1)

                @block.tensor
                def _(pe):
                    pe.wait_ge(loaded.sem, loaded.at(16))
                    for q in range(4):
                        pe.transpose(PS[0][0:q4, q * P:q * P + P], slots[:, q * q4:(q + 1) * q4, 2], ident[:, :])\
                          .then_inc(multiplied.sem, 1)
            loaded.base += 16 * 7
            step.base += 5
            placed.base += 2
            multiplied.base += 4

        def find_borders():
            ends = arena[0:1, 0:2 * T].rearrange("p (k t) -> p k t", k=2)
            tb = tile_border[:, :].rearrange("p (b c) -> p b c", c=33)
            lane, late, early = small[:, 2:3], differs[:, 3744:3744 + 16], differs[:, 3760:3760 + 16]
            firsts, lasts = seg_lane[:, :, 1], seg_lane[:, :, P]
            last_of = PS[0][:, 0:T].rearrange("p (b t) -> p b t", t=BT)
            first_of = PS[1][:, 0:T].rearrange("p (b t) -> p b t", t=BT)
            with nc.Block() as block:
                @block.sync
                def _(sp):
                    seg = seg_dram.tensor
                    for h in range(H):
                        sp.dma_start(seg_lane[16 * h:16 * h + 16, :, :],
                                     bass.AP(tensor=seg, offset=0, ap=[[P, 16], [BT * P, NB], [1, P + 2]]))\
                          .then_inc(loaded.sem, 16)
                    with nc.allow_non_contiguous_dma(reason="a number for each tile, once"):
                        for k, off in ((0, P), (1, 1)):
                            sp.dma_start(ends[:, k, :], bass.AP(tensor=seg, offset=off, ap=[[T * P, 1], [P, T]]))\
                              .then_inc(loaded.sem, 16)
                    sp.wait_ge(loaded.sem, loaded.at(160))

                @block.tensor
                def _(pe):
                    pe.wait_ge(loaded.sem, loaded.at(160))
                    for k in range(2):
                        pe.matmul(PS[k][:, 0:T], ones[0:1, :], ends[:, k, :], start=True, stop=True)\
                          .then_inc(multiplied.sem, 1)

                @block.vector
                def _(dve):
                    n = 0

                    def link(op):
                        nonlocal n
                        n += 1
                        op.then_inc(step.sem, 1)
                        dve.wait_ge(step.sem, step.at(n))

                    link(dve.tensor_tensor(late, lane_mask[:, :], iota_row[:, 0:16], ALU.mult))
                    link(dve.tensor_reduce(lane, late, AX, ALU.add))
                    link(dve.tensor_scalar(late, iota_row[:, 0:16], lane, None, ALU.is_ge))
                    link(dve.tensor_scalar(early, iota_row[:, 0:16], lane, None, ALU.is_le))
                    dve.wait_ge(loaded.sem, loaded.at(160))
                    dif = differs[:, 0:NB * (P + 1)].rearrange("p (b s) -> p b s", b=NB)
                    link(dve.tensor_tensor(dif, seg_lane[:, :, 1:P + 2], seg_lane[:, :, 0:P + 1], ALU.not_equal))
                    link(dve.tensor_scalar(border[:, :], differs[:, 0:NB * (P + 1)], -BIG, None, ALU.mult))
                    dve.wait_ge(multiplied.sem, multiplied.at(2))
                    across = [P, NB, BT]
                    link(dve.tensor_tensor(tb[:, :, 0:16], last_of, firsts.unsqueeze(2).to_broadcast(across),
                                           ALU.not_equal))
                    link(dve.tensor_tensor(tb[:, :, 0:16], tb[:, :, 0:16], late.unsqueeze(1).to_broadcast(across),
                                           ALU.max))
                    link(dve.tensor_tensor(tb[:, :, 17:33], first_of, lasts.unsqueeze(2).to_broadcast(across),
                                           ALU.not_equal))
                    link(dve.tensor_tensor(tb[:, :, 17:33], tb[:, :, 17:33], early.unsqueeze(1).to_broadcast(across),
                                           ALU.max))
                    link(dve.memset(tb[:, 0:1, 16:17], 1.0))
                    link(dve.tensor_tensor(tb[:, 1:NB, 16], last_of[:, 0:NB - 1, BT - 1], firsts[:, 1:NB],
                                           ALU.not_equal))
                    link(dve.tensor_scalar(tile_border[:, :], tile_border[:, :], -BIG, None, ALU.mult))
                    loc, same = differs[:, 0:NB], differs[:, 32:32 + NB]
                    link(dve.tensor_scalar(loc, block_f[:, 0:(NB - 1) * BG + 1:BG], -float(P), None, ALU.mult))
                    link(dve.tensor_tensor(loc, first_of[:, :, 0], loc, ALU.add))
                    link(dve.tensor_scalar(loc, loc, small[:, 0:1], None, ALU.is_equal))
                    link(dve.tensor_copy(differs[:, 64:64 + NB], last_of[:, :, BT - 1]))
                    link(dve.memset(same, 0.0))
                    link(dve.tensor_tensor(same[:, 1:NB], first_of[:, 1:NB, 0], differs[:, 64:64 + NB - 1],
                                           ALU.is_equal))
                    link(dve.tensor_tensor(straddle[:, :], loc, same, ALU.mult))
                    marks["step"] = n
            loaded.base += 160
            multiplied.base += 2
            step.base += marks["step"]

        rows_sb = arena[:, 0:QTAB].rearrange("p (a t c) -> p a t c", a=2, t=BT)
        TAIL = QTAB + NT * D
        weighted = arena[:, TAIL:TAIL + 4 * 272].rearrange("p (a t c) -> p a t c", a=2, t=GT)
        seg_a, seg_b, shifted, powers, final_max, logits = [arena[:, TAIL + 1088 + P * i:TAIL + 1088 + P * i + P]
                                                    for i in range(6)]
        onehots = sb("onehots", [P, 2, BT, P])
        spreads = sb("spreads", [P, 2, GT * P])
        raw = sb("raw", [P, 2, BT * H])
        bars = sb("bars", [P, P + 1])
        seg_max = sb("seg_max", [P, 2, P])
        spread_cols = sb("spread_cols", [P, 33])
        carried = sb("carried", [P, 33])
        carry = sb("carry", [P, 4])
        head_rhs = sb("head_rhs", [P, H])
        rescale = sb("rescale", [P, 2 * H])
        att = sb("att", [P, 2 * D])
        idx = sb("idx", [P, 2, BT], I32)

        names = ("oh_made", "oh_turned", "spread_made", "target_spread", "activated", "leaked", "multiplied_rows", "raw_made",
                 "logits_made", "logits_turned", "mid", "cols_made", "cols_spread", "shifted_made", "powers_made",
                 "powers_turned", "powers_kept", "scale_rhs", "scale_spread", "scale_in", "scale_made", "weighted_made",
                 "denominator_made", "summed", "added_up", "idx_made", "distance", "rescaled")
        S = {n: sig(n) for n in names}
        arrived = [[sig(f"arrived{a}{k}") for k in range(BG)] for a in range(2)]

        def edge_pass(kind, table, width):
            gin, gatv2, gat, hgt = (kind == k for k in ("gin", "gatv2", "gat", "hgt"))
            cw = {"gatv2": width, "gat": H, "hgt": D, "gin": 0}[kind]
            C = width // H if gatv2 else D // H
            v0 = D if hgt else 0
            wc = D if gin else H * (C + (2 if gat else 1))
            loc = slot_loc
            index = slot_typed if hgt else slot_src
            pot = [PS[0][:, 0:GT * P], PS[1][:, 0:GT * P]]
            z = [PS[2][:, :].rearrange("p (t c) -> p t c", t=GT), PS[3][:, :].rearrange("p (t c) -> p t c", t=GT)]
            sums = [PS[4][:, 0:wc], PS[5][:, 0:wc]]
            plt, pcols, pscale = PS[6][:, 0:P], PS[6][:, P:P + 33], PS[6][:, 192:192 + H]
            pat = PS[7][:, 0:P].rearrange("p (h t) -> p h t", h=H)
            powers_sb = stats[:, 0:P].rearrange("p (h t) -> p h t", h=H)
            max_sb = stats[:, P:2 * P].rearrange("p (h t) -> p h t", h=H)
            oh_dve = gatv2 or gin
            w_dve = gat or hgt

            def one_hots(dve, x):
                if needed(x.g - 2 * BG + 1):
                    dve.wait_ge(S["summed"].sem, S["summed"].at(x.g - 2 * BG + 1))
                for t in (GT * x.k, GT * x.k + 1):
                    op = dve.tensor_scalar(onehots[:, x.a, t, :], iota_row[:, :], loc[:, ds(BT * x.batch + t, 1)],
                                           None, ALU.is_equal)
                op.then_inc(S["oh_made"].sem, 1)

            def one_hots_act(act, x):
                if needed(x.g - 2 * BG + 1):
                    act.wait_ge(S["summed"].sem, S["summed"].at(x.g - 2 * BG + 1))
                for t in (GT * x.k, GT * x.k + 1):
                    act.activation(onehots[:, x.a, t, :], iota_row[:, :], ACT.Abs, scale=-1.0,
                                   bias=loc[:, ds(BT * x.batch + t, 1)]).then_inc(S["distance"].sem, 1)
                act.wait_ge(S["distance"].sem, S["distance"].at(2 * x.g + 2))
                both = onehots[:, x.a, GT * x.k:GT * x.k + GT, :]
                act.activation(both, both, ACT.Relu, scale=-1.0, bias=1.0).then_inc(S["oh_made"].sem, 1)

            def lane_split(ap, c):
                return ap.rearrange("p t (h c) -> p t h c", c=c)

            def next_blocks(engine, shifted_by, col):
                return nc.values_load_multi_w_load_instructions(
                    block_of[0:1, shifted_by, ds(col, BG)], engines=[engine], min_val=0, max_val=NT - 1,
                    skip_runtime_bounds_check_because="place_nodes counts blocks: the values are 0 to NT - 1")[1]

            class Group:

                def __init__(self, i, w, lag):
                    ahead, self.k = (w - lag) // BG, (w - lag) % BG
                    self.a = ahead % 2
                    self.batch, self.use = 2 * i + ahead, i + (ahead - self.a) // 2
                    self.g = 2 * BG * i + w - lag
                    self.there = not isinstance(i, int) or 0 <= self.g < NB * BG

            def at_batch(i, w, lag):
                x = Group(i, w, lag)
                return x if x.there and x.k == 0 else None

            LAG = dict(one_hots=0, turn=1, target=2, logit=3, weigh=14, add_up=15, keep=16)
            if gin:
                LAG.update(add_up=7, keep=8)
            LOGITS, TURN_LOGITS, IN_TILE, ACROSS, POWERS = 10, 11, 11, 12, 13
            FULL = NB * BG // (2 * BG)
            SLOTS = NB * BG + LAG["keep"]
            G16 = 2 * BG

            with nc.Block() as block:
                def slots(eng, slot_fn):
                    for i in range(2):
                        for w in range(G16):
                            slot_fn(i, w)
                    with eng.Fori(2, FULL) as i:
                        for w in range(G16):
                            slot_fn(i, w)
                    for q in range(FULL * G16, SLOTS):
                        slot_fn(q // G16, q % G16)

                def batches(eng, batch_fn):
                    batch_fn(0, 0, 0)
                    batch_fn(1, 1, 0)
                    with eng.Fori(1, (NB - 1) // 2) as i:
                        batch_fn(2 * i, 0, i)
                        batch_fn(2 * i + 1, 1, i)
                    batch_fn(NB - 1, 0, (NB - 1) // 2)

                @block.gpsimd
                def _(pool):
                    freed = S["summed"] if gin else S["weighted_made"]

                    def batch_fn(s, a, use):
                        for k in range(BG):
                            if needed(32 * use):
                                pool.wait_ge(arrived[a][k].sem, arrived[a][k].at(32 * use))
                                pool.sem_inc(tick.sem, 1)
                        pool.tensor_copy(idx[:, a, :], index[:, ds(BT * s, BT)]).then_inc(S["idx_made"].sem, 1)
                        if needed(s + 1):
                            pool.wait_ge(S["idx_made"].sem, S["idx_made"].at(s + 1))
                            pool.sem_inc(tick.sem, 1)
                        for k in range(BG):
                            if needed(BG * (s - 2) + k + 1):
                                pool.wait_ge(freed.sem, freed.at(BG * (s - 2) + k + 1))
                                pool.sem_inc(tick.sem, 1)
                            if not gin:
                                if needed(BG * (s - 2) + k + 1):
                                    pool.wait_ge(S["raw_made"].sem, S["raw_made"].at(BG * (s - 2) + k + 1))
                                    pool.sem_inc(tick.sem, 1)
                            for t in (GT * k, GT * k + 1):
                                pool.indirect_dma_start(
                                    out=rows_sb[:, a, t, 0:width], out_offset=None, in_=table[:, :],
                                    in_offset=bass.IndirectOffsetOnAxis(ap=idx[:, a, t:t + 1], axis=0),
                                    bounds_check=table.shape[0] - 1, oob_is_err=False)\
                                    .then_inc(arrived[a][k].sem, 16)

                    batches(pool, batch_fn)

                @block.tensor
                def _(pe):
                    block_no = None

                    def slot_fn(i, w):
                        nonlocal block_no
                        x = at_batch(i, w, TURN_LOGITS)
                        if x and not gin:
                            pe.wait_ge(S["logits_made"].sem, S["logits_made"].at(x.batch + 1))
                            if needed(x.batch):
                                pe.wait_ge(S["scale_in"].sem, S["scale_in"].at(x.batch))
                            pe.transpose(plt, logits[:, :], ident[:, :]).then_inc(S["logits_turned"].sem, 1)
                        x = Group(i, w, LAG["turn"])
                        if x.there and not gin:
                            pe.wait_ge(S["oh_made"].sem, S["oh_made"].at(x.g + 1))
                            if needed(x.g - 1):
                                pe.wait_ge(S["spread_made"].sem, S["spread_made"].at(x.g - 1))
                            pe.transpose(pot[x.k % 2][:, 0:P], onehots[:, x.a, GT * x.k, :], ident[:, :])
                            pe.transpose(pot[x.k % 2][:, P:2 * P], onehots[:, x.a, GT * x.k + 1, :], ident[:, :])\
                              .then_inc(S["oh_turned"].sem, 1)
                        if w % BG == 0 and not gin and not (isinstance(i, int) and G16 * i + w >= NB * BG + 2):
                            block_no = next_blocks(mybir.EngineType.PE, 1, G16 * i + w)
                        x = Group(i, w, LAG["target"])
                        if x.there and not gin:
                            pe.wait_ge(S["spread_made"].sem, S["spread_made"].at(x.g + 1))
                            if needed(x.g - 1):
                                pe.wait_ge(S["raw_made"].sem, S["raw_made"].at(x.g - 1))
                            if gatv2:
                                pe.wait_ge(arrived[x.a][x.k].sem, arrived[x.a][x.k].at(32 * (x.use + 1)))
                            for t in range(GT):
                                mm = pe.matmul(z[x.k % 2][:, t, 0:cw], spreads[:, x.k % 2, t * P:t * P + P],
                                               qtab[:, block_no[w % BG], 0:cw], start=True, stop=not gatv2)
                                if gatv2:
                                    mm = pe.matmul(z[x.k % 2][:, t, 0:cw], ident[:, :],
                                                   rows_sb[:, x.a, GT * x.k + t, 0:cw], start=False, stop=True)
                            mm.then_inc(S["target_spread"].sem, 1)
                        x = at_batch(i, w, ACROSS)
                        if x and not gin:
                            pe.wait_ge(S["cols_made"].sem, S["cols_made"].at(x.batch + 1))
                            pe.matmul(pcols, same_head[:, :], spread_cols[:, :], start=True, stop=True)\
                              .then_inc(S["cols_spread"].sem, 1)
                        x = at_batch(i, w, POWERS)
                        if x and not gin:
                            pe.wait_ge(S["scale_rhs"].sem, S["scale_rhs"].at(x.batch + 1))
                            pe.matmul(pscale, ones[:, :], head_rhs[:, :], start=True, stop=True)\
                              .then_inc(S["scale_spread"].sem, 1)
                            pe.wait_ge(S["powers_made"].sem, S["powers_made"].at(x.batch + 1))
                            if gatv2:
                                if needed(x.batch):
                                    pe.wait_ge(S["powers_kept"].sem, S["powers_kept"].at(x.batch))
                            else:
                                if needed(BG * x.batch):
                                    pe.wait_ge(S["weighted_made"].sem, S["weighted_made"].at(BG * x.batch))
                            if gat:
                                pe.transpose(PS[7][:, P:2 * P], final_max[:, :], ident[:, :])
                            pe.transpose(PS[7][:, 0:P], powers[:, :], ident[:, :])\
                              .then_inc(S["powers_turned"].sem, 1)
                        x = Group(i, w, LAG["add_up"])
                        if x.there:
                            if gin:
                                pe.wait_ge(S["oh_made"].sem, S["oh_made"].at(x.g + 1))
                                pe.wait_ge(arrived[x.a][x.k].sem, arrived[x.a][x.k].at(32 * (x.use + 1)))
                            else:
                                pe.wait_ge(S["weighted_made"].sem, S["weighted_made"].at(x.g + 1))
                                pe.wait_ge(S["denominator_made"].sem, S["denominator_made"].at(x.g + 1))
                            if needed(x.g - 1):
                                pe.wait_ge(S["added_up"].sem, S["added_up"].at(x.g - 1))
                            for t in range(GT):
                                rhs = rows_sb[:, x.a, GT * x.k + t, 0:wc] if gin else weighted[:, x.k % 2, t, 0:wc]
                                mm = pe.matmul(sums[x.k % 2], onehots[:, x.a, GT * x.k + t, :], rhs,
                                               start=t == 0, stop=t == GT - 1)
                            mm.then_inc(S["summed"].sem, 1)

                    slots(pe, slot_fn)

                @block.scalar
                def _(act):
                    def slot_fn(i, w):
                        x = Group(i, w, LAG["turn"])
                        if x.there:
                            act.wait_ge(S["oh_turned"].sem, S["oh_turned"].at(x.g + 1))
                            if needed(x.g - 1):
                                act.wait_ge(S["target_spread"].sem, S["target_spread"].at(x.g - 1))
                            act.activation(spreads[:, x.k % 2, :], pot[x.k % 2], ACT.Copy)\
                               .then_inc(S["spread_made"].sem, 1)
                        x = Group(i, w, LAG["target"])
                        if x.there and gatv2:
                            act.wait_ge(S["target_spread"].sem, S["target_spread"].at(x.g + 1))
                            act.activation(rows_sb[:, x.a, GT * x.k:GT * x.k + GT, D:D + cw], z[x.k % 2][:, :, 0:cw],
                                           ACT.Copy, scale=0.2)\
                               .then_inc(S["activated"].sem, 1)
                        x = Group(i, w, LAG["one_hots"])
                        if x.there and not oh_dve:
                            one_hots_act(act, x)
                        x = at_batch(i, w, ACROSS)
                        if x:
                            act.wait_ge(S["shifted_made"].sem, S["shifted_made"].at(x.batch + 1))
                            if needed(x.batch):
                                act.wait_ge(S["powers_turned"].sem, S["powers_turned"].at(x.batch))
                            act.activation(powers[:, :], shifted[:, :], ACT.Exp).then_inc(S["powers_made"].sem, 1)
                        x = at_batch(i, w, LAG["weigh"])
                        if x:
                            act.wait_ge(S["powers_turned"].sem, S["powers_turned"].at(x.batch + 1))
                            if needed(BG * x.batch):
                                act.wait_ge(S["denominator_made"].sem, S["denominator_made"].at(BG * x.batch))
                            act.activation(stats[:, 0:(2 if gat else 1) * P], PS[7][:, 0:(2 if gat else 1) * P],
                                           ACT.Copy).then_inc(S["powers_kept"].sem, 1)
                            act.wait_ge(S["powers_kept"].sem, S["powers_kept"].at(x.batch + 1))
                        x = Group(i, w, LAG["weigh"])
                        if x.there:
                            if needed(x.g - 1):
                                act.wait_ge(S["summed"].sem, S["summed"].at(x.g - 1))
                            wt = lane_split(weighted[:, x.k % 2, :, 0:wc], wc // H)
                            if gat:
                                act.activation(wt[:, :, :, C + 1],
                                               max_sb[:, :, GT * x.k:GT * x.k + GT].rearrange("p h t -> p t h"),
                                               ACT.Copy).then_inc(kept.sem, 1)
                            if gatv2:
                                act.wait_ge(arrived[x.a][x.k].sem, arrived[x.a][x.k].at(32 * (x.use + 1)))
                                for t in range(GT):
                                    for h in range(2):
                                        lanes = slice(h * H // 2, (h + 1) * H // 2)
                                        op = act.activation(
                                            wt[:, t, lanes, 0:C],
                                            rows_sb[:, x.a, GT * x.k + t, h * cw // 2:(h + 1) * cw // 2]
                                            .rearrange("p (r c) -> p r c", r=H // 2),
                                            ACT.Copy, scale=powers_sb[:, h * H // 2, GT * x.k + t:GT * x.k + t + 1])
                                op.then_inc(S["weighted_made"].sem, 1)
                            act.activation(wt[:, :, :, C],
                                           powers_sb[:, :, GT * x.k:GT * x.k + GT].rearrange("p h t -> p t h"),
                                           ACT.Copy).then_inc(S["denominator_made"].sem, 1)
                        x = at_batch(i, w, LAG["weigh"])
                        if x:
                            act.wait_ge(S["scale_in"].sem, S["scale_in"].at(x.batch + 1))
                            if needed(x.batch):
                                act.wait_ge(S["rescaled"].sem, S["rescaled"].at(x.batch))
                            act.activation(rescale[:, H:2 * H], rescale[:, 0:H], ACT.Exp)\
                               .then_inc(S["scale_made"].sem, 1)

                    if not gin:
                        slots(act, slot_fn)

                @block.vector
                def _(dve):
                    dve.memset(acc[:, :, :], 0.0).then_inc(step.sem, 1)
                    dve.memset(seg_max[:, :, :], 0.0).then_inc(step.sem, 1)
                    dve.wait_ge(step.sem, step.at(2))
                    block_no = None

                    def weigh(x):
                        dve.wait_ge(S["powers_kept"].sem, S["powers_kept"].at(x.batch + 1))
                        if needed(x.g - 1):
                            dve.wait_ge(S["summed"].sem, S["summed"].at(x.g - 1))
                        wt = lane_split(weighted[:, x.k % 2, :, 0:wc], wc // H)
                        src = rows_sb[:, x.a, GT * x.k:GT * x.k + GT, v0:v0 + H * C]
                        p = pat[:, :, GT * x.k:GT * x.k + GT].rearrange("p h t -> p t h")
                        dve.tensor_tensor(wt[:, :, :, 0:C], lane_split(src, C),
                                          p.unsqueeze(3).to_broadcast([P, GT, H, C]), ALU.mult)\
                           .then_inc(S["weighted_made"].sem, 1)

                    def slot_fn(i, w):
                        nonlocal block_no
                        linked = 0
                        x = Group(i, w, LAG["one_hots"])
                        if x.there and oh_dve:
                            one_hots(dve, x)
                        xl = Group(i, w, LAG["logit"])
                        pr = z[xl.k % 2][:, :, 0:cw]
                        src = rows_sb[:, xl.a, GT * xl.k:GT * xl.k + GT, :]
                        if xl.there and gatv2:
                            dve.wait_ge(S["activated"].sem, S["activated"].at(xl.g + 1))
                            dve.tensor_tensor(pr, pr, src[:, :, D:D + cw], ALU.max).then_inc(S["leaked"].sem, 1)
                        elif xl.there and not gin:
                            dve.wait_ge(S["target_spread"].sem, S["target_spread"].at(xl.g + 1))
                            dve.wait_ge(arrived[xl.a][xl.k].sem, arrived[xl.a][xl.k].at(32 * (xl.use + 1)))
                        if xl.there and hgt:
                            dve.tensor_tensor(pr, pr, src[:, :, 0:D], ALU.mult).then_inc(S["multiplied_rows"].sem, 1)
                        xw = Group(i, w, LAG["weigh"])
                        if xw.there and w_dve and xw.k > 0:
                            weigh(xw)

                        def link(op):
                            nonlocal linked
                            linked += 1
                            op.then_inc(S["mid"].sem, 1)
                            dve.wait_ge(S["mid"].sem, S["mid"].at(MID * x.batch + linked))

                        x = at_batch(i, w, IN_TILE)
                        if x and not gin:
                            linked = 1
                            if needed(MID * x.batch + 1):
                                dve.wait_ge(S["mid"].sem, S["mid"].at(MID * x.batch + 1))
                            dve.wait_ge(S["logits_turned"].sem, S["logits_turned"].at(x.batch + 1))
                            link(dve.tensor_tensor_scan(seg_a[:, :], bars[:, 0:P], plt, -BIG, ALU.add, ALU.max))
                            link(dve.tensor_tensor_scan(seg_b[:, ::-1], bars[:, P:0:-1], seg_a[:, ::-1], -BIG,
                                                        ALU.add, ALU.max))
                            dve.tensor_scalar(spread_cols[:, 0:16], lane_mask[:, :], seg_b[:, P - 1:P], None, ALU.mult)
                            dve.tensor_scalar(spread_cols[:, 16:17], lane_mask[:, 15:16], seg_max[:, 1 - x.a, P - 1:P],
                                              None, ALU.mult)
                            dve.tensor_scalar(spread_cols[:, 17:33], lane_mask[:, :], seg_b[:, 0:1], None, ALU.mult)\
                               .then_inc(S["cols_made"].sem, 1)
                        x = at_batch(i, w, ACROSS)
                        if x and not gin:
                            linked = 3
                            dve.wait_ge(S["cols_spread"].sem, S["cols_spread"].at(x.batch + 1))
                            link(dve.tensor_tensor(carried[:, :], pcols, tile_border[:, ds(33 * x.batch, 33)],
                                                   ALU.add))
                            dve.tensor_reduce(carry[:, 0:1], carried[:, 0:17], AX, ALU.max)
                            link(dve.tensor_reduce(carry[:, 1:2], carried[:, 17:33], AX, ALU.max))
                            link(dve.tensor_tensor_scan(seg_a[:, :], bars[:, 0:P], seg_b[:, :], carry[:, 0:1],
                                                        ALU.add, ALU.max))
                            link(dve.tensor_tensor_scan(seg_max[:, x.a, ::-1], bars[:, P:0:-1], seg_a[:, ::-1],
                                                        carry[:, 1:2], ALU.add, ALU.max))
                            if needed(x.batch):
                                dve.wait_ge(S["powers_made"].sem, S["powers_made"].at(x.batch))
                            if gat:
                                if needed(x.batch):
                                    dve.wait_ge(S["powers_turned"].sem, S["powers_turned"].at(x.batch))
                                dve.scalar_tensor_tensor(final_max[:, :], bars[:, 1:P + 1], -1.0 / BIG,
                                                         seg_max[:, x.a, :], ALU.mult, ALU.mult)
                            dve.tensor_tensor(shifted[:, :], plt, seg_max[:, x.a, :], ALU.subtract)\
                               .then_inc(S["shifted_made"].sem, 1)
                        r = raw[:, xl.a, 0:BT * (2 if gatv2 else H)].rearrange("p (t h) -> p t h", t=BT)
                        r = r[:, GT * xl.k:GT * xl.k + GT, :]
                        if xl.there and gatv2:
                            dve.wait_ge(S["leaked"].sem, S["leaked"].at(xl.g + 1))
                            for t in range(GT):
                                for h in range(2):
                                    ch = slice(cw // 2 * h, cw // 2 * h + cw // 2)
                                    op = dve.tensor_tensor_reduce(
                                        out=z[xl.k % 2][:, t, ch], in0=z[xl.k % 2][:, t, ch], in1=att[:, ch],
                                        scale=1.0, scalar=0.0, op0=ALU.mult, op1=ALU.add,
                                        accum_out=r[:, t, h:h + 1])
                            op.then_inc(S["raw_made"].sem, 1)
                        elif xl.there and gat:
                            dve.tensor_tensor(r, pr, src[:, :, D:D + H], ALU.add).then_inc(S["raw_made"].sem, 1)
                        elif xl.there and hgt:
                            dve.wait_ge(S["multiplied_rows"].sem, S["multiplied_rows"].at(xl.g + 1))
                            dve.tensor_reduce(r, lane_split(pr, C), AX, ALU.add).then_inc(S["raw_made"].sem, 1)
                        if w % BG == 0 and not (isinstance(i, int) and G16 * i + w < LAG["keep"]):
                            block_no = next_blocks(mybir.EngineType.DVE, 0, G16 * i + w - LAG["keep"])
                        x = Group(i, w, LAG["keep"])
                        if x.there:
                            if needed(x.g):
                                dve.wait_ge(S["added_up"].sem, S["added_up"].at(x.g))
                            av = acc[:, block_no[x.k], 0:wc]
                            if x.k == 0 and not gin:
                                dve.wait_ge(S["scale_made"].sem, S["scale_made"].at(x.batch + 1))
                                dve.tensor_tensor(av.rearrange("p (h c) -> p h c", h=H),
                                                  av.rearrange("p (h c) -> p h c", h=H),
                                                  rescale[:, H:2 * H].unsqueeze(2).to_broadcast([P, H, wc // H]),
                                                  ALU.mult).then_inc(S["rescaled"].sem, 1)
                                dve.wait_ge(S["rescaled"].sem, S["rescaled"].at(x.batch + 1))
                            dve.wait_ge(S["summed"].sem, S["summed"].at(x.g + 1))
                            dve.tensor_tensor(av, av, sums[x.k % 2], ALU.add).then_inc(S["added_up"].sem, 1)
                        if xw.there and w_dve and xw.k == 0:
                            weigh(xw)
                        x = at_batch(i, w, ACROSS)
                        if x and not gin:
                            linked = 7
                            link(dve.tensor_scalar(carry[:, 2:3], seg_max[:, x.a, 0:1], lane_mask[:, 0:1], None,
                                                   ALU.mult))
                            link(dve.scalar_tensor_tensor(carry[:, 3:4], seg_max[:, 1 - x.a, P - 1:P],
                                                          lane_mask[:, 15:16], carry[:, 2:3], ALU.mult,
                                                          ALU.subtract))
                            if needed(x.batch):
                                dve.wait_ge(S["scale_spread"].sem, S["scale_spread"].at(x.batch))
                            dve.tensor_scalar(head_rhs[:, :], head_col[:, :], carry[:, 3:4], None, ALU.mult)\
                               .then_inc(S["scale_rhs"].sem, 1)
                        x = at_batch(i, w, POWERS)
                        if x and not gin:
                            dve.wait_ge(S["scale_spread"].sem, S["scale_spread"].at(x.batch + 1))
                            if needed(x.batch):
                                dve.wait_ge(S["scale_made"].sem, S["scale_made"].at(x.batch))
                            dve.tensor_scalar(rescale[:, 0:H], pscale, straddle[:, ds(x.batch, 1)], None, ALU.mult)\
                               .then_inc(S["scale_in"].sem, 1)
                        x = at_batch(i, w, LOGITS)
                        if x and not gin:
                            if needed(BG * x.batch + BG):
                                dve.wait_ge(S["raw_made"].sem, S["raw_made"].at(BG * x.batch + BG))
                            if needed(x.batch):
                                dve.wait_ge(S["logits_turned"].sem, S["logits_turned"].at(x.batch))
                            out_l = logits[:, :].rearrange("p (h t) -> p h t", h=H)
                            if gatv2:
                                r = raw[:, x.a, 0:2 * BT].rearrange("p (t h) -> p h t", t=BT)
                                op = dve.tensor_copy(logits[:, :].rearrange("p (h r t) -> p h r t", h=2, r=H // 2),
                                                     r.unsqueeze(2).to_broadcast([P, 2, H // 2, BT]))
                            else:
                                r = raw[:, x.a, :].rearrange("p (t h) -> p h t", t=BT)
                                if gat:
                                    op = dve.scalar_tensor_tensor(out_l, r, 0.2, r, ALU.mult, ALU.max)
                                else:
                                    op = dve.tensor_tensor(out_l, r, slot_bar[:, ds(BT * x.batch, BT)].unsqueeze(1)
                                                           .to_broadcast([P, H, BT]), ALU.add)
                            op.then_inc(S["logits_made"].sem, 1)
                            if needed(x.batch):
                                dve.wait_ge(S["scale_in"].sem, S["scale_in"].at(x.batch))
                            dve.tensor_copy(bars[:, :], border[:, ds((P + 1) * x.batch, P + 1)])\
                               .then_inc(S["mid"].sem, 1)

                    MID = 9
                    slots(dve, slot_fn)
                    step.base += 2
            G = NB * BG
            per_group = ("oh_made", "summed", "added_up")
            if not gin:
                per_group += ("oh_turned", "spread_made", "target_spread", "raw_made", "weighted_made",
                              "denominator_made")
                for n in ("logits_made", "logits_turned", "cols_made", "cols_spread", "shifted_made", "powers_made",
                          "rescaled", "powers_turned", "powers_kept", "scale_rhs", "scale_spread", "scale_in", "scale_made"):
                    S[n].base += NB
                S["mid"].base += NB * 9
            if gatv2:
                per_group += ("activated", "leaked")
            if hgt:
                per_group += ("multiplied_rows",)
            if gat or hgt:
                S["distance"].base += 2 * G
            for n in per_group:
                S[n].base += G
            S["idx_made"].base += NB
            if gat:
                kept.base += G
            for a in range(2):
                for k in range(BG):
                    arrived[a][k].base += 32 * ((NB + 1 - a) // 2)

        hbuf = arena[:, 4096:4096 + NT * D].rearrange("p (j c) -> p j c", j=NT)
        stage = arena[:, 10496:10496 + 2 * 3 * 512].rearrange("p (a c) -> p a c", a=2)
        xin = arena[:, 13568:13568 + 2 * D].rearrange("p (a c) -> p a c", a=2)
        tmp = arena[:, 14080:14080 + 2 * D].rearrange("p (a c) -> p a c", a=2)
        vecs = sb("vecs", [P, 4 * D])
        cols = sb("cols", [P, 32])
        stats = sb("stats", [P, 256])
        ln = sb("ln", [P, 6 * NT])
        flat = "p j c -> p (j c)"

        D_ = {n: sig("d_" + n) for n in ("in", "turned", "turned_sb", "product", "act_out", "dve_out", "tmp",
                                         "hidden", "hidden_sb", "biased", "stats", "normed", "keys", "keys_sb", "typed", "values")}
        stored = [sig("stored0"), sig("stored1")]
        straight = sig("straight")

        def sweep(eng, *stages):
            def one(s, a):
                for k, f in enumerate(stages):
                    if f is not None and not (isinstance(s, int) and not 0 <= s - k < NT):
                        f(s - k, (a - k) % 2)

            for s in range(6):
                one(s, s % 2)
            with eng.Fori(3, NT // 2) as i:
                one(2 * i, 0)
                one(2 * i + 1, 1)
            for s in range(NT - 1, NT - 1 + len(stages)):
                one(s, s % 2)

        def load(*pairs):
            with nc.Block() as block:
                @block.sync
                def _(sp):
                    with nc.allow_non_contiguous_dma(reason="small weights, once"):
                        for dst, src in pairs[0::2]:
                            sp.dma_start(dst, src).then_inc(loaded.sem, 16)
                    sp.wait_ge(loaded.sem, loaded.at(16 * len(pairs)))

                @block.scalar
                def _(act):
                    with nc.allow_non_contiguous_dma(reason="small weights, once"):
                        for dst, src in pairs[1::2]:
                            act.dma_start(dst, src).then_inc(loaded.sem, 16)
            loaded.base += 16 * len(pairs)

        def vector_phase(f):
            with nc.Block() as block:
                @block.vector
                def _(dve):
                    n = 0

                    def link(op):
                        nonlocal n
                        n += 1
                        op.then_inc(step.sem, 1)
                        dve.wait_ge(step.sem, step.at(n))

                    f(dve, link)
                    marks["step"] = n
            step.base += marks["step"]

        def scalar_phase(*calls):
            with nc.Block() as block:
                @block.scalar
                def _(act):
                    for out_, in_, func in calls:
                        act.activation(out_, in_, func).then_inc(straight.sem, 1)
            straight.base += len(calls)

        def row(ap):
            return bass.AP(tensor=ap.tensor, offset=ap.offset, ap=[[0, P], [1, ap.shape[-1]]])

        def over_blocks(v):
            return v.unsqueeze(1).to_broadcast([P, NT, D])

        def block_stats(dve, j):
            return dve.bn_stats(out=stats[:, 0:6 * NT].rearrange("p (j f) -> p j f", f=6)[:, j, :], in_=X[:, j, :])

        def layer_norm(gain=None, bias=None, stats_made=False, apply=True):
            st = stats[:, 0:6 * NT].rearrange("p (j f) -> p j f", f=6)
            mean, var, rs, nm, t1, t2 = [ln[:, i * NT:(i + 1) * NT] for i in range(6)]

            def first(dve, link):
                if not stats_made:
                    for j in range(NT):
                        block_stats(dve, j).then_inc(kept.sem, 1)
                    dve.wait_ge(kept.sem, kept.at(NT))
                    kept.base += NT
                link(dve.tensor_tensor(t1, st[:, :, 1], st[:, :, 4], ALU.add))
                link(dve.tensor_scalar(mean, t1, 0.5, None, ALU.mult))
                link(dve.tensor_tensor(t1, st[:, :, 1], st[:, :, 4], ALU.subtract))
                link(dve.tensor_scalar(t1, t1, 0.5, None, ALU.mult))
                link(dve.tensor_tensor(t1, t1, t1, ALU.mult))
                link(dve.tensor_tensor(t2, st[:, :, 2], st[:, :, 5], ALU.add))
                link(dve.tensor_scalar(t2, t2, 1.0 / D, 1e-5, ALU.mult, ALU.add))
                link(dve.tensor_tensor(var, t1, t2, ALU.add))

            def second(dve, link):
                link(dve.reciprocal(rs, t1))
                link(dve.scalar_tensor_tensor(nm, mean, -1.0, rs, ALU.mult, ALU.mult))
                if not apply:
                    return
                for j in range(NT):
                    dve.tensor_scalar(X[:, j, :], X[:, j, :], rs[:, j:j + 1], nm[:, j:j + 1],
                                      ALU.mult, ALU.add).then_inc(kept.sem, 1)
                dve.wait_ge(kept.sem, kept.at(NT))
                kept.base += NT
                if gain is not None:
                    link(dve.tensor_tensor(X[:, :, :], X[:, :, :], over_blocks(gain), ALU.mult))
                    link(dve.tensor_tensor(X[:, :, :], X[:, :, :], over_blocks(bias), ALU.add))

            vector_phase(first)
            scalar_phase((t1, var, ACT.Sqrt))
            vector_phase(second)

        def project(src, kb, rhs, n, act_out=None, dve_out=None, dve_ops=1, table=None, width=0, bias=None):
            turned = [PS[0][:, 0:kb * P], PS[1][:, 0:kb * P]]
            xT = spreads
            prod = [PS[2][:, 0:n], PS[3][:, 0:n]]
            with nc.Block() as block:
                @block.vector
                def _(dve):
                    def take(j, a):
                        if needed(j - 1):
                            dve.wait_ge(D_["turned"].sem, D_["turned"].at(j - 1))
                        dve.tensor_copy(xin[:, a, 0:kb * P], src(j)).then_inc(D_["in"].sem, 1)

                    def give(j, a):
                        dve.wait_ge(D_["product"].sem, D_["product"].at(j + 1))
                        if act_out:
                            dve.wait_ge(D_["act_out"].sem, D_["act_out"].at(j + 1))
                        if table is not None:
                            wait_stored(dve, j, a)
                        if bias is not None:
                            dve.wait_ge(D_["biased"].sem, D_["biased"].at(j + 1))
                        dve_out(dve, j, a, prod[a])

                    def add_bias(j, a):
                        dve.tensor_tensor(X[:, j, :], X[:, j, :], bias, ALU.add).then_inc(D_["biased"].sem, 1)

                    def take_stats(j, a):
                        dve.wait_ge(D_["dve_out"].sem, D_["dve_out"].at(j + 1))
                        block_stats(dve, j).then_inc(D_["stats"].sem, 1)

                    if bias is None:
                        sweep(dve, take, None, give if dve_out else None)
                    else:
                        sweep(dve, take, add_bias, give, take_stats)
                        dve.wait_ge(D_["stats"].sem, D_["stats"].at(NT))

                @block.tensor
                def _(pe):
                    def turn(j, a):
                        pe.wait_ge(D_["in"].sem, D_["in"].at(j + 1))
                        if needed(j - 1):
                            pe.wait_ge(D_["turned_sb"].sem, D_["turned_sb"].at(j - 1))
                        for k in range(kb):
                            op = pe.transpose(turned[a][:, k * P:k * P + P], xin[:, a, k * P:k * P + P], ident[:, :])
                        op.then_inc(D_["turned"].sem, 1)

                    def multiply(j, a):
                        pe.wait_ge(D_["turned_sb"].sem, D_["turned_sb"].at(j + 1))
                        if act_out:
                            if needed(j - 1):
                                pe.wait_ge(D_["act_out"].sem, D_["act_out"].at(j - 1))
                        if dve_out:
                            if needed(dve_ops * (j - 1)):
                                pe.wait_ge(D_["dve_out"].sem, D_["dve_out"].at(dve_ops * (j - 1)))
                        for k in range(kb):
                            op = pe.matmul(prod[a], xT[:, a, k * P:k * P + P], rhs[:, k, 0:n], start=k == 0,
                                           stop=k == kb - 1)
                        op.then_inc(D_["product"].sem, 1)

                    sweep(pe, turn, multiply)

                @block.scalar
                def _(act):
                    def turn(j, a):
                        act.wait_ge(D_["turned"].sem, D_["turned"].at(j + 1))
                        if needed(j - 1):
                            act.wait_ge(D_["product"].sem, D_["product"].at(j - 1))
                        act.activation(xT[:, a, 0:kb * P], turned[a], ACT.Copy).then_inc(D_["turned_sb"].sem, 1)

                    def give(j, a):
                        act.wait_ge(D_["product"].sem, D_["product"].at(j + 1))
                        if table is not None:
                            wait_stored(act, j, a)
                        act_out(act, j, a, prod[a]).then_inc(D_["act_out"].sem, 1)

                    sweep(act, turn, None, give if act_out else None)

                if table is not None:
                    @block.sync
                    def _(sp):
                        def store(j, a):
                            if act_out:
                                sp.wait_ge(D_["act_out"].sem, D_["act_out"].at(j + 1))
                                sp.sem_inc(tick.sem, 1)
                            if dve_out:
                                if needed(dve_ops * (j + 1)):
                                    sp.wait_ge(D_["dve_out"].sem, D_["dve_out"].at(dve_ops * (j + 1)))
                                    sp.sem_inc(tick.sem, 1)
                            sp.dma_start(table[ds(P * j, P), :], stage[:, a, 0:width]).then_inc(stored[a].sem, 16)

                        sweep(sp, store)
                        for a in range(2):
                            if needed(16 * ((NT + 1 - a) // 2)):
                                sp.wait_ge(stored[a].sem, stored[a].at(16 * ((NT + 1 - a) // 2)))
                                sp.sem_inc(tick.sem, 1)
            for n_ in ("in", "turned", "turned_sb", "product") + (() if bias is None else ("biased", "stats")):
                D_[n_].base += NT
            if act_out:
                D_["act_out"].base += NT
            if dve_out:
                D_["dve_out"].base += NT * dve_ops
            if table is not None:
                for a in range(2):
                    stored[a].base += 16 * ((NT + 1 - a) // 2)

        def wait_stored(eng, j, a):
            if needed(8 * (j - a)):
                eng.wait_ge(stored[a].sem, stored[a].at(8 * (j - a)))

        def normalised(lanes, C, denominator):
            def f(dve, link):
                av = acc[:, :, 0:H * lanes].rearrange("p j (h c) -> p j h c", h=H)
                inv = stats[:, 0:NT * H].rearrange("p (j h) -> p j h", j=NT)
                denominator(dve, link, av, inv)
                hv = hbuf[:, :, 0:H * C].rearrange("p j (h c) -> p j h c", h=H)
                for h in range(H):
                    op = dve.tensor_tensor(hv[:, :, h, :], av[:, :, h, 0:C],
                                           inv[:, :, h:h + 1].to_broadcast([P, NT, C]), ALU.mult)
                    link(op)
            return f

        def layer_0():
            w = arena[:, 0:4096].rearrange("p (k n) -> p k n", k=2)
            load(*[(w[:, k, 0:128], A["L0_gnn_Wl0"][k * P:k * P + P, :]) for k in range(2)],
                 *[(w[:, k, 128:256], A["L0_gnn_Wr0"][k * P:k * P + P, :]) for k in range(2)],
                 (w[:, 0, 256:512], A["L0_gnn_Wl1"][:, :]), (w[:, 0, 512:768], A["L0_gnn_Wr1"][:, :]),
                 (att[:, 0:128], row(A["L0_gnn_att0"].rearrange("h c -> (h c)"))),
                 (att[:, 256:512], row(A["L0_gnn_att1"].rearrange("h c -> (h c)"))),
                 (vecs[:, 0:128], row(A["L0_gnn_b0"])), (vecs[:, 256:512], row(A["L0_gnn_b1"])))
            project(lambda j: X[:, j, :], 2, w[:, :, 0:256], 256,
                    act_out=lambda act, j, a, ps: act.activation(stage[:, a, 0:128], ps[:, 0:128], ACT.Copy),
                    dve_out=lambda dve, j, a, ps: dve.tensor_copy(qtab[:, j, 0:128], ps[:, 128:256])
                    .then_inc(D_["dve_out"].sem, 1), table=tab_l0a, width=128)
            edge_pass("gatv2", tab_l0a, 128)

            def denominator(C):
                def f(dve, link, av, inv):
                    link(dve.tensor_scalar(inv, av[:, :, :, C], 1e-30, None, ALU.max))
                    link(dve.reciprocal(inv, inv))
                return f

            def relu(dve, link):
                normalised(17, 16, denominator(16))(dve, link)
                hv = hbuf[:, :, 0:128]
                link(dve.tensor_tensor(hv, hv, vecs[:, 0:128].unsqueeze(1).to_broadcast([P, NT, 128]), ALU.add))
                link(dve.tensor_scalar(hv, hv, 0.0, None, ALU.max))
                link(dve.tensor_copy(att[:, 0:256], att[:, 256:512]))

            vector_phase(relu)
            load((w[:, 0, 256:512], A["L0_gnn_Wl1"][:, :]), (w[:, 0, 512:768], A["L0_gnn_Wr1"][:, :]))
            project(lambda j: hbuf[:, j, 0:128], 1, w[:, :, 256:768], 512,
                    act_out=lambda act, j, a, ps: act.activation(stage[:, a, 0:256], ps[:, 0:256], ACT.Copy),
                    dve_out=lambda dve, j, a, ps: dve.tensor_copy(qtab[:, j, :], ps[:, 256:512])
                    .then_inc(D_["dve_out"].sem, 1), table=tab_l0b, width=256)
            edge_pass("gatv2", tab_l0b, 256)

            def close(dve, link):
                normalised(33, 32, denominator(32))(dve, link)
                link(dve.tensor_tensor(hbuf[:, :, :], hbuf[:, :, :], over_blocks(vecs[:, 256:512]), ALU.add))
                link(dve.tensor_tensor(X[:, :, :], X[:, :, :], hbuf[:, :, :], ALU.add))

            vector_phase(close)
            layer_norm()

        def layer_1():
            w_in = arena[:, 0:512].rearrange("p (o n) -> p o n", o=2)
            w = arena[:, 512:1024].rearrange("p (k n) -> p k n", k=2)
            load(*[(w_in[:, o, :], A["L1_gnn_W"][o * P:o * P + P, :]) for o in range(2)],
                 (att[:, 0:256], row(A["L1_gnn_attn_l"].rearrange("a h c -> (a h c)"))),
                 (att[:, 256:512], row(A["L1_gnn_attn_r"].rearrange("a h c -> (a h c)"))))
            with nc.Block() as block:
                @block.tensor
                def _(pe):
                    for k in range(2):
                        for o in range(2):
                            pe.transpose(PS[0][:, k * D + o * P:k * D + o * P + P], w_in[:, o, k * P:k * P + P],
                                         ident[:, :]).then_inc(multiplied.sem, 1)

                @block.vector
                def _(dve):
                    dve.wait_ge(multiplied.sem, multiplied.at(4))
                    dve.tensor_copy(w, PS[0][:, :].rearrange("p (k n) -> p k n", k=2)).then_inc(step.sem, 1)
            multiplied.base += 4
            step.base += 1

            def logit_parts(dve, j, a, ps):
                for k, out_ in ((0, stage[:, a, D:D + H]), (1, qtab[:, j, 0:H])):
                    if needed(2 * j + k):
                        dve.wait_ge(D_["dve_out"].sem, D_["dve_out"].at(2 * j + k))
                    dve.tensor_tensor(tmp[:, 0, :], ps, att[:, k * D:k * D + D], ALU.mult).then_inc(D_["tmp"].sem, 1)
                    if needed(2 * j + k + 1):
                        dve.wait_ge(D_["tmp"].sem, D_["tmp"].at(2 * j + k + 1))
                    dve.tensor_reduce(out_, tmp[:, 0, :].rearrange("p (h c) -> p h c", h=H), AX, ALU.add)\
                       .then_inc(D_["dve_out"].sem, 1)

            project(lambda j: X[:, j, :], 2, w, 256,
                    act_out=lambda act, j, a, ps: act.activation(stage[:, a, 0:256], ps, ACT.Copy),
                    dve_out=logit_parts, dve_ops=2, table=tab_l1, width=D + H)
            D_["tmp"].base += 2 * NT
            edge_pass("gat", tab_l1, D + H)

            av = acc[:, :, 0:H * 34].rearrange("p j (h c) -> p j h c", h=H)
            top = tmp[:, 0, 0:NT * H].rearrange("p (j h) -> p j h", j=NT)
            factor = tmp[:, 1, 0:NT * H].rearrange("p (j h) -> p j h", j=NT)
            peak, peaks = small[:, 16:24], small[:, 24:32]

            def maxima(dve, link):
                link(dve.tensor_copy(top, av[:, :, :, 33]))
                link(dve.tensor_scalar(small[:, 8:9], small[:, 0:1], float(NLAST), -BIG, ALU.is_ge, ALU.mult))
                link(dve.tensor_scalar(top[:, NT - 1, :], top[:, NT - 1, :], small[:, 8:9], None, ALU.add))
                link(dve.tensor_reduce(peak, top.rearrange("p j h -> p h j"), AX, ALU.max))

            vector_phase(maxima)
            with nc.Block() as block:
                @block.gpsimd
                def _(pool):
                    pool.partition_all_reduce(peaks, peak, P, RMAX).then_inc(made.sem, 1)
            made.base += 1
            vector_phase(lambda dve, link: link(dve.tensor_tensor(
                top, top, peaks.unsqueeze(1).to_broadcast([P, NT, H]), ALU.subtract)))
            scalar_phase((factor, top, ACT.Exp))

            def denominator(dve, link, av, inv):
                link(dve.tensor_tensor(inv, av[:, :, :, 32], factor, ALU.mult))
                link(dve.tensor_scalar(inv, inv, 1e-6, None, ALU.max))
                link(dve.reciprocal(inv, inv))
                link(dve.tensor_tensor(inv, inv, factor, ALU.mult))

            def close(dve, link):
                normalised(34, 32, denominator)(dve, link)
                link(dve.tensor_tensor(X[:, :, :], X[:, :, :], hbuf[:, :, :], ALU.add))

            vector_phase(close)
            layer_norm()

        flat_oh = onehots[:, :, :, :].rearrange("p a t c -> p (a t c)")

        def typed_tables(l):
            w_qv = arena[:, 0:2048].rearrange("p (a k c n) -> p a k c n", a=4, k=2, c=2)
            w_k = arena[:, 2048:3072].rearrange("p (a k n) -> p a k n", a=4, k=2)
            w_e = arena[:, 3072:3840].rearrange("p (k a n) -> p k a n", k=2, a=3)
            mu = small[:, 32:56].rearrange("p (h t) -> p t h", t=3)
            masked_x = flat_oh[:, 0:2048].rearrange("p (a t c) -> p a t c", a=2, t=4)
            turned_x = flat_oh[:, 2048:4096].rearrange("p (a k t c) -> p a k t c", a=2, k=2, t=4)
            is_type = stats[:, 0:4 * NT].rearrange("p (t j) -> p t j", t=4)
            keysT = spreads

            def prepare(dve, link):
                link(dve.memset(arena[:, 0:3840], 0.0))
                for t in range(4):
                    link(dve.tensor_scalar(is_type[:, t, :], type_of[:, :], float(t), None, ALU.is_equal))

            vector_phase(prepare)
            pairs = []
            for hh in range(4):
                q = slice(32 * hh, 32 * hh + 32)
                for k in range(2):
                    h = 4 * k + hh
                    pairs += [(w_qv[q, :, k, 0, q], A["L2_gnn_W_Q"][l, :, h].rearrange("a d e -> d a e")),
                              (w_qv[q, :, k, 1, q], A["L2_gnn_W_V"][l, :, h].rearrange("a d e -> d a e")),
                              (w_k[q, :, k, q], A["L2_gnn_W_K"][l, :, h].rearrange("a d e -> d a e")),
                              (w_e[q, k, :, q], A["L2_gnn_W_E"][l, :, h].rearrange("a d e -> d a e"))]
            mu_ap = A["L2_gnn_mu"]
            pairs.append((small[:, 32:56], bass.AP(tensor=mu_ap.tensor, offset=l * H * 3, ap=[[0, P], [1, 3 * H]])))
            load(*pairs)
            vector_phase(lambda dve, link: link(dve.tensor_scalar(small[:, 32:56], small[:, 32:56],
                                                                  float(32.0 ** -0.5), None, ALU.mult)))
            qv = [PS[2][:, :].rearrange("p (k c n) -> p k c n", k=2, c=2),
                  PS[3][:, :].rearrange("p (k c n) -> p k c n", k=2, c=2)]
            kt = [PS[4][:, 0:D], PS[7][:, 0:D]]
            ke = [PS[5][:, 0:384].rearrange("p (t n) -> p t n", t=3), PS[6][:, 0:384].rearrange("p (t n) -> p t n", t=3)]

            with nc.Block() as block:
                @block.vector
                def _(dve):
                    def mask(j, a):
                        if needed(j - 1):
                            dve.wait_ge(D_["turned"].sem, D_["turned"].at(j - 1))
                        for t in range(4):
                            op = dve.tensor_scalar(masked_x[:, a, t, :], X[:, j, :], is_type_at(t, j), None, ALU.mult)
                        op.then_inc(D_["in"].sem, 1)

                    def is_type_at(t, j):
                        return stats[:, ds(t * NT + j, 1)]

                    def queries(j, a):
                        dve.wait_ge(D_["values"].sem, D_["values"].at(3 * (j + 1)))
                        dve.tensor_copy(qtab[:, j, :].rearrange("p (k n) -> p k n", k=2), qv[a][:, :, 0, :])\
                           .then_inc(D_["dve_out"].sem, 1)

                    def keys(j, a):
                        dve.wait_ge(D_["typed"].sem, D_["typed"].at(j + 1))
                        wait_stored(dve, j, a)
                        st = stage[:, a, :].rearrange("p (t c) -> p t c", t=3)
                        for k in range(2):
                            dve.tensor_tensor(
                                st[:, :, k * P:k * P + P].rearrange("p t (h e) -> p t h e", e=32),
                                ke[k].rearrange("p t (h e) -> p t h e", e=32),
                                mu[:, :, 4 * k:4 * k + 4].unsqueeze(3).to_broadcast([P, 3, 4, 32]), ALU.mult)\
                               .then_inc(D_["keys"].sem, 1)

                    sweep(dve, mask, None, queries, keys)

                @block.tensor
                def _(pe):
                    def turn(j, a):
                        pe.wait_ge(D_["in"].sem, D_["in"].at(j + 1))
                        if needed(2 * j):
                            pe.wait_ge(D_["turned_sb"].sem, D_["turned_sb"].at(2 * j))
                        for k in range(2):
                            for t in range(4):
                                op = pe.transpose(PS[k][:, t * P:t * P + P], masked_x[:, a, t, k * P:k * P + P],
                                                  ident[:, :])
                        op.then_inc(D_["turned"].sem, 1)

                    def transform(j, a):
                        pe.wait_ge(D_["turned_sb"].sem, D_["turned_sb"].at(2 * j + 2))
                        if needed(j - 1):
                            pe.wait_ge(D_["dve_out"].sem, D_["dve_out"].at(j - 1))
                        if needed(3 * (j - 1)):
                            pe.wait_ge(D_["values"].sem, D_["values"].at(3 * (j - 1)))
                        if needed(j - 1):
                            pe.wait_ge(D_["keys_sb"].sem, D_["keys_sb"].at(j - 1))
                        for k in range(2):
                            for t in range(4):
                                pe.matmul(kt[a][:, k * P:k * P + P], w_k[:, t, k, :], turned_x[:, a, k, t, :],
                                          start=t == 0, stop=t == 3).then_inc(kept.sem, 1)
                        for k in range(2):
                            for t in range(4):
                                op = pe.matmul(qv[a][:, k, :, :].rearrange("p c n -> p (c n)"),
                                               turned_x[:, a, k, t, :],
                                               w_qv[:, t, k, :, :].rearrange("p c n -> p (c n)"),
                                               start=t == 0, stop=t == 3)
                        op.then_inc(D_["product"].sem, 1)

                    def edge_types(j, a):
                        pe.wait_ge(D_["keys_sb"].sem, D_["keys_sb"].at(j + 1))
                        if needed(2 * j):
                            pe.wait_ge(D_["keys"].sem, D_["keys"].at(2 * j))
                        for k in range(2):
                            op = pe.matmul(ke[k].rearrange("p t n -> p (t n)"), keysT[:, a, k * P:k * P + P],
                                           w_e[:, k, :, :].rearrange("p t n -> p (t n)"), start=True, stop=True)
                        op.then_inc(D_["typed"].sem, 1)

                    sweep(pe, turn, transform, edge_types)

                @block.scalar
                def _(act):
                    def turn(j, a):
                        act.wait_ge(D_["turned"].sem, D_["turned"].at(j + 1))
                        if needed(j - 1):
                            act.wait_ge(D_["product"].sem, D_["product"].at(j - 1))
                        for k in range(2):
                            act.activation(turned_x[:, a, k, :, :].rearrange("p t c -> p (t c)"), PS[k][:, :], ACT.Copy)\
                               .then_inc(D_["turned_sb"].sem, 1)

                    def keys(j, a):
                        act.wait_ge(D_["product"].sem, D_["product"].at(j + 1))
                        if needed(j - 1):
                            act.wait_ge(D_["typed"].sem, D_["typed"].at(j - 1))
                        act.activation(keysT[:, a, :], kt[a], ACT.Copy).then_inc(D_["keys_sb"].sem, 1)
                        wait_stored(act, j, a)
                        st = stage[:, a, :].rearrange("p (t c) -> p t c", t=3)
                        for t in range(3):
                            act.activation(st[:, t, D:2 * D].rearrange("p (k n) -> p k n", k=2), qv[a][:, :, 1, :],
                                           ACT.Copy).then_inc(D_["values"].sem, 1)

                    sweep(act, turn, keys)

                @block.sync
                def _(sp):
                    def store(j, a):
                        sp.wait_ge(D_["values"].sem, D_["values"].at(3 * (j + 1)))
                        sp.sem_inc(tick.sem, 1)
                        sp.wait_ge(D_["keys"].sem, D_["keys"].at(2 * (j + 1)))
                        sp.sem_inc(tick.sem, 1)
                        sp.dma_start(tab_l2[:, :].rearrange("(t n) c -> n t c", t=3)[ds(P * j, P), :, :],
                                     stage[:, a, :].rearrange("p (t c) -> p t c", t=3)).then_inc(stored[a].sem, 16)

                    sweep(sp, store)
                    for a in range(2):
                        if needed(16 * ((NT + 1 - a) // 2)):
                            sp.wait_ge(stored[a].sem, stored[a].at(16 * ((NT + 1 - a) // 2)))
                            sp.sem_inc(tick.sem, 1)
            for n_ in ("in", "turned", "product", "dve_out", "typed", "keys_sb"):
                D_[n_].base += NT
            D_["turned_sb"].base += 2 * NT
            D_["keys"].base += 2 * NT
            D_["values"].base += 3 * NT
            kept.base += 8 * NT
            for a in range(2):
                stored[a].base += 16 * ((NT + 1 - a) // 2)

        def perceptron(up, down, bias, func, gain, offset, down_bias):
            hid = [stage_h[:, 0, :, :], stage_h[:, 1, :, :]]
            turned = [PS[0][:, 0:D], PS[7][:, 0:D]]
            hp = [[PS[1], PS[2]], [PS[3], PS[4]]]
            prod = [PS[5][:, 0:D], PS[6][:, 0:D]]
            with nc.Block() as block:
                @block.vector
                def _(dve):
                    def take(j, a):
                        if needed(j - 1):
                            dve.wait_ge(D_["turned"].sem, D_["turned"].at(j - 1))
                        dve.wait_ge(D_["normed"].sem, D_["normed"].at(3 * j + 2))
                        dve.tensor_tensor(xin[:, a, :], X[:, j, :], offset, ALU.add).then_inc(D_["in"].sem, 1)
                        dve.tensor_tensor(X[:, j, :], X[:, j, :], offset, ALU.add).then_inc(D_["normed"].sem, 1)

                    def normalise(j, a):
                        dve.tensor_scalar(X[:, j, :], X[:, j, :], ln[:, ds(2 * NT + j, 1)], ln[:, ds(3 * NT + j, 1)],
                                          ALU.mult, ALU.add).then_inc(D_["normed"].sem, 1)
                        dve.wait_ge(D_["normed"].sem, D_["normed"].at(3 * j + 1))
                        dve.tensor_tensor(X[:, j, :], X[:, j, :], gain, ALU.mult).then_inc(D_["normed"].sem, 1)

                    def add_bias(j, a):
                        dve.wait_ge(D_["normed"].sem, D_["normed"].at(3 * j + 3))
                        dve.tensor_tensor(X[:, j, :], X[:, j, :], down_bias, ALU.add)\
                           .then_inc(D_["biased"].sem, 1)

                    def take_stats(j, a):
                        dve.wait_ge(D_["dve_out"].sem, D_["dve_out"].at(j + 1))
                        block_stats(dve, j).then_inc(D_["stats"].sem, 1)

                    def give(j, a):
                        dve.wait_ge(D_["biased"].sem, D_["biased"].at(j + 1))
                        dve.wait_ge(D_["product"].sem, D_["product"].at(j + 1))
                        dve.tensor_tensor(X[:, j, :], X[:, j, :], prod[a], ALU.add).then_inc(D_["dve_out"].sem, 1)

                    normalise(0, 0)
                    sweep(dve, lambda j, a: (take(j, a), isinstance(j, int) and j == NT - 1 or normalise(j + 1, a)),
                          add_bias, None, give, take_stats)
                    dve.wait_ge(D_["stats"].sem, D_["stats"].at(NT))

                @block.tensor
                def _(pe):
                    def turn(j, a):
                        pe.wait_ge(D_["in"].sem, D_["in"].at(j + 1))
                        if needed(j - 1):
                            pe.wait_ge(D_["turned_sb"].sem, D_["turned_sb"].at(j - 1))
                        for k in range(2):
                            op = pe.transpose(turned[a][:, k * P:k * P + P], xin[:, a, k * P:k * P + P], ident[:, :])
                        op.then_inc(D_["turned"].sem, 1)

                    def ups(j, a):
                        pe.wait_ge(D_["turned_sb"].sem, D_["turned_sb"].at(j + 1))
                        if needed(8 * (j - 1)):
                            pe.wait_ge(D_["hidden_sb"].sem, D_["hidden_sb"].at(8 * (j - 1)))
                        for m in range(8):
                            for k in range(2):
                                op = pe.matmul(hp[a][m // 4][:, m % 4 * P:m % 4 * P + P], up[:, k, m * P:m * P + P],
                                               spreads[:, a, k * P:k * P + P], start=k == 0, stop=k == 1)
                            op.then_inc(D_["hidden"].sem, 1)

                    def downs(j, a):
                        pe.wait_ge(D_["hidden_sb"].sem, D_["hidden_sb"].at(8 * (j + 1)))
                        if needed(j - 1):
                            pe.wait_ge(D_["dve_out"].sem, D_["dve_out"].at(j - 1))
                        for m in range(8):
                            op = pe.matmul(prod[a], hid[a][:, m, :], down[:, m, :], start=m == 0, stop=m == 7)
                        op.then_inc(D_["product"].sem, 1)

                    sweep(pe, turn, ups, downs)

                @block.scalar
                def _(act):
                    def turn(j, a):
                        act.wait_ge(D_["turned"].sem, D_["turned"].at(j + 1))
                        if needed(8 * (j - 1)):
                            act.wait_ge(D_["hidden"].sem, D_["hidden"].at(8 * (j - 1)))
                        act.activation(spreads[:, a, :], turned[a], ACT.Copy).then_inc(D_["turned_sb"].sem, 1)

                    def hidden(j, a):
                        if needed(j - 1):
                            act.wait_ge(D_["product"].sem, D_["product"].at(j - 1))
                        for m in range(8):
                            if needed(8 * j + m // 4 * 4 + 4):
                                act.wait_ge(D_["hidden"].sem, D_["hidden"].at(8 * j + m // 4 * 4 + 4))
                            act.activation(hid[a][:, m, :], hp[a][m // 4][:, m % 4 * P:m % 4 * P + P], func,
                                           bias=bias[:, m:m + 1]).then_inc(D_["hidden_sb"].sem, 1)

                    sweep(act, turn, hidden)
            for n_ in ("in", "turned", "turned_sb", "product", "dve_out", "biased", "stats"):
                D_[n_].base += NT
            D_["normed"].base += 3 * NT
            D_["hidden"].base += 8 * NT
            D_["hidden_sb"].base += 8 * NT

        stage_h = stage.rearrange("p a c -> p (a c)")[:, 0:2048].rearrange("p (a m c) -> p a m c", a=2, m=8)

        def transformer_layer(l):
            typed_tables(l)
            edge_pass("hgt", tab_l2, 2 * D)

            def denominator(dve, link, av, inv):
                link(dve.tensor_scalar(inv, av[:, :, :, 32], 1e-10, None, ALU.add))
                link(dve.reciprocal(inv, inv))

            vector_phase(normalised(33, 32, denominator))
            w1 = arena[:, 0:2048].rearrange("p (k n) -> p k n", k=2)
            w2 = arena[:, 2048:4096].rearrange("p (m n) -> p m n", m=8)
            wo = flat_oh[:, 0:512].rearrange("p (k n) -> p k n", k=2)
            load((wo, A["L2_gnn_Wo"][l].rearrange("(k p) n -> p k n", p=P)),
                 (w1, A["L2_gnn_w1"][l].rearrange("(k p) n -> p k n", p=P)),
                 (w2, A["L2_gnn_w2"][l].rearrange("(m p) n -> p m n", p=P)),
                 (vecs[:, 0:D], row(A["L2_gnn_bo"][l])), (vecs[:, D:2 * D], row(A["L2_gnn_b2"][l])),
                 (vecs[:, 2 * D:3 * D], row(A["L2_gnn_ln1_g"][l])), (vecs[:, 3 * D:4 * D], row(A["L2_gnn_ln1_b"][l])),
                 (att[:, 0:D], row(A["L2_gnn_ln2_g"][l])), (att[:, D:2 * D], row(A["L2_gnn_ln2_b"][l])),
                 (cols[:, 0:8], A["L2_gnn_b1"][l].rearrange("(m p) -> p m", p=P)))
            project(lambda j: hbuf[:, j, :], 2, wo, 256,
                    dve_out=lambda dve, j, a, ps: dve.tensor_tensor(X[:, j, :], X[:, j, :], ps, ALU.add)
                    .then_inc(D_["dve_out"].sem, 1), bias=vecs[:, 0:D])
            layer_norm(stats_made=True, apply=False)
            perceptron(w1, w2, cols[:, 0:8], ACT.Gelu, vecs[:, 2 * D:3 * D], vecs[:, 3 * D:4 * D], vecs[:, D:2 * D])
            layer_norm(att[:, 0:D], att[:, D:2 * D], stats_made=True)

        def layer_2():
            blocks = lambda t: t[:, :].rearrange("(j p) c -> p j c", p=P)
            load((blocks(residual), X[:, :, :]))

            def self_loops(sign):
                vector_phase(lambda dve, link: link(dve.scalar_tensor_tensor(
                    slot_loc[:, :], slot_bar[:, :], -sign * PADLOC / BIG, slot_loc[:, :], ALU.mult, ALU.add)))

            self_loops(1)
            for l in range(3):
                transformer_layer(l)
            self_loops(-1)
            load((vecs[:, 0:D], row(A["L2_gnn_out_g"])), (vecs[:, D:2 * D], row(A["L2_gnn_out_b"])),
                 (hbuf[:, :, :], blocks(residual)))
            layer_norm(vecs[:, 0:D], vecs[:, D:2 * D])
            vector_phase(lambda dve, link: link(dve.tensor_tensor(X[:, :, :], X[:, :, :], hbuf[:, :, :], ALU.add)))
            layer_norm()

        def layer_3():
            w1 = flat_oh[:, 0:2048].rearrange("p (k n) -> p k n", k=2)
            w2 = flat_oh[:, 2048:4096].rearrange("p (m n) -> p m n", m=8)
            load((tab_l3[:, :].rearrange("(j p) c -> p j c", p=P), X[:, :, :]))
            edge_pass("gin", tab_l3, D)
            load((w1, A["L3_gnn_W1"].rearrange("(k p) n -> p k n", p=P)),
                 (w2, A["L3_gnn_W2"].rearrange("(m p) n -> p m n", p=P)),
                 (vecs[:, 0:D], row(A["L3_gnn_b2"])),
                 (cols[:, 0:8], A["L3_gnn_b1"].rearrange("(m p) -> p m", p=P)),
                 (cols[:, 8:16], A["L3_gnn_gamma"].rearrange("(m p) -> p m", p=P)),
                 (cols[:, 16:24], A["L3_gnn_beta"].rearrange("(m p) -> p m", p=P)))
            hid = [arena[:, NP * m:NP * m + NP] for m in range(7)] + [border[:, 0:NP]]
            turned = [PS[0][:, 0:D], PS[7][:, 0:D]]
            hp = [[PS[1], PS[2]], [PS[3], PS[4]]]
            rows_in = vecs[:, D:3 * D].rearrange("p (a c) -> p a c", a=2)
            with nc.Block() as block:
                @block.vector
                def _(dve):
                    def take(j, a):
                        if needed(j - 1):
                            dve.wait_ge(D_["turned"].sem, D_["turned"].at(j - 1))
                        dve.tensor_copy(rows_in[:, a, :], acc[:, j, 0:D]).then_inc(D_["in"].sem, 1)

                    sweep(dve, take)

                @block.tensor
                def _(pe):
                    def turn(j, a):
                        pe.wait_ge(D_["in"].sem, D_["in"].at(j + 1))
                        if needed(j - 1):
                            pe.wait_ge(D_["turned_sb"].sem, D_["turned_sb"].at(j - 1))
                        for k in range(2):
                            op = pe.transpose(turned[a][:, k * P:k * P + P], rows_in[:, a, k * P:k * P + P],
                                              ident[:, :])
                        op.then_inc(D_["turned"].sem, 1)

                    def ups(j, a):
                        pe.wait_ge(D_["turned_sb"].sem, D_["turned_sb"].at(j + 1))
                        if needed(8 * (j - 1)):
                            pe.wait_ge(D_["hidden_sb"].sem, D_["hidden_sb"].at(8 * (j - 1)))
                        for m in range(8):
                            for k in range(2):
                                op = pe.matmul(hp[a][m // 4][:, m % 4 * P:m % 4 * P + P], w1[:, k, m * P:m * P + P],
                                               spreads[:, a, k * P:k * P + P], start=k == 0, stop=k == 1)
                            op.then_inc(D_["hidden"].sem, 1)

                    sweep(pe, turn, ups)

                @block.scalar
                def _(act):
                    def turn(j, a):
                        act.wait_ge(D_["turned"].sem, D_["turned"].at(j + 1))
                        if needed(8 * (j - 1)):
                            act.wait_ge(D_["hidden"].sem, D_["hidden"].at(8 * (j - 1)))
                        act.activation(spreads[:, a, :], turned[a], ACT.Copy).then_inc(D_["turned_sb"].sem, 1)

                    def keep(j, a):
                        for m in range(8):
                            if needed(8 * j + m // 4 * 4 + 4):
                                act.wait_ge(D_["hidden"].sem, D_["hidden"].at(8 * j + m // 4 * 4 + 4))
                            act.activation(hid[m][:, ds(P * j, P)], hp[a][m // 4][:, m % 4 * P:m % 4 * P + P],
                                           ACT.Identity, bias=cols[:, m:m + 1]).then_inc(D_["hidden_sb"].sem, 1)

                    sweep(act, turn, keep)
            for n_ in ("in", "turned", "turned_sb"):
                D_[n_].base += NT
            D_["hidden"].base += 8 * NT
            D_["hidden_sb"].base += 8 * NT

            chunks = [(c, min(512, N - c)) for c in range(0, N, 512)]
            part = acc[:, 0:2, :].rearrange("p a b -> p (a b)")[:, 0:8 * len(chunks) * 6]\
                .rearrange("p (m c f) -> p m c f", m=8, f=6)
            mv = acc[:, 2, 0:16].rearrange("p (m f) -> p m f", f=2)
            sd, sc, bi = acc[:, 3, 0:8], acc[:, 3, 8:16], acc[:, 3, 16:24]

            def batch_stats(dve, link):
                for m in range(8):
                    for c, (c0, n_) in enumerate(chunks):
                        op = dve.bn_stats(out=part[:, m, c, :], in_=hid[m][:, c0:c0 + n_])
                link(op)
                for m in range(8):
                    op = dve.bn_aggr(out=mv[:, m, :], in_=part[:, m, :, :])
                link(op)
                link(dve.tensor_scalar(sd, mv[:, :, 1], 1e-5, None, ALU.add))

            vector_phase(batch_stats)
            scalar_phase((sc, sd, ACT.Sqrt))

            def affine(dve, link):
                link(dve.reciprocal(sd, sc))
                link(dve.tensor_tensor(sc, sd, cols[:, 8:16], ALU.mult))
                link(dve.tensor_tensor(bi, mv[:, :, 0], sc, ALU.mult))
                link(dve.tensor_tensor(bi, cols[:, 16:24], bi, ALU.subtract))

            vector_phase(affine)

            hin = acc[:, 4:12, :].rearrange("p a b -> p (a b)")[:, 0:2048].rearrange("p (a m c) -> p a m c", a=2, m=8)
            sums = acc[:, 12, 0:D]
            prod = [PS[5][:, 0:D], PS[6][:, 0:D]]
            with nc.Block() as block:
                @block.scalar
                def _(act):
                    def hidden(j, a):
                        if needed(j - 1):
                            act.wait_ge(D_["product"].sem, D_["product"].at(j - 1))
                        for m in range(8):
                            act.activation(hin[:, a, m, :], hid[m][:, ds(P * j, P)], ACT.Relu, bias=bi[:, m:m + 1],
                                           scale=sc[:, m:m + 1]).then_inc(D_["hidden_sb"].sem, 1)

                    sweep(act, hidden)

                @block.tensor
                def _(pe):
                    def downs(j, a):
                        pe.wait_ge(D_["hidden_sb"].sem, D_["hidden_sb"].at(8 * (j + 1)))
                        if needed(j - 1):
                            pe.wait_ge(D_["tmp"].sem, D_["tmp"].at(j - 1))
                        for m in range(8):
                            op = pe.matmul(prod[a], hin[:, a, m, :], w2[:, m, :], start=m == 0, stop=m == 7)
                        op.then_inc(D_["product"].sem, 1)

                    sweep(pe, downs)

                @block.vector
                def _(dve):
                    def give(j, a):
                        dve.wait_ge(D_["product"].sem, D_["product"].at(j + 1))
                        if needed(j):
                            dve.wait_ge(D_["dve_out"].sem, D_["dve_out"].at(j))
                        dve.tensor_tensor(sums, prod[a], vecs[:, 0:D], ALU.add).then_inc(D_["tmp"].sem, 1)
                        dve.wait_ge(D_["tmp"].sem, D_["tmp"].at(j + 1))
                        dve.scalar_tensor_tensor(X[:, j, :], sums, 0.0, X[:, j, :], ALU.max, ALU.add)\
                           .then_inc(D_["dve_out"].sem, 1)

                    sweep(dve, give)
            D_["hidden_sb"].base += 8 * NT
            for n_ in ("product", "tmp", "dve_out"):
                D_[n_].base += NT
            layer_norm()

        constants()
        load_edges()
        histogram()
        place_nodes()
        make_records()
        sort_edges()
        load_slots()
        find_borders()
        layer_0()
        layer_1()
        layer_2()
        layer_3()
        load((out[0:(NT - 1) * P, :].rearrange("(j p) c -> p j c", p=P), X[:, 0:NT - 1, :]),
             (out[(NT - 1) * P:N, :], X[0:NLAST, NT - 1, :]))


def kernel(**inputs):
    import numpy as np
    import concourse.bacc as bacc
    from concourse.bass_utils import run_bass_kernel_spmd

    nc = bacc.Bacc("TRN2", target_bir_lowering=False, num_devices=1)
    arrays = {name: np.ascontiguousarray(a) for name, a in inputs.items()}
    A = {name: nc.dram_tensor(name, a.shape, mybir.dt.from_np(a.dtype), kind="ExternalInput").ap()
         for name, a in arrays.items()}
    out = nc.dram_tensor("out", (N, D), F32, kind="ExternalOutput").ap()
    gnn_kernel(nc, A, out)
    result = run_bass_kernel_spmd(nc, [arrays], core_ids=[0])
    return result.results[0]["out"]
```
